# Optimizing a Trainium2 kernel written in Bass

```python
import numpy as np
import jax
import jax.numpy as jnp

def _softmax(x, axis=-1):
    return jax.nn.softmax(x, axis=axis)

def _gelu(x):
    return jax.nn.gelu(x, approximate=True)

def _silu(x):
    return jax.nn.silu(x)

def _sigmoid(x):
    return jax.nn.sigmoid(x)

def _layernorm(x, axis=-1, eps=1e-05):
    m = jnp.mean(x, axis=axis, keepdims=True)
    v = jnp.var(x, axis=axis, keepdims=True)
    return (x - m) / jnp.sqrt(v + eps)

def _scatter_add(tgt, idx, src, axis=0):
    return tgt.at[idx].add(src)

def _segment_sum(src, seg, n):
    return jax.ops.segment_sum(src, seg, n)
kernel_name = 'mk_pixart_seq_d2_seqx_r4_19f760'

def setup_inputs(seed: int=0):
    np.random.seed(seed)
    _w = jnp.asarray

    def _rec_inputs():
        import jax
        import jax.numpy as jnp
        _rk = jax.random.key(seed)
        x = 7.22e-05 + 1 * jax.random.normal(jax.random.fold_in(_rk, 1), (64, 128, 256), jnp.float32)
        _lenS = 128 - jax.random.randint(jax.random.fold_in(_rk, 7), (64,), 0, max(1, 128 // 4) + 1, jnp.int32)
        _lenS2 = 128 - jax.random.randint(jax.random.fold_in(_rk, 8), (64,), 0, max(1, 128 // 4) + 1, jnp.int32)
        cond_1024 = 0.000887014 + 1.03683 * jax.random.normal(jax.random.fold_in(_rk, 11), (64, 256), jnp.float32)
        _ctx_1024P = jax.random.normal(jax.random.fold_in(_rk, 12), (64, 16, 256), jnp.float32)
        _ctx_1024c = jax.random.dirichlet(jax.random.fold_in(_rk, 512), 0.3 * jnp.ones((16,), jnp.float32), (64, 128))
        _ctx_1024t = jnp.einsum('bsk,bkd->bsd', _ctx_1024c, _ctx_1024P)
        _ctx_1024t = _ctx_1024t * jax.lax.rsqrt(jnp.mean(jnp.square(_ctx_1024t)) + 1e-12) * 0.953939
        ctx_1024 = 0.00086875 + 0.999764 * (_ctx_1024t + 0.3 * jax.random.normal(jax.random.fold_in(_rk, 612), (64, 128, 256), jnp.float32))
        return (x, cond_1024, ctx_1024)
    x, cond_1024, ctx_1024 = _rec_inputs()

    def _L0_xcond_setup():
        import jax, jax.numpy as jnp
        import numpy as np
        C = 256
        H = 16
        D = C // H
        WIN = 128
        SHIFT = 64
        TOPK = 16
        HID = 1024
        EPS = 1e-06

        def _ln(x):
            x32 = x.astype(jnp.float32)
            m = x32.mean(-1, keepdims=True)
            v = jnp.mean((x32 - m) ** 2, axis=-1, keepdims=True)
            return ((x32 - m) * jax.lax.rsqrt(v + EPS)).astype(x.dtype)

        def _self_attn(h, w_qkv, b_qkv, w_so, b_so):
            B, L, _ = h.shape
            qkv = h @ w_qkv + b_qkv
            qkv = jnp.roll(qkv, -SHIFT, axis=1)
            nw = L // WIN
            qkv = qkv.reshape(B, nw, WIN, 3, H, D)
            q, k, v = (qkv[:, :, :, 0], qkv[:, :, :, 1], qkv[:, :, :, 2])
            scores = jnp.einsum('bnqhd,bnkhd->bnhqk', q, k) / jnp.sqrt(jnp.float32(D)).astype(h.dtype)
            attn = jax.nn.softmax(scores, axis=-1)
            o = jnp.einsum('bnhqk,bnkhd->bnqhd', attn, v).reshape(B, L, C)
            o = jnp.roll(o, SHIFT, axis=1)
            return o @ w_so + b_so

        def _topk_cross_attn(h, ctx, w_q, b_q, w_kv, b_kv, w_co, b_co):
            B, L, _ = h.shape
            Lc = ctx.shape[1]
            q = (h @ w_q + b_q).reshape(B, L, H, D)
            kv = (ctx @ w_kv + b_kv).reshape(B, Lc, 2, H, D)
            k, v = (kv[:, :, 0], kv[:, :, 1])
            scores = jnp.einsum('bqhd,bkhd->bhqk', q, k) / jnp.sqrt(jnp.float32(D)).astype(h.dtype)
            top_s, top_i = jax.lax.top_k(scores, TOPK)
            attn = jax.nn.softmax(top_s, axis=-1)
            v_bh = jnp.transpose(v, (0, 2, 1, 3))
            vg = jnp.take_along_axis(v_bh[:, :, None, :, :], top_i[..., None], axis=3)
            o = jnp.einsum('bhqk,bhqkd->bqhd', attn, vg).reshape(B, L, C)
            return o @ w_co + b_co

        def _swiglu(h, w_m1, b_m1, w_m2, b_m2):
            u = h @ w_m1 + b_m1
            a, b = (u[..., :HID], u[..., HID:])
            return jax.nn.silu(a) * b @ w_m2 + b_m2
        key = jax.random.key(seed)
        ks = jax.random.split(key, 24)
        s = 0.02
        inp = {'x': jax.random.normal(ks[0], (2, 1024, C), jnp.float32), 'mod': jax.random.normal(ks[1], (2, C), jnp.float32), 'context': jax.random.normal(ks[2], (2, 256, C), jnp.float32), 'w_ada': jax.random.normal(ks[3], (C, 9 * C), jnp.float32) * s, 'b_ada': jnp.zeros((9 * C,), jnp.float32), 'w_qkv': jax.random.normal(ks[4], (C, 3 * C), jnp.float32) * s, 'b_qkv': jnp.zeros((3 * C,), jnp.float32), 'w_so': jax.random.normal(ks[5], (C, C), jnp.float32) * s, 'b_so': jnp.zeros((C,), jnp.float32), 'w_q': jax.random.normal(ks[6], (C, C), jnp.float32) * s, 'b_q': jnp.zeros((C,), jnp.float32), 'w_kv': jax.random.normal(ks[7], (C, 2 * C), jnp.float32) * s, 'b_kv': jnp.zeros((2 * C,), jnp.float32), 'w_co': jax.random.normal(ks[8], (C, C), jnp.float32) * s, 'b_co': jnp.zeros((C,), jnp.float32), 'w_m1': jax.random.normal(ks[9], (C, 2 * HID), jnp.float32) * s, 'b_m1': jnp.zeros((2 * HID,), jnp.float32), 'w_m2': jax.random.normal(ks[10], (HID, C), jnp.float32) * s, 'b_m2': jnp.zeros((C,), jnp.float32)}
        return inp
    _L0_xcond_all = _L0_xcond_setup()
    _L0_xcond_in = {k: v for k, v in _L0_xcond_all.items() if k in ('w_ada', 'b_ada', 'w_qkv', 'b_qkv', 'w_so', 'b_so', 'w_q', 'b_q', 'w_kv', 'b_kv', 'w_co', 'b_co', 'w_m1', 'b_m1', 'w_m2', 'b_m2')}
    del _L0_xcond_all

    def _L1_xcond_setup():
        import jax, jax.numpy as jnp
        import numpy as np
        H = 256
        RH = 2 * H
        E = 3
        B, T, P = (8, 512, 64)
        LN_EPS = 1e-05

        def _layer_norm(x, gamma, beta):
            mu = jnp.mean(x, axis=-1, keepdims=True)
            var = jnp.mean(jnp.square(x - mu), axis=-1, keepdims=True)
            return (x - mu) * jax.lax.rsqrt(var + LN_EPS) * gamma + beta
        key = jax.random.key(seed)
        ks = jax.random.split(key, 24)
        s = lambda fan_in: 1.0 / np.sqrt(fan_in)
        inp = {'mix_hidden_states': jax.random.normal(ks[0], (B, T, H), jnp.float32), 'global_anchor': jax.random.normal(ks[1], (B, H), jnp.float32), 'prototype_bank': jax.random.normal(ks[2], (B, P, H), jnp.float32), 'ln_gamma': jnp.ones((H,), jnp.float32), 'ln_beta': jnp.zeros((H,), jnp.float32), 'Wq': jax.random.normal(ks[3], (H, H), jnp.float32) * s(H), 'Wk': jax.random.normal(ks[4], (H, H), jnp.float32) * s(H), 'Wv': jax.random.normal(ks[5], (H, H), jnp.float32) * s(H), 'router_W': jax.random.normal(ks[6], (3 * H, E), jnp.float32) * s(3 * H), 'router_b': jnp.zeros((E,), jnp.float32), 'e_w1': jax.random.normal(ks[7], (E, 3 * H, RH), jnp.float32) * s(3 * H), 'e_b1': jnp.zeros((E, RH), jnp.float32), 'e_w2': jax.random.normal(ks[8], (E, RH, H), jnp.float32) * s(RH), 'e_b2': jnp.zeros((E, H), jnp.float32), 'gate_w1': jax.random.normal(ks[9], (3 * H, H), jnp.float32) * s(3 * H), 'gate_b1': jnp.zeros((H,), jnp.float32), 'gate_w2': jax.random.normal(ks[10], (H, H), jnp.float32) * s(H), 'gate_b2': jnp.zeros((H,), jnp.float32), 'out_w': jax.random.normal(ks[11], (H, H), jnp.float32) * s(H), 'out_b': jnp.zeros((H,), jnp.float32)}
        return inp
    _L1_xcond_all = _L1_xcond_setup()
    _L1_xcond_in = {k: v for k, v in _L1_xcond_all.items() if k in ('ln_gamma', 'ln_beta', 'Wq', 'Wk', 'Wv', 'router_W', 'router_b', 'e_w1', 'e_b1', 'e_w2', 'e_b2', 'gate_w1', 'gate_b1', 'gate_w2', 'gate_b2', 'out_w', 'out_b')}
    del _L1_xcond_all
    return {'x': x, 'cond_1024': cond_1024, 'ctx_1024': ctx_1024, 'L0_xcond_w_ada': _L0_xcond_in['w_ada'], 'L0_xcond_b_ada': _L0_xcond_in['b_ada'], 'L0_xcond_w_qkv': _L0_xcond_in['w_qkv'], 'L0_xcond_b_qkv': _L0_xcond_in['b_qkv'], 'L0_xcond_w_so': _L0_xcond_in['w_so'], 'L0_xcond_b_so': _L0_xcond_in['b_so'], 'L0_xcond_w_q': _L0_xcond_in['w_q'], 'L0_xcond_b_q': _L0_xcond_in['b_q'], 'L0_xcond_w_kv': _L0_xcond_in['w_kv'], 'L0_xcond_b_kv': _L0_xcond_in['b_kv'], 'L0_xcond_w_co': _L0_xcond_in['w_co'], 'L0_xcond_b_co': _L0_xcond_in['b_co'], 'L0_xcond_w_m1': _L0_xcond_in['w_m1'], 'L0_xcond_b_m1': _L0_xcond_in['b_m1'], 'L0_xcond_w_m2': _L0_xcond_in['w_m2'], 'L0_xcond_b_m2': _L0_xcond_in['b_m2'], 'L1_xcond_ln_gamma': _L1_xcond_in['ln_gamma'], 'L1_xcond_ln_beta': _L1_xcond_in['ln_beta'], 'L1_xcond_Wq': _L1_xcond_in['Wq'], 'L1_xcond_Wk': _L1_xcond_in['Wk'], 'L1_xcond_Wv': _L1_xcond_in['Wv'], 'L1_xcond_router_W': _L1_xcond_in['router_W'], 'L1_xcond_router_b': _L1_xcond_in['router_b'], 'L1_xcond_e_w1': _L1_xcond_in['e_w1'], 'L1_xcond_e_b1': _L1_xcond_in['e_b1'], 'L1_xcond_e_w2': _L1_xcond_in['e_w2'], 'L1_xcond_e_b2': _L1_xcond_in['e_b2'], 'L1_xcond_gate_w1': _L1_xcond_in['gate_w1'], 'L1_xcond_gate_b1': _L1_xcond_in['gate_b1'], 'L1_xcond_gate_w2': _L1_xcond_in['gate_w2'], 'L1_xcond_gate_b2': _L1_xcond_in['gate_b2'], 'L1_xcond_out_w': _L1_xcond_in['out_w'], 'L1_xcond_out_b': _L1_xcond_in['out_b']}

def reference(x, cond_1024, ctx_1024, L0_xcond_w_ada, L0_xcond_b_ada, L0_xcond_w_qkv, L0_xcond_b_qkv, L0_xcond_w_so, L0_xcond_b_so, L0_xcond_w_q, L0_xcond_b_q, L0_xcond_w_kv, L0_xcond_b_kv, L0_xcond_w_co, L0_xcond_b_co, L0_xcond_w_m1, L0_xcond_b_m1, L0_xcond_w_m2, L0_xcond_b_m2, L1_xcond_ln_gamma, L1_xcond_ln_beta, L1_xcond_Wq, L1_xcond_Wk, L1_xcond_Wv, L1_xcond_router_W, L1_xcond_router_b, L1_xcond_e_w1, L1_xcond_e_b1, L1_xcond_e_w2, L1_xcond_e_b2, L1_xcond_gate_w1, L1_xcond_gate_b1, L1_xcond_gate_w2, L1_xcond_gate_b2, L1_xcond_out_w, L1_xcond_out_b):
    import jax
    import jax.numpy as jnp

    def _L0_xcond_ref(x, mod, context, w_ada, b_ada, w_qkv, b_qkv, w_so, b_so, w_q, b_q, w_kv, b_kv, w_co, b_co, w_m1, b_m1, w_m2, b_m2):
        import jax, jax.numpy as jnp
        import numpy as np
        C = 256
        H = 16
        D = C // H
        WIN = 128
        SHIFT = 64
        TOPK = 16
        HID = 1024
        EPS = 1e-06

        def _ln(x):
            x32 = x.astype(jnp.float32)
            m = x32.mean(-1, keepdims=True)
            v = jnp.mean((x32 - m) ** 2, axis=-1, keepdims=True)
            return ((x32 - m) * jax.lax.rsqrt(v + EPS)).astype(x.dtype)

        def _self_attn(h, w_qkv, b_qkv, w_so, b_so):
            B, L, _ = h.shape
            qkv = h @ w_qkv + b_qkv
            qkv = jnp.roll(qkv, -SHIFT, axis=1)
            nw = L // WIN
            qkv = qkv.reshape(B, nw, WIN, 3, H, D)
            q, k, v = (qkv[:, :, :, 0], qkv[:, :, :, 1], qkv[:, :, :, 2])
            scores = jnp.einsum('bnqhd,bnkhd->bnhqk', q, k) / jnp.sqrt(jnp.float32(D)).astype(h.dtype)
            attn = jax.nn.softmax(scores, axis=-1)
            o = jnp.einsum('bnhqk,bnkhd->bnqhd', attn, v).reshape(B, L, C)
            o = jnp.roll(o, SHIFT, axis=1)
            return o @ w_so + b_so

        def _topk_cross_attn(h, ctx, w_q, b_q, w_kv, b_kv, w_co, b_co):
            B, L, _ = h.shape
            Lc = ctx.shape[1]
            q = (h @ w_q + b_q).reshape(B, L, H, D)
            kv = (ctx @ w_kv + b_kv).reshape(B, Lc, 2, H, D)
            k, v = (kv[:, :, 0], kv[:, :, 1])
            scores = jnp.einsum('bqhd,bkhd->bhqk', q, k) / jnp.sqrt(jnp.float32(D)).astype(h.dtype)
            top_s, top_i = jax.lax.top_k(scores, TOPK)
            attn = jax.nn.softmax(top_s, axis=-1)
            v_bh = jnp.transpose(v, (0, 2, 1, 3))
            vg = jnp.take_along_axis(v_bh[:, :, None, :, :], top_i[..., None], axis=3)
            o = jnp.einsum('bhqk,bhqkd->bqhd', attn, vg).reshape(B, L, C)
            return o @ w_co + b_co

        def _swiglu(h, w_m1, b_m1, w_m2, b_m2):
            u = h @ w_m1 + b_m1
            a, b = (u[..., :HID], u[..., HID:])
            return jax.nn.silu(a) * b @ w_m2 + b_m2
        m = jax.nn.silu(mod) @ w_ada + b_ada
        sh_msa, sc_msa, g_msa, sh_mca, sc_mca, g_mca, sh_mlp, sc_mlp, g_mlp = [m[:, i * C:(i + 1) * C][:, None, :] for i in range(9)]
        h = _ln(x) * (1 + sc_msa) + sh_msa
        h = _self_attn(h, w_qkv, b_qkv, w_so, b_so)
        x = x + h * g_msa
        h = _ln(x) * (1 + sc_mca) + sh_mca
        h = _topk_cross_attn(h, context, w_q, b_q, w_kv, b_kv, w_co, b_co)
        x = x + h * g_mca
        h = _ln(x) * (1 + sc_mlp) + sh_mlp
        h = _swiglu(h, w_m1, b_m1, w_m2, b_m2)
        x = x + h * g_mlp
        return x

    def _L1_xcond_ref(mix_hidden_states, global_anchor, prototype_bank, ln_gamma, ln_beta, Wq, Wk, Wv, router_W, router_b, e_w1, e_b1, e_w2, e_b2, gate_w1, gate_b1, gate_w2, gate_b2, out_w, out_b):
        import jax, jax.numpy as jnp
        import numpy as np
        H = 256
        RH = 2 * H
        E = 3
        B, T, P = (8, 512, 64)
        LN_EPS = 1e-05

        def _layer_norm(x, gamma, beta):
            mu = jnp.mean(x, axis=-1, keepdims=True)
            var = jnp.mean(jnp.square(x - mu), axis=-1, keepdims=True)
            return (x - mu) * jax.lax.rsqrt(var + LN_EPS) * gamma + beta
        x = mix_hidden_states
        nx = _layer_norm(x, ln_gamma, ln_beta)
        q = nx @ Wq
        k = prototype_bank @ Wk
        v = prototype_bank @ Wv
        scores = jnp.einsum('bth,bph->btp', q, k) * H ** (-0.5)
        weights = jax.nn.softmax(scores, axis=-1)
        evidence = jnp.einsum('btp,bph->bth', weights, v)
        anchor = jnp.broadcast_to(global_anchor[:, None, :], nx.shape)
        combined = jnp.concatenate([nx, evidence, anchor], axis=-1)
        router_logits = combined @ router_W + router_b
        router_probs = jax.nn.softmax(router_logits, axis=-1)
        h = jax.nn.silu(jnp.einsum('btc,ecr->bter', combined, e_w1) + e_b1)
        expert_out = jnp.einsum('bter,erh->bteh', h, e_w2) + e_b2
        routed = jnp.sum(expert_out * router_probs[..., None], axis=-2)
        g = jax.nn.sigmoid(jax.nn.silu(combined @ gate_w1 + gate_b1) @ gate_w2 + gate_b2)
        refined_delta = g * (routed @ out_w + out_b)
        return x + refined_delta
    x = _L0_xcond_ref(x, cond_1024, ctx_1024, L0_xcond_w_ada, L0_xcond_b_ada, L0_xcond_w_qkv, L0_xcond_b_qkv, L0_xcond_w_so, L0_xcond_b_so, L0_xcond_w_q, L0_xcond_b_q, L0_xcond_w_kv, L0_xcond_b_kv, L0_xcond_w_co, L0_xcond_b_co, L0_xcond_w_m1, L0_xcond_b_m1, L0_xcond_w_m2, L0_xcond_b_m2)
    x = _L1_xcond_ref(x, cond_1024, ctx_1024, L1_xcond_ln_gamma, L1_xcond_ln_beta, L1_xcond_Wq, L1_xcond_Wk, L1_xcond_Wv, L1_xcond_router_W, L1_xcond_router_b, L1_xcond_e_w1, L1_xcond_e_b1, L1_xcond_e_w2, L1_xcond_e_b2, L1_xcond_gate_w1, L1_xcond_gate_b1, L1_xcond_gate_w2, L1_xcond_gate_b2, L1_xcond_out_w, L1_xcond_out_b)
    return x

_drawn_inputs = setup_inputs


def setup_inputs(seed=0):
    import zlib

    import numpy as np

    out = dict(_drawn_inputs(seed))
    spreads = {'L0_xcond_b_ada': (0.0, 0.394),
     'L0_xcond_b_qkv': (0.0, 0.8),
     'L0_xcond_b_so': (0.0, 0.372),
     'L0_xcond_b_q': (0.0, 0.8),
     'L0_xcond_b_kv': (0.0, 0.8),
     'L0_xcond_b_co': (0.0, 0.402),
     'L0_xcond_b_m1': (0.0, 0.8),
     'L0_xcond_b_m2': (0.0, 1.444),
     'L1_xcond_ln_gamma': (1.0, 0.6),
     'L1_xcond_ln_beta': (0.0, 2.0),
     'L1_xcond_router_b': (0.0, 2.0),
     'L1_xcond_e_b1': (0.0, 2.0),
     'L1_xcond_e_b2': (0.0, 0.8),
     'L1_xcond_gate_b1': (0.0, 2.0),
     'L1_xcond_gate_b2': (0.0, 2.0),
     'L1_xcond_out_b': (0.0, 0.8)}
    factors = {'L0_xcond_w_qkv': 8.0,
     'L0_xcond_w_so': 6.053,
     'L0_xcond_w_q': 6.219,
     'L0_xcond_w_kv': 3.805,
     'L0_xcond_w_co': 3.446,
     'L0_xcond_w_m1': 6.193,
     'L0_xcond_w_m2': 6.176,
     'L1_xcond_Wq': 8.0,
     'L1_xcond_Wk': 8.0,
     'L1_xcond_Wv': 4.6,
     'L1_xcond_router_W': 3.385,
     'L1_xcond_gate_w1': 6.784,
     'L1_xcond_gate_w2': 5.203}
    for name, (base, spread) in spreads.items():
        noise = np.random.default_rng([zlib.crc32(name.encode()), seed]).standard_normal(out[name].shape)
        drawn = base * np.exp(spread * noise) if base else spread * noise
        out[name] = jnp.asarray(drawn.astype(out[name].dtype))
    for name, factor in factors.items():
        out[name] = (out[name] * factor).astype(out[name].dtype)
    return out
```

```python
from contextlib import ExitStack

import concourse.bass as bass
from concourse import mybir
import numpy as np

F32 = mybir.dt.float32
ACT = mybir.ActivationFunctionType
ALU = mybir.AluOpType
AX = mybir.AxisListType

P = 128
C = 256
KC = C // P
G = 4
T = G * P
H = 16
D = C // H
HID = 1024
E = 3
RH = 2 * C
EC = E * RH // P
MC = HID // P
TOPK = 16
GONE = float(np.float32(-3.0e38))
EPS0, EPS1 = 1e-6, 1e-5

SH1, SC1, GA1, SH2, SC2, GA2, SH3, SC3, GA3 = range(0, 18, 2)
GB1, GB2, GB3 = 18, 20, 22
N_SMALL, N_FOLD, N_MAIN, SETUP_FILLS = 18, 11, 12, 36
EB = 24
GB = EB + EC
NV = GB + 2

UNITS = 2 * G


def attention_steps(n):
    ks = range(n * UNITS, (n + 1) * UNITS)
    return [(s, k) for k in ks for s in ("unit_a", "unit_b")] + [("last_a", ks[-1]), ("last_b", ks[-1])]


STAGE_A = (
    [("ln", 1), ("turn_x", 1), ("q", 1), ("k", 1), ("v", 1), ("first_scores", 0)]
    + attention_steps(0)
    + [("turn_o", 1), ("k", 2), ("project", 1), ("v", 2), ("residual", 1), ("ln", 2), ("turn_x", 2), ("q", 2),
       ("first_scores", UNITS)]
    + attention_steps(1)
    + [("turn_o", 2), ("project", 2), ("residual", 2)]
)
STAGE_B = (
    [("lnb", 3), ("turn_b", 3)]
    + [(s, m) for m in range(MC) for s in ("mlp_a", "mlp_b")]
    + [("mlp_down", i) for i in range(MC)]
    + [("residual_b", 0), ("lnb", 4), ("turn_b", 4), ("query", 0), ("query", 1), ("match", 0), ("normalise", 0)]
    + [("weights", 0), ("evidence", 0), ("evidence", 1), ("router", 0), ("router_turn", 0), ("route", 0)]
    + [(s, j) for j in range(EC + 2) for s in ("expert_x", "expert_v")] + [("expert_end", 0)]
    + [(s, b) for b in range(G) for s in ("mix0", "mix1", "add")]
)


def weight(step):
    return 5 if step[0] in ("unit_a", "unit_b") and step[1] >= UNITS else 3


def merged():
    out, b = [], 0
    total = sum(weight(s) for s in STAGE_A)
    seen = 0
    for s in STAGE_A:
        out.append(("A", s))
        seen += weight(s)
        while b < len(STAGE_B) and b * total < seen * len(STAGE_B):
            out.append(("B", STAGE_B[b]))
            b += 1
    return out + [("B", s) for s in STAGE_B[b:]]


ONLY_A = [("A", s) for s in STAGE_A]
ONLY_B = [("B", s) for s in STAGE_B]
BOTH = merged()


def uses(names, banks):
    count, out = {b: 0 for b in banks}, {}
    for i, name in enumerate(names):
        b = banks[i % len(banks)]
        out[name] = (b, count[b])
        count[b] += 1
    return out


def two(*names):
    return [(n, i) for n in names for i in range(2)]


A_BEFORE = two("ctx", "x1", "q1", "k1", "v1")
A_BETWEEN = two("o1", "k2", "y1", "v2", "r1", "x2", "q2")
A_AFTER = two("o2", "y2", "r2")
A_USE = uses(A_BEFORE + A_BETWEEN + A_AFTER, (4, 5))
B_USE = uses(
    two("x3")
    + [(n, m) for m in range(MC) for n in ("a", "b")]
    + two("down", "r3", "x4", "query") + [("match", 0), ("weights", 0)] + two("evidence")
    + [("router", 0), ("router", 1)] + [("expert", j) for j in range(EC + 2)]
    + [("mix", 2 * b + i) for b in range(G) for i in range(2)],
    (6, 7),
)


def slot_of(h):
    c, g, e = h // 8, h % 8 // 2, h % 2
    return 4 * g + 2 * c + e


HEAD_AT = sorted(range(H), key=slot_of)


def program(nc, t, out):
    B = t["x"].shape[0]
    NG = B // G
    ctx = ExitStack()
    with ctx:
        def sb(name, shape):
            return ctx.enter_context(nc.sbuf_tensor(name, shape, F32))

        ident = sb("ident", [P, P])
        w_qkv = sb("w_qkv", [P, KC, 3 * C])
        w_so = sb("w_so", [P, KC, C])
        w_q = sb("w_q", [P, KC, C])
        w_kv = sb("w_kv", [P, KC, 2 * C])
        w_co = sb("w_co", [P, KC, C])
        w_m1 = sb("w_m1", [P, KC, 2 * HID])
        w_m2 = sb("w_m2", [P, MC, C])
        w_query = sb("w_query", [P, KC, C])
        w_r = sb("w_r", [P, 2 * KC, E])
        w_e1 = sb("w_e1", [P, 2 * KC, E * RH])
        w_g1 = sb("w_g1", [P, 2 * KC, C])
        w_g2 = sb("w_g2", [P, KC, C])
        w_e2 = sb("w_e2", [P, EC, C])
        bias_rows = sb("bias_rows", [E + 1, C])
        row_of = sb("row_of", [E + 1, E + 1, P])
        router_b = sb("router_b", [E, NG, G])
        vec_a = sb("vec_a", [P, NV, G])
        vec_b = sb("vec_b", [P, NV, G])
        rb_b = sb("rb_b", [E, G])
        minus_half = sb("minus_half", [P, G])
        b_qkv = sb("b_qkv", [P, 6])
        b_q = sb("b_q", [P, 2])
        b_kv = sb("b_kv", [P, 4])
        b_out = sb("b_out", [P, 6])
        b_m1 = sb("b_m1", [P, 2 * MC])
        b_m1h = sb("b_m1h", [P, 2 * MC])
        gamma = sb("gamma", [P, KC])
        beta = sb("beta", [P, KC])
        head_mask = sb("head_mask", [P, 2])
        b_k = sb("b_k", [P, 2, 2, KC])

        with ExitStack() as early:
            def st(name, shape):
                return early.enter_context(nc.sbuf_tensor(name, shape, F32))

            w_ada = st("w_ada", [P, KC, 9 * C])
            e1_anchor = st("e1_anchor", [P, KC, E * RH])
            e1_ev = st("e1_ev", [P, KC, E * RH])
            g1_raw = st("g1_raw", [P, 2 * KC, C])
            r_raw = st("r_raw", [P, 2 * KC, E])
            Wq = st("Wq", [P, KC, C])
            Wk = st("Wk", [P, KC, C])
            Wv = st("Wv", [P, KC, C])
            out_w = st("out_w", [P, KC, C])
            WqT = st("WqT", [P, KC, C])
            WkT = st("WkT", [P, KC, C])
            WvT = st("WvT", [P, KC, C])
            e2 = st("e2", [P, EC, C])
            e2T = st("e2T", [P, KC, EC * P])
            eb2T = st("eb2T", [P, KC, E])
            out_b3 = st("out_b3", [E, C])
            vectors = st("vectors", [P, NG, NV, G])
            cond = st("cond", [B, C])
            cond_silu = st("cond_silu", [B, C])
            cond_th = st("cond_th", [B, C])
            condT = st("condT", [P, KC, B])
            siluT = st("siluT", [P, KC, B])
            b_ada = st("b_ada", [P, 18])
            b_e1 = st("b_e1", [P, EC + 2])
            b_r = st("b_r", [E, 1])

        x_in = sb("x_in", [P, G, C])
        ctx_a = sb("ctx_a", [P, G, C])
        ctxT_a = sb("ctxT_a", [P, KC, T])
        xn = sb("xn", [P, G, C])
        o_tok = xn
        hT = sb("hT", [P, KC, T])
        yT = hT
        qT = sb("qT", [P, KC, T])
        oT = qT
        kM = sb("kM", [P, KC, G, 2, P])
        v1 = sb("v1", [P, G, H, D + 1])
        stats = sb("stats", [P, G, 6])
        mean_var = sb("mean_var", [P, G, 2])
        var_eps = sb("var_eps", [P, G])
        rstd = sb("rstd", [P, G])
        top1 = sb("top1", [P, 8, 8])
        top2 = sb("top2", [P, 8, 8])
        rowmax = sb("rowmax", [P, 8])
        neg_max = sb("neg_max", [P, 2, 8])
        left = sb("left", [P, 8, P])
        prob = sb("prob", [P, 2, 8, P])
        probT = sb("probT", [P, 8, P])
        o_inv = sb("o_inv", [P, H])
        x1 = sb("x1", [P, G, C])
        x_mid = x1
        ctx_b = sb("ctx_b", [P, G, C])
        ctxT_b = sb("ctxT_b", [P, KC, T])
        xnb = sb("xnb", [P, G, C])
        qs = xnb[:, :, :].rearrange("p (k g) c -> p k (g c)", k=KC)
        evT = qs
        mix = xnb
        hB = sb("hB", [P, KC, T])
        z = sb("z", [P, 2, T])
        th = sb("th", [P, 2, T])
        hidden = sb("hidden", [P, EC + 2, T])
        x2 = sb("x2", [P, G, C])
        stats_b = sb("stats_b", [P, G, 6])
        mean_var_b = sb("mean_var_b", [P, G, 2])
        var_eps_b = sb("var_eps_b", [P, G])
        rstd_b = sb("rstd_b", [P, G])
        wgt = z[:, 0, :].rearrange("p (b n) -> p b n", b=G)
        wgtT = z[:, 1, :]
        w_max = sb("w_max", [P, G])
        w_sum = sb("w_sum", [P, G])
        logitT = th[0:E, 0, :]
        logit = sb("logit", [P, G, E])
        l_max = sb("l_max", [P, G])
        l_exp = sb("l_exp", [P, G, E])
        l_sum = sb("l_sum", [P, G])
        route = sb("route", [P, G, E])
        gate_th = z[:, 0, :].rearrange("p (i c) -> p i c", i=2)

        bank = [ctx.enter_context(nc.psum_tensor(f"bank{i}", [P, T], F32)) for i in range(4, 8)]
        bank = {i + 4: b for i, b in enumerate(bank)}
        score = ctx.enter_context(nc.psum_tensor("score", [P, 2, 8, P], F32))

        def sem(name):
            return ctx.enter_context(nc.semaphore(name))

        go, seen = sem("go"), sem("seen")
        s_small, s_ada, s_fold, s_main, s_group, s_vectors = (
            sem(n) for n in ("s_small", "s_ada", "s_fold", "s_main", "s_group", "s_vectors"))
        s_fill, s_drain = sem("s_fill"), sem("s_drain")
        s_const, s_dve, s_act, s_ready = sem("s_const"), sem("s_dve"), sem("s_act"), sem("s_ready")
        names = ("arrived filled4 filled5 filled6 filled7 drained4 drained5 drained6 drained7 "
                 "vec_a_loaded vec_b_loaded rb_ready var_ready rstd_ready xn_ready var_ready_b rstd_ready_b xn_ready_b "
                 "scored maxed exped picked turned copied valued o_ready dve_step act_step "
                 "th_ready hidden_ready wmax_ready wgt_ready lexp_ready "
                 "gate_ready summed loaded moved stored").split()
        R = {n: sem(n) for n in names}
        nums = [R[n].num for n in names]
        round_sems = range(min(nums), max(nums) + 1)
        assert len(round_sems) == len(names)
        filled = {i: R[f"filled{i}"] for i in (4, 5, 6, 7)}
        drained = {i: R[f"drained{i}"] for i in (4, 5, 6, 7)}

        def all_o_before(name):
            return {True: 0}.get(name in A_BEFORE, G if name in A_BETWEEN else 2 * G)

        vectors_d = nc.dram_tensor("vectors_d", [NG, P, NV * G], F32, kind="Internal").ap()
        x_d = t["x"].rearrange("(n g) l c -> n l g c", g=G)
        ctx_d = t["ctx_1024"].rearrange("(n g) l c -> n l g c", g=G)
        out_d = out.rearrange("(n g) l c -> n g l c", g=G)

        def rows(a):
            return a.rearrange("(k p) n -> p k n", p=P)

        def cols(a):
            return a.rearrange("(m p) -> p m", p=P)

        e_w1 = t["L1_xcond_e_w1"]
        g_w1 = rows(t["L1_xcond_gate_w1"])
        r_w = rows(t["L1_xcond_router_W"])

        def e1_part(part):
            return [rows(e_w1[e])[:, KC * part:KC * part + KC, :] for e in range(E)]

        block = ctx.enter_context(nc.Block())

        @block.sync
        def _(sp):
            n_small = 0
            for dst, src in [
                (cond[:, :], t["cond_1024"]), (b_ada[:, :], cols(t["L0_xcond_b_ada"])),
                (b_e1[:, 0:EC], t["L1_xcond_e_b1"].rearrange("e (m p) -> p (e m)", p=P)),
                (b_e1[:, EC:EC + 2], cols(t["L1_xcond_gate_b1"])),
                (b_r[:, :], t["L1_xcond_router_b"].rearrange("(e a) -> e a", a=1)),
                (b_qkv[:, :], cols(t["L0_xcond_b_qkv"])), (b_q[:, :], cols(t["L0_xcond_b_q"])),
                (b_kv[:, :], cols(t["L0_xcond_b_kv"])), (b_out[:, 0:2], cols(t["L0_xcond_b_so"])),
                (b_out[:, 2:4], cols(t["L0_xcond_b_co"])), (b_out[:, 4:6], cols(t["L0_xcond_b_m2"])),
                (b_m1[:, :], cols(t["L0_xcond_b_m1"])),
                (gamma[:, :], cols(t["L1_xcond_ln_gamma"])), (beta[:, :], cols(t["L1_xcond_ln_beta"])),
                (eb2T[:, 0, :], t["L1_xcond_e_b2"].rearrange("e (k p) -> p k e", p=P)[:, 0, :]),
                (eb2T[:, 1, :], t["L1_xcond_e_b2"].rearrange("e (k p) -> p k e", p=P)[:, 1, :]),
                (out_b3[:, :], t["L1_xcond_out_b"].rearrange("(a n) -> a n", a=1).to_broadcast([E, C])),
                (bias_rows[E:E + 1, :], t["L1_xcond_gate_b2"].rearrange("(a n) -> a n", a=1)),
            ]:
                sp.dma_start(dst, src, allow_slow_non_contiguous=True).then_inc(s_small, 16)
                n_small += 1
            assert n_small == N_SMALL
            sp.dma_start(w_ada[:, :, :], rows(t["L0_xcond_w_ada"])).then_inc(s_ada, 16)
            for e, src in enumerate(e1_part(2)):
                sp.dma_start(e1_anchor[:, :, e * RH:(e + 1) * RH], src).then_inc(s_ada, 16)
            sp.dma_start(g1_raw[:, :, :], g_w1[:, KC:, :]).then_inc(s_ada, 16)
            sp.dma_start(r_raw[:, :, :], r_w[:, KC:, :]).then_inc(s_ada, 16)
            for dst, name in ((Wq, "Wq"), (Wk, "Wk"), (Wv, "Wv"), (out_w, "out_w"), (w_g2, "gate_w2")):
                sp.dma_start(dst[:, :, :], rows(t[f"L1_xcond_{name}"])).then_inc(s_fold, 16)
            for e, src in enumerate(e1_part(1)):
                sp.dma_start(e1_ev[:, :, e * RH:(e + 1) * RH], src).then_inc(s_fold, 16)
            for e in range(E):
                sp.dma_start(e2[:, 4 * e:4 * e + 4, :], rows(t["L1_xcond_e_w2"][e])).then_inc(s_fold, 16)
            for dst, name in ((w_qkv, "w_qkv"), (w_so, "w_so"), (w_q, "w_q"), (w_kv, "w_kv"), (w_co, "w_co"),
                              (w_m1, "w_m1"), (w_m2, "w_m2")):
                sp.dma_start(dst[:, :, :], rows(t[f"L0_xcond_{name}"])).then_inc(s_main, 16)
            for e, src in enumerate(e1_part(0)):
                sp.dma_start(w_e1[:, 0:KC, e * RH:(e + 1) * RH], src).then_inc(s_main, 16)
            sp.dma_start(w_g1[:, 0:KC, :], g_w1[:, 0:KC, :]).then_inc(s_main, 16)
            sp.dma_start(w_r[:, 0:KC, :], r_w[:, 0:KC, :]).then_inc(s_main, 16)
            sp.wait_ge(s_ready, 4)
            sp.dma_start(vectors_d.rearrange("n p v -> p n v"), vectors[:, :, :, :].rearrange("p n v g -> p n (v g)"))\
                .then_inc(s_vectors, 16)
            sp.wait_ge(s_vectors, 16)
            sp.dma_start(x_in[:, :, :], x_d[0]).then_inc(s_group, 16)
            sp.dma_start(ctx_a[:, :, :], ctx_d[0]).then_inc(s_group, 16)
            sp.wait_ge(s_group, 32)
            sp.wait_ge(s_main, 16 * N_MAIN)
            sp.sem_inc(go)

            def after(use):
                b, n = use
                sp.wait_ge(drained[b], n + 1)

            def round_(with_a, with_b, next_a, group_b):
                if with_a:
                    sp.dma_start(vec_a[:, :, :].rearrange("p v g -> p (v g)"), vectors_d[group_b + 1])\
                        .then_inc(R["vec_a_loaded"], 16)
                if with_b:
                    sp.dma_start(vec_b[:, :, :].rearrange("p v g -> p (v g)"), vectors_d[group_b])\
                        .then_inc(R["vec_b_loaded"], 16)
                if with_a:
                    after(A_USE["r1", 1])
                    sp.dma_start(x_in[:, :, :], x_d[next_a]).then_inc(R["loaded"], 16)
                    after(A_USE["v2", 1])
                    sp.wait_ge(filled[A_USE["k2", 1][0]], A_USE["k2", 1][1] + 1)
                    if with_b:
                        after(B_USE["evidence", 1])
                    sp.dma_start(ctx_b[:, :, :], ctx_a[:, :, :]).then_inc(R["moved"], 16)
                    sp.dma_start(ctxT_b[:, :, :], ctxT_a[:, :, :]).then_inc(R["moved"], 16)
                    sp.wait_ge(R["moved"], 32)
                    sp.dma_start(ctx_a[:, :, :], ctx_d[next_a]).then_inc(R["loaded"], 16)
                if with_b:
                    for b in range(G):
                        sp.wait_ge(R["summed"], b + 1)
                        sp.dma_start(out_d[group_b, b], mix[:, b, :]).then_inc(R["stored"], 16)
                    sp.wait_ge(R["stored"], 16 * G)
                if with_a:
                    sp.wait_ge(R["loaded"], 32)
                sp.wait_ge(R["arrived"], 4)
                sp.sem_clear(round_sems)
                sp.sem_inc(go)

            round_(True, False, 1 % NG, -1)
            with sp.Fori(1, NG) as i:
                round_(True, True, (i + 1) % NG, i - 1)
            round_(False, True, None, NG - 1)

        def enter(eng, n):
            eng.wait_ge(go, n)
            eng.sem_inc(seen)

        def leave(eng):
            eng.drain().then_inc(R["arrived"], 1)

        @block.gpsimd
        def _(pool):
            pool.memset(minus_half[:, :], -0.5).then_inc(s_const, 1)
            pool.memset(ident[:, :], 0.0).then_inc(s_const, 1)
            pool.memset(row_of[:, :, :], 0.0).then_inc(s_const, 1)
            pool.wait_ge(s_const, 3)
            pool.affine_select(out=ident[:, :], in_=ident[:, :], compare_op=ALU.not_equal, fill=1.0, base=0,
                               pattern=[[-1, P]], channel_multiplier=1).then_inc(s_const, 1)
            pool.affine_select(out=row_of[:, :, :], in_=row_of[:, :, :], compare_op=ALU.not_equal, fill=1.0,
                               base=0, pattern=[[-1, E + 1], [0, P]], channel_multiplier=1).then_inc(s_const, 1)
            pool.drain().then_inc(s_ready, 1)

            def round_(steps, n, group_b):
                enter(pool, n)
                if group_b is None:
                    pool.memset(v1[:, :, :, D:D + 1], 1.0).then_inc(s_const, 1)
                else:
                    pool.tensor_copy(rb_b[:, :], router_b[:, group_b, :]).then_inc(R["rb_ready"], 1)
                for stage, (name, k) in steps:
                    if name == "ln":
                        pool.wait_ge(R["var_ready"], k)
                        pool.tensor_tensor(rstd[:, :], var_eps[:, :], minus_half[:, :], ALU.pow)\
                            .then_inc(R["rstd_ready"], 1)
                    elif name == "lnb":
                        pool.wait_ge(R["var_ready_b"], k - 2)
                        pool.tensor_tensor(rstd_b[:, :], var_eps_b[:, :], minus_half[:, :], ALU.pow)\
                            .then_inc(R["rstd_ready_b"], 1)
                    elif name == "add":
                        b, n_ = B_USE["mix", 2 * k + 1]
                        pool.wait_ge(drained[b], n_ + 1)
                        pool.tensor_tensor(mix[:, k, :], mix[:, k, :], x2[:, k, :], ALU.add)\
                            .then_inc(R["summed"], 1)
                leave(pool)

            round_(ONLY_A, 1, None)
            with pool.Fori(1, NG) as i:
                round_(BOTH, i + 1, i - 1)
            round_(ONLY_B, NG + 1, NG - 1)

        @block.tensor
        def _(pe):
            mm = nc.tensor.matmul

            fills = [0]

            def begin():
                if fills[0] >= 4:
                    pe.wait_ge(s_drain, fills[0] - 3)
                return bank[4 + fills[0] % 4]

            def end(ins):
                ins.then_inc(s_fill, 1)
                fills[0] += 1

            pe.wait_ge(s_const, 5)
            pe.wait_ge(s_dve, 1)
            ps = begin()
            for i, a in enumerate((cond, cond_silu)):
                for c in range(KC):
                    last = nc.tensor.transpose(ps[:, (2 * i + c) * B:(2 * i + c + 1) * B], a[:, c * P:(c + 1) * P],
                                               ident[0:B, 0:B])
            end(last)
            pe.wait_ge(s_ada, 16 * 6)
            pe.wait_ge(s_drain, 1)
            for m in range(18):
                if m % 4 == 0:
                    ps = begin()
                for kk in range(KC):
                    last = mm(ps[:, m % 4 * B:(m % 4 + 1) * B], w_ada[:, kk, m * P:(m + 1) * P], siluT[:, kk, :],
                              start=kk == 0, stop=kk == KC - 1)
                if m % 4 == 3 or m == 17:
                    end(last)
            for j in range(EC + 2):
                if j % 4 == 0:
                    ps = begin()
                for kk in range(KC):
                    w = e1_anchor[:, kk, j * P:(j + 1) * P] if j < EC else \
                        g1_raw[:, KC + kk, (j - EC) * P:(j - EC + 1) * P]
                    last = mm(ps[:, j % 4 * B:(j % 4 + 1) * B], w, condT[:, kk, :], start=kk == 0, stop=kk == KC - 1)
                if j % 4 == 3 or j == EC + 1:
                    end(last)
            ps = begin()
            for kk in range(KC):
                last = mm(ps[0:E, 0:B], r_raw[:, KC + kk, :], condT[:, kk, :], start=kk == 0, stop=kk == KC - 1)
            end(last)
            pe.wait_ge(s_fold, 16 * N_FOLD)
            for a in (Wq, Wk, Wv):
                ps = begin()
                for jj in range(KC):
                    for kk in range(KC):
                        last = nc.tensor.transpose(ps[:, (jj * KC + kk) * P:(jj * KC + kk + 1) * P],
                                                   a[:, kk, jj * P:(jj + 1) * P], ident[:, :])
                end(last)
            for i in range(EC // 2):
                ps = begin()
                for c in range(KC):
                    for r in range(2):
                        last = nc.tensor.transpose(ps[:, (c * 2 + r) * P:(c * 2 + r + 1) * P],
                                                   e2[:, 2 * i + r, c * P:(c + 1) * P], ident[:, :])
                end(last)
            pe.wait_ge(s_drain, fills[0])
            ps = begin()
            for kk in range(KC):
                for jj in range(KC):
                    last = mm(ps[:, kk * C:(kk + 1) * C], WqT[:, jj, kk * P:(kk + 1) * P], WkT[:, jj, :],
                              start=jj == 0, stop=jj == KC - 1)
            end(last)
            for kk in range(KC):
                for e in range(E):
                    ps = begin()
                    for jj in range(KC):
                        last = mm(ps[:, :], WvT[:, jj, kk * P:(kk + 1) * P], e1_ev[:, jj, e * RH:(e + 1) * RH],
                                  start=jj == 0, stop=jj == KC - 1)
                    end(last)
            ps = begin()
            for kk in range(KC):
                for jj in range(KC):
                    last = mm(ps[:, kk * C:(kk + 1) * C], WvT[:, jj, kk * P:(kk + 1) * P], g1_raw[:, jj, :],
                              start=jj == 0, stop=jj == KC - 1)
            end(last)
            ps = begin()
            for kk in range(KC):
                for jj in range(KC):
                    last = mm(ps[:, kk * E:(kk + 1) * E], WvT[:, jj, kk * P:(kk + 1) * P], r_raw[:, jj, :],
                              start=jj == 0, stop=jj == KC - 1)
            end(last)
            for i in range(EC // 2):
                ps = begin()
                for r in range(2):
                    for c in range(KC):
                        last = mm(ps[:, r * C:(r + 1) * C], e2T[:, c, (2 * i + r) * P:(2 * i + r + 1) * P],
                                  out_w[:, c, :], start=c == 0, stop=c == KC - 1)
                end(last)
            ps = begin()
            for c in range(KC):
                last = mm(ps[0:E, 0:C], eb2T[:, c, :], out_w[:, c, :], start=c == 0, stop=c == KC - 1)
            end(last)
            assert fills[0] == SETUP_FILLS
            pe.drain().then_inc(s_ready, 1)

            def fill_a(name):
                b, n = A_USE[name]
                if n:
                    pe.wait_ge(drained[b], n)
                if b == 5 and all_o_before(name):
                    pe.wait_ge(R["o_ready"], all_o_before(name))
                return bank[b], filled[b]

            def fill_b(name):
                b, n = B_USE[name]
                if n:
                    pe.wait_ge(drained[b], n)
                return bank[b], filled[b]

            def has(use):
                pe.wait_ge(drained[use[0]], use[1] + 1)

            def scores(k):
                b, half = k % UNITS // 2, k % 2
                if k >= 2:
                    pe.wait_ge(R["copied"], k - 1)
                for g in range(2):
                    for c in range(KC):
                        r = slice(32 * (2 * half + g), 32 * (2 * half + g) + 32)
                        last = mm(score[:, k % 2, 4 * g + 2 * c:4 * g + 2 * c + 2, :].rearrange("p e n -> p (e n)"),
                                  qT[r, c, b * P:(b + 1) * P],
                                  kM[r, c, b, :, :].rearrange("p e n -> p (e n)"), start=True, stop=True)
                last.then_inc(R["scored"], 1)

            def turn_probs(k):
                if k < UNITS:
                    pe.wait_ge(R["exped"], 2 * k + 2)
                else:
                    pe.wait_ge(R["picked"], k - UNITS + 1)
                for j in range(8):
                    last = nc.tensor.transpose(score[:, k % 2, j, :], prob[:, k % 2, j, :], ident[:, :])
                last.then_inc(R["turned"], 1)

            def values(k):
                b, half = k % UNITS // 2, k % 2
                pe.wait_ge(R["copied"], k + 1)
                if half == 0:
                    n = k // 2
                    if n:
                        pe.wait_ge(R["o_ready"], n)
                    if n % G == 0:
                        u = A_USE[[a for a in (A_BETWEEN if n else A_BEFORE) if A_USE[a][0] == 5][-1]]
                        has(u)
                for j in range(8):
                    h = HEAD_AT[8 * half + j]
                    last = mm(bank[5][:, h * (D + 1):(h + 1) * (D + 1)], probT[:, j, :], v1[:, b, h, :],
                              start=True, stop=True)
                last.then_inc(R["valued"], 1)

            def project(names, weight, c0, source):
                for m in range(KC):
                    ps, f = fill_a((names, m))
                    for kk in range(KC):
                        last = mm(ps[:, :], weight[:, kk, c0 + m * P:c0 + (m + 1) * P], source[:, kk, :],
                                  start=kk == 0, stop=kk == KC - 1)
                    last.then_inc(f, 1)

            def turn(names, source, fill):
                for c in range(KC):
                    ps, f = fill((names, c))
                    for b in range(G):
                        last = nc.tensor.transpose(ps[:, b * P:(b + 1) * P], source[:, b, c * P:(c + 1) * P],
                                                   ident[:, :])
                    last.then_inc(f, 1)

            def turn_back(names, source, fill):
                for p in range(2):
                    ps, f = fill((names, p))
                    for b in range(2):
                        for c in range(KC):
                            last = nc.tensor.transpose(ps[:, b * C + c * P:b * C + (c + 1) * P],
                                                       source[:, c, (2 * p + b) * P:(2 * p + b + 1) * P], ident[:, :])
                    last.then_inc(f, 1)

            def step_a(name, k):
                if name == "ln" and k == 1:
                    turn("ctx", ctx_a, fill_a)
                elif name == "turn_x":
                    pe.wait_ge(R["xn_ready"], k)
                    turn(f"x{k}", xn, fill_a)
                elif name == "q":
                    has(A_USE[f"x{k}", 1])
                    has(A_USE[f"x{k}", 0])
                    project(f"q{k}", *((w_qkv, 0) if k == 1 else (w_q, 0)), hT)
                elif name == "k":
                    project(f"k{k}", *((w_qkv, C) if k == 1 else (w_kv, 0)), hT if k == 1 else ctxT_a)
                elif name == "v":
                    source, w, c0 = (hT, w_qkv, 2 * C) if k == 1 else (ctxT_a, w_kv, C)
                    for p in range(2):
                        ps, f = fill_a((f"v{k}", p))
                        for b in range(2):
                            for kk in range(KC):
                                last = mm(ps[:, b * C:(b + 1) * C],
                                          source[:, kk, (2 * p + b) * P:(2 * p + b + 1) * P],
                                          w[:, kk, c0:c0 + C], start=kk == 0, stop=kk == KC - 1)
                        last.then_inc(f, 1)
                elif name == "first_scores":
                    n = 1 if k == 0 else 2
                    for u in (f"q{n}", f"k{n}", f"v{n}"):
                        has(A_USE[u, 0])
                        has(A_USE[u, 1])
                    scores(k)
                elif name == "unit_a":
                    if k % UNITS:
                        turn_probs(k - 1)
                elif name == "unit_b":
                    if k % UNITS:
                        values(k - 1)
                    if (k + 1) % UNITS:
                        scores(k + 1)
                elif name == "last_a":
                    turn_probs(k)
                elif name == "last_b":
                    values(k)
                elif name == "turn_o":
                    pe.wait_ge(R["o_ready"], k * G)
                    turn(f"o{k}", o_tok, fill_a)
                elif name == "project":
                    has(A_USE[f"o{k}", 0])
                    has(A_USE[f"o{k}", 1])
                    project(f"y{k}", w_so if k == 1 else w_co, 0, oT)
                elif name == "residual":
                    has(A_USE[f"y{k}", 0])
                    has(A_USE[f"y{k}", 1])
                    turn_back(f"r{k}", yT, fill_a)

            def step_b(name, k):
                if name == "turn_b":
                    pe.wait_ge(R["xn_ready_b"], k - 2)
                    turn(f"x{k}", xnb, fill_b)
                elif name in ("mlp_a", "mlp_b"):
                    ps, f = fill_b((name[-1], k))
                    if (name, k) == ("mlp_a", 0):
                        has(B_USE["x3", 0])
                        has(B_USE["x3", 1])
                    c0 = (HID if name == "mlp_b" else 0) + k * P
                    for kk in range(KC):
                        last = mm(ps[:, :], w_m1[:, kk, c0:c0 + P], hB[:, kk, :], start=kk == 0, stop=kk == KC - 1)
                    last.then_inc(f, 1)
                elif name == "mlp_down":
                    m, quarter = k // 4, k % 4
                    if quarter == 0:
                        fill_b(("down", m))
                        has(B_USE["b", MC - 1])
                    b = B_USE["down", m][0]
                    for kk in (2 * quarter, 2 * quarter + 1):
                        last = mm(bank[b][:, :], w_m2[:, kk, m * P:(m + 1) * P], hidden[:, kk, :],
                                  start=kk == 0, stop=kk == MC - 1)
                    if quarter == 3:
                        last.then_inc(filled[b], 1)
                elif name == "residual_b":
                    has(B_USE["down", 0])
                    has(B_USE["down", 1])
                    turn_back("r3", hB, fill_b)
                elif name == "query":
                    ps, f = fill_b(("query", k))
                    if k == 0:
                        has(B_USE["x4", 0])
                        has(B_USE["x4", 1])
                    for kk in range(KC):
                        last = mm(ps[:, :], w_query[:, kk, k * P:(k + 1) * P], hB[:, kk, :],
                                  start=kk == 0, stop=kk == KC - 1)
                    last.then_inc(f, 1)
                elif name == "match":
                    ps, f = fill_b(("match", 0))
                    has(B_USE["query", 0])
                    has(B_USE["query", 1])
                    for b in range(G):
                        for kk in range(KC):
                            last = mm(ps[:, b * P:(b + 1) * P], qs[:, kk, b * P:(b + 1) * P],
                                      ctxT_b[:, kk, b * P:(b + 1) * P], start=kk == 0, stop=kk == KC - 1)
                    last.then_inc(f, 1)
                elif name == "weights":
                    ps, f = fill_b(("weights", 0))
                    pe.wait_ge(R["wgt_ready"], 1)
                    for b in range(G):
                        last = nc.tensor.transpose(ps[:, b * P:(b + 1) * P], wgt[:, b, :], ident[:, :])
                    last.then_inc(f, 1)
                elif name == "evidence":
                    ps, f = fill_b(("evidence", k))
                    has(B_USE["weights", 0])
                    for b in range(G):
                        last = mm(ps[:, b * P:(b + 1) * P], ctx_b[:, b, k * P:(k + 1) * P],
                                  wgtT[:, b * P:(b + 1) * P], start=True, stop=True)
                    last.then_inc(f, 1)
                elif name == "router":
                    ps, f = fill_b(("router", 0))
                    has(B_USE["evidence", 0])
                    has(B_USE["evidence", 1])
                    for kk in range(2 * KC):
                        source = hB if kk < KC else evT
                        last = mm(ps[0:E, :], w_r[:, kk, :], source[:, kk % KC, :], start=kk == 0,
                                  stop=kk == 2 * KC - 1)
                    last.then_inc(f, 1)
                elif name == "router_turn":
                    ps, f = fill_b(("router", 1))
                    has(B_USE["router", 0])
                    for b in range(G):
                        last = nc.tensor.transpose(ps[:, b * E:(b + 1) * E], logitT[:, b * P:(b + 1) * P],
                                                   ident[0:E, 0:E])
                    last.then_inc(f, 1)
                elif name in ("expert_x", "expert_v"):
                    w, c0 = (w_e1, k * P) if k < EC else (w_g1, (k - EC) * P)
                    if name == "expert_x":
                        fill_b(("expert", k))
                    b = B_USE["expert", k][0]
                    source, k0 = (hB, 0) if name == "expert_x" else (evT, KC)
                    for kk in range(KC):
                        last = mm(bank[b][:, :], w[:, k0 + kk, c0:c0 + P], source[:, kk, :],
                                  start=k0 + kk == 0, stop=k0 + kk == 2 * KC - 1)
                    if name == "expert_v":
                        last.then_inc(filled[b], 1)
                elif name in ("mix0", "mix1"):
                    half = int(name[-1])
                    ps, f = fill_b(("mix", 2 * k + half))
                    if k == half == 0:
                        pe.wait_ge(R["hidden_ready"], EC + 2)
                    for side in range(2):
                        e = 2 * half + side
                        chunks = range(4 * e, 4 * e + 4) if e < E else range(EC, EC + 2)
                        o = ps[:, side * C:(side + 1) * C]
                        for j in chunks:
                            w = w_e2[:, j, :] if e < E else w_g2[:, j - EC, :]
                            mm(o, hidden[:, j, k * P:(k + 1) * P], w, start=j == chunks[0], stop=False)
                        last = mm(o, row_of[:, e, :], bias_rows[:, :], start=False, stop=True)
                    last.then_inc(f, 1)

            def round_(steps, n):
                enter(pe, n)
                if steps is ONLY_A:
                    pe.wait_ge(s_const, 6)
                for stage, step in steps:
                    (step_a if stage == "A" else step_b)(*step)
                leave(pe)

            round_(ONLY_A, 1)
            with pe.Fori(1, NG) as i:
                round_(BOTH, i + 1)
            round_(ONLY_B, NG + 1)

        @block.scalar
        def _(act):
            f_ = nc.scalar.activation

            drains = [0]

            def begin():
                act.wait_ge(s_fill, drains[0] + 1)
                return bank[4 + drains[0] % 4]

            def end(ins):
                ins.then_inc(s_drain, 1)
                drains[0] += 1

            act.wait_ge(s_small, 16 * N_SMALL)
            f_(cond_th[:, :], cond[:, :], ACT.Tanh, scale=0.5).then_inc(s_act, 1)
            ps = begin()
            f_(condT[:, :, :].rearrange("p c b -> p (c b)"), ps[:, 0:KC * B], ACT.Copy)
            end(f_(siluT[:, :, :].rearrange("p c b -> p (c b)"), ps[:, KC * B:2 * KC * B], ACT.Copy, scale=0.5))

            def vector_rows(first, count, bias):
                for j in range(count):
                    if j % 4 == 0:
                        ps = begin()
                    ins = f_(vectors[:, :, first + j, :], ps[:, j % 4 * B:(j % 4 + 1) * B]
                             .rearrange("p (n g) -> p n g", g=G), ACT.Identity, bias=bias[:, j:j + 1])
                    if j % 4 == 3 or j == count - 1:
                        end(ins)

            vector_rows(0, 18, b_ada)
            vector_rows(EB, EC + 2, b_e1)
            ps = begin()
            end(f_(router_b[:, :, :], ps[0:E, 0:B].rearrange("p (n g) -> p n g", g=G), ACT.Identity,
                   bias=b_r[:, 0:1]))
            for a in (WqT, WkT, WvT):
                ps = begin()
                end(f_(a[:, :, :].rearrange("p c n -> p (c n)"), ps[:, :], ACT.Copy))
            for i in range(EC // 2):
                ps = begin()
                end(f_(e2T[:, :, 2 * i * P:(2 * i + 2) * P], ps[:, :].rearrange("p (c n) -> p c n", c=KC), ACT.Copy))
            ps = begin()
            end(f_(w_query[:, :, :].rearrange("p c n -> p (c n)"), ps[:, :], ACT.Copy, scale=float(C) ** -0.5))
            for kk in range(KC):
                for e in range(E):
                    ps = begin()
                    end(f_(w_e1[:, KC + kk, e * RH:(e + 1) * RH], ps[:, :], ACT.Copy))
            ps = begin()
            end(f_(w_g1[:, KC:, :].rearrange("p c n -> p (c n)"), ps[:, :], ACT.Copy))
            ps = begin()
            end(f_(w_r[:, KC:, :].rearrange("p c n -> p (c n)"), ps[:, 0:KC * E], ACT.Copy))
            for i in range(EC // 2):
                ps = begin()
                end(f_(w_e2[:, 2 * i:2 * i + 2, :].rearrange("p c n -> p (c n)"), ps[:, :], ACT.Copy, scale=0.5))
            ps = begin()
            end(f_(bias_rows[0:E, :], ps[0:E, 0:C], ACT.Copy))
            assert drains[0] == SETUP_FILLS
            act.drain().then_inc(s_ready, 1)

            def take(use):
                b, n = use
                act.wait_ge(filled[b], n + 1)
                return bank[b], drained[b]

            def modulated(dest, use, scale, shift, vec):
                ps, d = take(use)
                for b in range(G):
                    last = f_(dest[:, b * P:(b + 1) * P], ps[:, b * P:(b + 1) * P], ACT.Identity,
                              scale=vec[:, scale, b:b + 1], bias=vec[:, shift, b:b + 1])
                last.then_inc(d, 1)

            def copied(dest, use, **kw):
                ps, d = take(use)
                f_(dest, ps[:, :], ACT.Identity if kw else ACT.Copy, **kw).then_inc(d, 1)

            def exps(k, half):
                act.wait_ge(R["maxed"], 2 * k + half + 1)
                for j in range(4 * half, 4 * half + 4):
                    last = f_(prob[:, k % 2, j, :], score[:, k % 2, j, :], ACT.Exp,
                              scale=float(D) ** -0.5, bias=neg_max[:, k % 2, j:j + 1])
                last.then_inc(R["exped"], 1)

            def copy_turned(k):
                act.wait_ge(R["turned"], k + 1)
                if k:
                    act.wait_ge(R["valued"], k)
                f_(probT[:, :, :], score[:, k % 2, :, :], ACT.Copy).then_inc(R["copied"], 1)

            def step_a(name, k):
                if name == "ln" and k == 1:
                    for c in range(KC):
                        copied(ctxT_a[:, c, :], A_USE["ctx", c])
                elif name == "turn_x":
                    if k == 1:
                        act.wait_ge(R["vec_a_loaded"], 16)
                    for c in range(KC):
                        modulated(hT[:, c, :], A_USE[f"x{k}", c], (SC1, SC2)[k - 1] + c, (SH1, SH2)[k - 1] + c, vec_a)
                elif name == "q":
                    for c in range(KC):
                        copied(qT[:, c, :], A_USE[f"q{k}", c], bias=(b_qkv if k == 1 else b_q)[:, c:c + 1])
                elif name == "k":
                    for c in range(KC):
                        ps, d = take(A_USE[f"k{k}", c])
                        for e in range(2):
                            last = f_(kM[:, c, :, e, :], ps[:, :].rearrange("p (b n) -> p b n", b=G), ACT.Identity,
                                      scale=head_mask[:, e:e + 1], bias=b_k[:, k - 1, e, c:c + 1])
                        last.then_inc(d, 1)
                elif name == "unit_a":
                    if k % UNITS:
                        copy_turned(k - 1)
                    exps(k, 0)
                elif name == "unit_b":
                    exps(k, 1)
                elif name == "last_a":
                    copy_turned(k)
                elif name == "turn_o":
                    for c in range(KC):
                        copied(oT[:, c, :], A_USE[f"o{k}", c],
                               bias=b_qkv[:, 4 + c:5 + c] if k == 1 else b_kv[:, 2 + c:3 + c])
                elif name == "project":
                    for c in range(KC):
                        modulated(yT[:, c, :], A_USE[f"y{k}", c], (GA1, GA2)[k - 1] + c, (GB1, GB2)[k - 1] + c, vec_a)

            def step_b(name, k):
                if name == "turn_b":
                    if k == 3:
                        act.wait_ge(R["vec_b_loaded"], 16)
                    for c in range(KC):
                        if k == 3:
                            modulated(hB[:, c, :], B_USE["x3", c], SC3 + c, SH3 + c, vec_b)
                        else:
                            copied(hB[:, c, :], B_USE["x4", c], scale=gamma[:, c:c + 1], bias=beta[:, c:c + 1])
                elif name == "mlp_a":
                    ps, d = take(B_USE["a", k])
                    if k >= 2:
                        use = B_USE["b", k - 2]
                        act.wait_ge(drained[use[0]], use[1] + 1)
                    f_(z[:, k % 2, :], ps[:, :], ACT.Identity, bias=b_m1[:, k:k + 1])
                    f_(th[:, k % 2, :], ps[:, :], ACT.Tanh, scale=0.5, bias=b_m1h[:, k:k + 1]).then_inc(d, 1)
                elif name == "mlp_down" and k % 4 == 3:
                    m = k // 4
                    modulated(hB[:, m, :], B_USE["down", m], GA3 + m, GB3 + m, vec_b)
                elif name == "query":
                    copied(qs[:, k, :], B_USE["query", k])
                elif name == "match":
                    ps, d = take(B_USE["match", 0])
                    act.wait_ge(R["wmax_ready"], 1)
                    for b in range(G):
                        last = f_(wgt[:, b, :], ps[:, b * P:(b + 1) * P], ACT.Exp, bias=w_max[:, b:b + 1])
                    last.then_inc(d, 1)
                elif name == "weights":
                    copied(wgtT[:, :], B_USE["weights", 0])
                elif name == "evidence":
                    copied(evT[:, k, :], B_USE["evidence", k])
                elif name == "router":
                    ps, d = take(B_USE["router", 0])
                    act.wait_ge(R["rb_ready"], 1)
                    for b in range(G):
                        last = f_(logitT[:, b * P:(b + 1) * P], ps[0:E, b * P:(b + 1) * P], ACT.Identity,
                                  bias=rb_b[:, b:b + 1])
                    last.then_inc(d, 1)
                elif name == "router_turn":
                    b, n = B_USE["router", 1]
                    act.wait_ge(drained[b], n + 1)
                    f_(l_exp[:, :, :], logit[:, :, :], ACT.Exp).then_inc(R["lexp_ready"], 1)
                elif name == "expert_v":
                    b, n = B_USE["expert", k]
                    act.wait_ge(drained[b], n + 1)
                    f_(th[:, k % 2, :], z[:, k % 2, :], ACT.Tanh, scale=0.5).then_inc(R["th_ready"], 1)
                elif name == "mix1":
                    ps, d = take(B_USE["mix", 2 * k + 1])
                    if k >= 2:
                        b, n = B_USE["mix", 2 * k - 3]
                        act.wait_ge(drained[b], n + 1)
                    f_(gate_th[:, k % 2, :], ps[:, C:2 * C], ACT.Tanh, scale=0.5).then_inc(R["gate_ready"], 1)

            def round_(steps, n):
                enter(act, n)
                for stage, step in steps:
                    (step_a if stage == "A" else step_b)(*step)
                leave(act)

            round_(ONLY_A, 1)
            with act.Fori(1, NG) as i:
                round_(BOTH, i + 1)
            round_(ONLY_B, NG + 1)

        @block.vector
        def _(dve):
            v = nc.vector

            setup = [0]

            def done(ins):
                ins.then_inc(s_dve, 1)
                setup[0] += 1

            def settle():
                dve.wait_ge(s_dve, setup[0])

            dve.wait_ge(s_small, 16 * N_SMALL)
            dve.wait_ge(s_act, 1)
            done(v.scalar_tensor_tensor(cond_silu[:, :], cond_th[:, :], 1.0, cond[:, :], ALU.add, ALU.mult))
            dve.wait_ge(s_const, 5)
            for e in range(2):
                done(v.tensor_reduce(head_mask[:, e:e + 1],
                                     ident[:, :].rearrange("p (g e d) -> p e g d", e=2, d=D)[:, e],
                                     AX.XY, ALU.add))
            settle()
            for e in range(2):
                done(v.tensor_scalar(b_k[:, 0, e, :], b_qkv[:, 2:4], head_mask[:, e:e + 1], None, ALU.mult))
                done(v.tensor_scalar(b_k[:, 1, e, :], b_kv[:, 0:2], head_mask[:, e:e + 1], None, ALU.mult))
            done(v.tensor_scalar(b_m1h[:, :], b_m1[:, :], 0.5, None, ALU.mult))
            dve.wait_ge(s_drain, 1 + 5)
            for row in (SC1, SC2, SC3):
                done(v.tensor_scalar(vectors[:, :, row:row + 2, :], vectors[:, :, row:row + 2, :], 1.0, None,
                                     ALU.add))
            for i, (gate, gb) in enumerate(((GA1, GB1), (GA2, GB2), (GA3, GB3))):
                for c in range(KC):
                    done(v.tensor_scalar(vectors[:, :, gb + c, :], vectors[:, :, gate + c, :],
                                         b_out[:, 2 * i + c:2 * i + c + 1], None, ALU.mult))
            settle()
            done(v.tensor_scalar(vectors[:, :, GA3:GA3 + 2, :], vectors[:, :, GA3:GA3 + 2, :], 0.5, None, ALU.mult))
            dve.wait_ge(s_fold, 16 * N_FOLD)
            done(v.tensor_scalar(w_g2[:, :, :], w_g2[:, :, :], 0.5, None, ALU.mult))
            dve.wait_ge(s_drain, SETUP_FILLS)
            done(v.tensor_tensor(bias_rows[0:E, :], bias_rows[0:E, :], out_b3[:, :], ALU.add))
            dve.drain().then_inc(s_ready, 1)

            count = [0]

            def step(ins):
                ins.then_inc(R["dve_step"], 1)
                count[0] += 1
                return count[0]

            def after(n):
                dve.wait_ge(R["dve_step"], n)

            def take(use):
                b, n = use
                dve.wait_ge(filled[b], n + 1)
                return bank[b], drained[b]

            def layer_norm(x, xn, k, stats, mean_var, var_eps, rstd, eps, sems):
                ready, rstd_ready, xn_ready = (R[s] for s in sems)
                ns = [step(v.bn_stats(stats[:, b, :], x[:, b, :])) for b in range(G)]
                for b in range(G):
                    after(ns[b])
                    n = step(v.bn_aggr(mean_var[:, b, :], stats[:, b, :]))
                after(n)
                v.tensor_scalar(var_eps[:, :], mean_var[:, :, 1], eps, None, ALU.add).then_inc(ready, 1)
                dve.wait_ge(rstd_ready, k)
                for b in range(G):
                    last = v.tensor_scalar(xn[:, b, :], x[:, b, :], mean_var[:, b, 0:1], rstd[:, b:b + 1],
                                           ALU.subtract, ALU.mult)
                last.then_inc(xn_ready, 1)

            def maxima(k, half):
                if half == 0:
                    dve.wait_ge(R["scored"], k + 1)
                j = slice(4 * half, 4 * half + 4)
                after(step(v.tensor_reduce(rowmax[:, j], score[:, k % 2, j, :], AX.X, ALU.max)))
                v.tensor_scalar(neg_max[:, k % 2, j], rowmax[:, j], -float(D) ** -0.5, None, ALU.mult)\
                    .then_inc(R["maxed"], 1)

            def top(k, half):
                if half == 0:
                    dve.wait_ge(R["scored"], k + 1)
                heads = range(4 * half, 4 * half + 4)
                s = score[:, k % 2]
                n = {j: step(v.max(top1[:, j, :], s[:, j, :])) for j in heads}
                for j in heads:
                    after(n[j])
                    n[j] = step(v.match_replace(left[:, j, :], top1[:, j, :], s[:, j, :], GONE))
                after(n[heads[-1]])
                v.tensor_scalar(neg_max[:, k % 2, heads[0]:heads[0] + 4], top1[:, heads[0]:heads[0] + 4, 0],
                                -float(D) ** -0.5, None, ALU.mult).then_inc(R["maxed"], 1)
                for j in heads:
                    after(n[j])
                    n[j] = step(v.max(top2[:, j, :], left[:, j, :]))
                for j in heads:
                    after(n[j])
                    n[j] = step(v.match_replace(left[:, j, :], top2[:, j, :], left[:, j, :], GONE))
                return n[heads[-1]]

            def pick(k, n):
                dve.wait_ge(R["exped"], 2 * k + 2)
                after(n)
                v.scalar_tensor_tensor(prob[:, k % 2, :, :], left[:, :, :], GONE, prob[:, k % 2, :, :],
                                       ALU.is_equal, ALU.mult).then_inc(R["picked"], 1)

            def output(k):
                b = k % UNITS // 2
                dve.wait_ge(R["valued"], k + 1)
                o = bank[5][:, 0:H * (D + 1)].rearrange("p (h d) -> p h d", h=H)
                after(step(v.reciprocal(o_inv[:, :], o[:, :, D])))
                v.tensor_tensor(o_tok[:, b, :].rearrange("p (h d) -> p h d", h=H), o[:, :, 0:D],
                                o_inv[:, :].unsqueeze(2).to_broadcast([P, H, D]), ALU.mult)\
                    .then_inc(R["o_ready"], 1)

            def step_a(name, k):
                if name == "ln":
                    if k == 2:
                        b, n = A_USE["r1", 1]
                        dve.wait_ge(drained[b], n + 1)
                        b, n = A_USE["r1", 0]
                        dve.wait_ge(drained[b], n + 1)
                    layer_norm(x_in if k == 1 else x_mid, xn, k, stats, mean_var, var_eps, rstd, EPS0,
                               ("var_ready", "rstd_ready", "xn_ready"))
                elif name == "v":
                    for p in range(2):
                        ps, d = take(A_USE[f"v{k}", p])
                        for b in range(2):
                            last = v.tensor_copy(v1[:, 2 * p + b, :, 0:D],
                                                 ps[:, b * C:(b + 1) * C].rearrange("p (h d) -> p h d", h=H))
                        last.then_inc(d, 1)
                elif name in ("unit_a", "unit_b"):
                    half = int(name == "unit_b")
                    if k < UNITS:
                        maxima(k, half)
                    else:
                        n = top(k, half)
                        if half:
                            pick(k, n)
                    if half and k % 2 == 0 and k % UNITS:
                        output(k - 1)
                elif name == "last_b":
                    output(k)
                elif name == "residual":
                    for p in range(2):
                        ps, d = take(A_USE[f"r{k}", p])
                        source, dest = x_in if k == 1 else x1, x1
                        if k == 1 and p == 0 and with_b[0]:
                            b, n = B_USE["r3", 1]
                            dve.wait_ge(drained[b], n + 1)
                        v.tensor_tensor(dest[:, 2 * p:2 * p + 2, :].rearrange("p b c -> p (b c)"), ps[:, :],
                                        source[:, 2 * p:2 * p + 2, :].rearrange("p b c -> p (b c)"), ALU.add)\
                            .then_inc(d, 1)

            def silu_done(j):
                dve.wait_ge(R["th_ready"], j + 1)
                v.scalar_tensor_tensor(hidden[:, j, :], th[:, j % 2, :], 1.0, z[:, j % 2, :], ALU.add, ALU.mult)\
                    .then_inc(R["hidden_ready"], 1)

            def step_b(name, k):
                if name == "lnb":
                    if k == 4:
                        for p in range(2):
                            b, n = B_USE["r3", p]
                            dve.wait_ge(drained[b], n + 1)
                    layer_norm(x1 if k == 3 else x2, xnb, k - 2, stats_b, mean_var_b, var_eps_b, rstd_b,
                               EPS0 if k == 3 else EPS1, ("var_ready_b", "rstd_ready_b", "xn_ready_b"))
                elif name == "mlp_b":
                    b, n = B_USE["a", k]
                    dve.wait_ge(drained[b], n + 1)
                    n = step(v.scalar_tensor_tensor(z[:, k % 2, :], th[:, k % 2, :], 1.0, z[:, k % 2, :],
                                                    ALU.add, ALU.mult))
                    ps, d = take(B_USE["b", k])
                    after(n)
                    v.scalar_tensor_tensor(hidden[:, k, :], ps[:, :], b_m1[:, MC + k:MC + k + 1], z[:, k % 2, :],
                                           ALU.add, ALU.mult).then_inc(d, 1)
                elif name == "residual_b":
                    for p in range(2):
                        ps, d = take(B_USE["r3", p])
                        v.tensor_tensor(x2[:, 2 * p:2 * p + 2, :].rearrange("p b c -> p (b c)"), ps[:, :],
                                        x1[:, 2 * p:2 * p + 2, :].rearrange("p b c -> p (b c)"), ALU.add)\
                            .then_inc(d, 1)
                elif name == "match":
                    ps, d = take(B_USE["match", 0])
                    v.tensor_reduce(w_max[:, :], ps[:, :].rearrange("p (b n) -> p b n", b=G), AX.X, ALU.max,
                                    negate=True).then_inc(R["wmax_ready"], 1)
                elif name == "normalise":
                    b, n = B_USE["match", 0]
                    dve.wait_ge(drained[b], n + 1)
                    after(step(v.tensor_reduce(w_sum[:, :], wgt[:, :, :], AX.X, ALU.add)))
                    after(step(v.reciprocal(w_sum[:, :], w_sum[:, :])))
                    v.tensor_tensor(wgt[:, :, :], wgt[:, :, :], w_sum[:, :].unsqueeze(2).to_broadcast([P, G, P]),
                                    ALU.mult).then_inc(R["wgt_ready"], 1)
                elif name == "router_turn":
                    ps, d = take(B_USE["router", 1])
                    logits = ps[:, 0:G * E].rearrange("p (b e) -> p b e", b=G)
                    after(step(v.tensor_reduce(l_max[:, :], logits, AX.X, ALU.max)))
                    v.tensor_tensor(logit[:, :, :], logits, l_max[:, :].unsqueeze(2).to_broadcast([P, G, E]),
                                    ALU.subtract).then_inc(d, 1)
                elif name == "route":
                    dve.wait_ge(R["lexp_ready"], 1)
                    after(step(v.tensor_reduce(l_sum[:, :], l_exp[:, :, :], AX.X, ALU.add)))
                    after(step(v.reciprocal(l_sum[:, :], l_sum[:, :])))
                    route_step[0] = step(v.scalar_tensor_tensor(
                        route[:, :, :], l_exp[:, :, :], 0.5, l_sum[:, :].unsqueeze(2).to_broadcast([P, G, E]),
                        ALU.mult, ALU.mult))
                elif name == "expert_v":
                    ps, d = take(B_USE["expert", k])
                    if k == 0:
                        dve.wait_ge(R["vec_b_loaded"], 16)
                    if k >= 2:
                        dve.wait_ge(R["hidden_ready"], k - 1)
                    v.tensor_tensor(z[:, k % 2, :].rearrange("p (b n) -> p b n", b=G),
                                    ps[:, :].rearrange("p (b n) -> p b n", b=G),
                                    vec_b[:, EB + k, :].unsqueeze(2).to_broadcast([P, G, P]), ALU.add)\
                        .then_inc(d, 1)
                    if k:
                        silu_done(k - 1)
                elif name == "expert_end":
                    silu_done(EC + 1)
                elif name == "mix0":
                    ps, d = take(B_USE["mix", 2 * k])
                    after(route_step[0])
                    after(step(v.tensor_scalar(mix[:, k, :], ps[:, 0:C], route[:, k, 0:1], None, ALU.mult)))
                    v.scalar_tensor_tensor(mix[:, k, :], ps[:, C:2 * C], route[:, k, 1:2], mix[:, k, :],
                                           ALU.mult, ALU.add).then_inc(d, 1)
                elif name == "mix1":
                    ps, d = take(B_USE["mix", 2 * k + 1])
                    b, n = B_USE["mix", 2 * k]
                    dve.wait_ge(drained[b], n + 1)
                    dve.wait_ge(R["gate_ready"], k + 1)
                    n = step(v.scalar_tensor_tensor(mix[:, k, :], ps[:, 0:C], route[:, k, 2:3], mix[:, k, :],
                                                    ALU.mult, ALU.add))
                    after(n)
                    v.scalar_tensor_tensor(mix[:, k, :], gate_th[:, k % 2, :], 1.0, mix[:, k, :],
                                           ALU.add, ALU.mult).then_inc(d, 1)

            route_step = [0]
            with_b = [False]

            def round_(steps, n):
                count[0] = 0
                with_b[0] = steps is BOTH
                enter(dve, n)
                for stage, step_ in steps:
                    (step_a if stage == "A" else step_b)(*step_)
                leave(dve)

            round_(ONLY_A, 1)
            with dve.Fori(1, NG) as i:
                round_(BOTH, i + 1)
            round_(ONLY_B, NG + 1)


_INS = ["x", "cond_1024", "ctx_1024"] + [f"L0_xcond_{n}" for n in (
    "w_ada", "b_ada", "w_qkv", "b_qkv", "w_so", "b_so", "w_q", "b_q", "w_kv", "b_kv", "w_co", "b_co", "w_m1", "b_m1",
    "w_m2", "b_m2")] + [f"L1_xcond_{n}" for n in (
        "ln_gamma", "ln_beta", "Wq", "Wk", "Wv", "router_W", "router_b", "e_w1", "e_b1", "e_w2", "e_b2", "gate_w1",
        "gate_b1", "gate_w2", "gate_b2", "out_w", "out_b")]


def kernel(**inputs):
    import numpy as _np
    import concourse.bacc as _bacc
    from concourse import mybir as _mybir
    from concourse.bass_utils import run_bass_kernel_spmd as _run

    nc = _bacc.Bacc("TRN2", target_bir_lowering=False, num_devices=1)
    arrays, t = {}, {}
    for name in _INS:
        a = _np.ascontiguousarray(inputs[name])
        arrays[f"in_{name}"] = a
        t[name] = nc.dram_tensor(f"in_{name}", a.shape, _mybir.dt.from_np(a.dtype), kind="ExternalInput").ap()
    out = nc.dram_tensor("out", arrays["in_x"].shape, _mybir.dt.float32, kind="ExternalOutput").ap()
    program(nc, t, out)
    r = _run(nc, [arrays], core_ids=[0])
    return r.results[0]["out"]
```

```python
from contextlib import ExitStack

import concourse.bass as bass
from concourse import mybir
import numpy as np

F32 = mybir.dt.float32
BF16 = mybir.dt.bfloat16
ACT = mybir.ActivationFunctionType
ALU = mybir.AluOpType
AX = mybir.AxisListType

P = 128
C = 256
KC = C // P
G = 4
T = G * P
H = 16
D = C // H
HID = 1024
E = 3
RH = 2 * C
EC = E * RH // P
MC = HID // P
TOPK = 16
GONE = float(np.float32(-3.0e38))
EPS0, EPS1 = 1e-6, 1e-5

SH1, SC1, GA1, SH2, SC2, GA2, SH3, SC3, GA3 = range(0, 18, 2)
GB1, GB2, GB3 = 18, 20, 22
N_SMALL, N_FOLD, N_MAIN, SETUP_FILLS = 22, 11, 12, 36
EB = 24
GB = EB + EC
NV = GB + 2
N1 = SC1 + 2
NA = GB2 + 2

UNITS = 2 * G


def attention_steps(n):
    ks = range(n * UNITS, (n + 1) * UNITS)
    return [(s, k) for k in ks for s in ("unit_a", "unit_b", "unit_c")] + [("last_a", ks[-1]), ("last_b", ks[-1])]


def with_next_ln(steps, at):
    return steps[:at] + [("ln", 3)] + steps[at:]


FIRST_LN = [("ln", 1)]
STAGE_A = (
    [("turn_x", 1), ("turn_ctx", 1), ("q", 1), ("k", 1), ("first_scores", 0), ("v", 1)]
    + attention_steps(0)
    + [("k", 2), ("project", 1), ("v", 2), ("residual", 1), ("ln", 2), ("turn_x", 2), ("q", 2),
       ("first_scores", UNITS)]
    + with_next_ln(attention_steps(1), 12)
    + [("project", 2), ("residual", 2)]
)
STAGE_B = (
    [("lnb", 3), ("turn_b", 3)]
    + [(s, m) for m in range(MC) for s in ("mlp_a", "mlp_b")]
    + [("mlp_down", i) for i in range(MC)]
    + [("residual_b", 0), ("lnb", 4), ("turn_b", 4), ("query", 0), ("query", 1), ("match", 0), ("normalise", 0)]
    + [("weights", 0), ("evidence", 0), ("evidence", 1), ("router", 0), ("router_turn", 0), ("route", 0)]
    + [(s, j) for j in range(EC + 2) for s in ("expert_x", "expert_v")] + [("expert_end", 0)]
    + [(s, b) for b in range(G) for s in ("mix0", "mix1", "add")]
)


ROOM = {"turn_x": 3.9, "q": 2, "k": 1, "v": 0.85, "turn_ctx": 1, "first_scores": 2, "ln": 6, "project": 2,
        "residual": 6, "self_a": 3.4, "self_b": 1.7, "self_c": 1.7, "cross_a": 5, "cross_b": 2.5, "cross_c": 2.5,
        "last_a": 3, "last_b": 2.55}
TAKES = {"lnb": 6, "turn_b": 3, "mlp_a": 3.4, "mlp_b": 1.7, "mlp_down": 1.7, "residual_b": 3, "query": 2,
         "match": 3, "normalise": 2, "weights": 2.3, "evidence": 1, "router": 4, "router_turn": 2, "route": 2,
         "expert_x": 1.7, "expert_v": 1.7, "expert_end": 3, "mix0": 4, "mix1": 4.02, "add": 0}
END = 8.97


def room(step):
    name, k = step
    return ROOM[name.replace("unit", "self" if k < UNITS else "cross")]


def merged():
    out, b, placed, seen = [], 0, 0.0, 0.0
    scale = (sum(TAKES[n] for n, _ in STAGE_B) + END) / sum(room(s) for s in STAGE_A)
    for s in STAGE_A:
        out.append(("A", s))
        seen += room(s) * scale
        while b < len(STAGE_B) and placed + TAKES[STAGE_B[b][0]] / 2 < seen:
            out.append(("B", STAGE_B[b]))
            placed += TAKES[STAGE_B[b][0]]
            b += 1
    return out + [("B", s) for s in STAGE_B[b:]]


ONLY_A = [("A", s) for s in FIRST_LN + list(STAGE_A)]
ONLY_B = [("B", s) for s in STAGE_B]
BOTH = merged()


def uses(names, banks):
    count, out = {b: 0 for b in banks}, {}
    for i, name in enumerate(names):
        b = banks[i % len(banks)]
        out[name] = (b, count[b])
        count[b] += 1
    return out


def two(*names):
    return [(n, i) for n in names for i in range(2)]


A_BEFORE = two("x1", "ctx", "q1", "k1", "v1")
A_BETWEEN = two("k2", "y1", "v2", "r1", "x2", "q2")
A_AFTER = two("y2", "r2")
A_USE = uses(A_BEFORE + A_BETWEEN + A_AFTER, (4, 5))
B_USE = uses(
    two("x3")
    + [(n, m) for m in range(MC) for n in ("a", "b")]
    + two("down", "r3", "x4", "query") + [("match", 0), ("weights", 0)] + two("evidence")
    + [("router", 0), ("router", 1)] + [("expert", j) for j in range(EC + 2)]
    + [("mix", 2 * b + i) for b in range(G) for i in range(2)],
    (6, 7),
)


def slot_of(h):
    c, g, e = h // 8, h % 8 // 2, h % 2
    return 4 * g + 2 * c + e


HEAD_AT = sorted(range(H), key=slot_of)


def program(nc, t, out):
    B = t["x"].shape[0]
    NG = B // G
    ctx = ExitStack()
    with ctx:
        def sb(name, shape, kind=F32):
            return ctx.enter_context(nc.sbuf_tensor(name, shape, kind))

        ident = sb("ident", [P, P])
        w_qkv = sb("w_qkv", [P, KC, 3 * C])
        w_so = sb("w_so", [P, KC, C])
        w_q = sb("w_q", [P, KC, C])
        w_kv = sb("w_kv", [P, KC, 2 * C])
        w_co = sb("w_co", [P, KC, C])
        w_m1 = sb("w_m1", [P, KC, 2 * HID])
        w_m2 = sb("w_m2", [P, MC, C])
        w_query = sb("w_query", [P, KC, C])
        w_r = sb("w_r", [P, 2 * KC, E])
        w_e1 = sb("w_e1", [P, 2 * KC, E * RH])
        w_g1 = sb("w_g1", [P, 2 * KC, C])
        w_g2 = sb("w_g2", [P, KC, C])
        w_e2 = sb("w_e2", [P, EC, C])
        bias_parts = sb("bias_parts", [3 * 32, C], BF16)
        row_of = sb("row_of", [3 * 32, E + 1, P], BF16)
        router_b = sb("router_b", [E, NG, G])
        vec_a = sb("vec_a", [P, NA, G])
        vec_1 = sb("vec_1", [P, N1, G])
        vec_b = sb("vec_b", [P, NV, G])
        rb_b = sb("rb_b", [E, G])
        minus_half = sb("minus_half", [P, G])
        b_qkv = sb("b_qkv", [P, 6])
        b_q = sb("b_q", [P, 2])
        b_kv = sb("b_kv", [P, 4])
        b_out = sb("b_out", [P, 6])
        b_m1 = sb("b_m1", [P, 2 * MC])
        b_m1h = sb("b_m1h", [P, 2 * MC])
        gamma = sb("gamma", [P, KC])
        beta = sb("beta", [P, KC])
        head_mask = sb("head_mask", [P, 2])
        b_v = sb("b_v", [P, 2, C])
        b_k = sb("b_k", [P, 2, 2, KC])

        with ExitStack() as early:
            def st(name, shape, kind=F32):
                return early.enter_context(nc.sbuf_tensor(name, shape, kind))

            w_ada = st("w_ada", [P, KC, 9 * C])
            e1_anchor = st("e1_anchor", [P, KC, E * RH])
            e1_ev = st("e1_ev", [P, KC, E * RH])
            g1_raw = st("g1_raw", [P, 2 * KC, C])
            r_raw = st("r_raw", [P, 2 * KC, E])
            Wq = st("Wq", [P, KC, C])
            Wk = st("Wk", [P, KC, C])
            Wv = st("Wv", [P, KC, C])
            out_w = st("out_w", [P, KC, C])
            WqT = st("WqT", [P, KC, C])
            WkT = st("WkT", [P, KC, C])
            WvT = st("WvT", [P, KC, C])
            e2 = st("e2", [P, EC, C])
            e2T = st("e2T", [P, KC, EC * P])
            eb2T = st("eb2T", [P, KC, E])
            out_b3 = st("out_b3", [3 * 32, C])
            bias_rows = st("bias_rows", [3 * 32, C])
            bias_rest = st("bias_rest", [3 * 32, C])
            part_of = [st(f"part{i}", [3 * 32, C], BF16) for i in range(3)]
            row_of32 = st("row_of32", [3 * 32, E + 1, P])
            vectors = st("vectors", [P, NG, NV, G])
            cond = st("cond", [B, C])
            cond_silu = st("cond_silu", [B, C])
            cond_th = st("cond_th", [B, C])
            condT = st("condT", [P, KC, B])
            siluT = st("siluT", [P, KC, B])
            b_ada = st("b_ada", [P, 18])
            b_e1 = st("b_e1", [P, EC + 2])
            b_r = st("b_r", [E, 1])

        x_in = sb("x_in", [P, G, C])
        ctx_a = sb("ctx_a", [P, G, C])
        ctxT_a = sb("ctxT_a", [P, KC, T])
        xn = sb("xn", [P, G, C])
        hT = sb("hT", [P, KC, T])
        yT = hT
        qT = sb("qT", [P, KC, T])
        oT = qT
        kM = sb("kM", [P, KC, G, 2, P])
        vM = sb("vM", [P, G, H // 2, 3, D])
        mean_var = sb("mean_var", [P, G, 2])
        var_eps = sb("var_eps", [P, G])
        rstd = sb("rstd", [P, G])
        top1 = sb("top1", [P, 4, 8])
        stats = top1[:, :, 0:6]
        top2 = sb("top2", [P, 4, 8])
        rowmax = sb("rowmax", [P, 8])
        neg_max = sb("neg_max", [P, 2, 8])
        left = sb("left", [P, 4, P])
        prob = sb("prob", [P, 2, 8, P])
        probT = sb("probT", [P, 2, 8, P])
        p_sum = sb("p_sum", [P, 2, H])
        p_inv = sb("p_inv", [P, 2, H])
        p_inv_wide = sb("p_inv_wide", [P, H, D])
        x1 = sb("x1", [P, G, C])
        x_mid = x1
        ctx_b = sb("ctx_b", [P, G, C])
        ctxT_b = sb("ctxT_b", [P, KC, T])
        xnb = sb("xnb", [P, G, C])
        qs = xnb[:, :, :].rearrange("p (k g) c -> p k (g c)", k=KC)
        evT = qs
        mix = xnb
        hB = sb("hB", [P, KC, T])
        z = sb("z", [P, 2, T])
        th = sb("th", [P, 2, T])
        hidden = sb("hidden", [P, EC + 2, T])
        x2 = sb("x2", [P, G, C])
        stats_b = top2[:, :, 0:6]
        mean_var_b = sb("mean_var_b", [P, G, 2])
        var_eps_b = sb("var_eps_b", [P, G])
        rstd_b = sb("rstd_b", [P, G])
        wgt = z[:, 0, :].rearrange("p (b n) -> p b n", b=G)
        wgtT = z[:, 1, :]
        w_max = sb("w_max", [P, G])
        w_sum = sb("w_sum", [P, G])
        logitT = th[0:E, 0, :]
        logit = sb("logit", [P, G, E])
        l_max = w_max
        l_exp = logit
        l_sum = w_sum
        route = sb("route", [P, G, E])
        gate_th = z[:, 0, :].rearrange("p (i c) -> p i c", i=2)

        bank = [ctx.enter_context(nc.psum_tensor(f"bank{i}", [P, T], F32)) for i in range(4, 8)]
        bank = {i + 4: b for i, b in enumerate(bank)}
        score = ctx.enter_context(nc.psum_tensor("score", [P, 2, 8, P], F32))

        def sem(name):
            return ctx.enter_context(nc.semaphore(name))

        go, seen = sem("go"), sem("seen")
        s_small, s_ada, s_fold, s_main, s_group, s_vectors = (
            sem(n) for n in ("s_small", "s_ada", "s_fold", "s_main", "s_group", "s_vectors"))
        s_fill, s_drain = sem("s_fill"), sem("s_drain")
        s_const, s_dve, s_act, s_ready = sem("s_const"), sem("s_dve"), sem("s_act"), sem("s_ready")
        names = ("arrived filled4 filled5 filled6 filled7 drained4 drained5 drained6 drained7 "
                 "vec_1_loaded vec_a_loaded vec_b_loaded rb_ready var_ready rstd_ready xn_ready var_ready_b rstd_ready_b xn_ready_b "
                 "scored maxed exped picked turned copied inverted widened valued inv_copied o_ready dve_step act_step "
                 "th_ready hidden_ready wmax_ready wgt_ready lexp_ready "
                 "gate_ready summed x_loaded loaded moved stored").split()
        R = {n: sem(n) for n in names}
        nums = [R[n].num for n in names]
        round_sems = range(min(nums), max(nums) + 1)
        assert len(round_sems) == len(names)
        filled = {i: R[f"filled{i}"] for i in (4, 5, 6, 7)}
        drained = {i: R[f"drained{i}"] for i in (4, 5, 6, 7)}

        def all_o_before(name):
            return {True: 0}.get(name in A_BEFORE, G if name in A_BETWEEN else 2 * G)

        vectors_d = nc.dram_tensor("vectors_d", [NG, P, NV * G], F32, kind="Internal").ap()
        x_d = t["x"].rearrange("(n g) l c -> n l g c", g=G)
        ctx_d = t["ctx_1024"].rearrange("(n g) l c -> n l g c", g=G)
        out_d = out.rearrange("(n g) l c -> n g l c", g=G)

        def rows(a):
            return a.rearrange("(k p) n -> p k n", p=P)

        def cols(a):
            return a.rearrange("(m p) -> p m", p=P)

        e_w1 = t["L1_xcond_e_w1"]
        g_w1 = rows(t["L1_xcond_gate_w1"])
        r_w = rows(t["L1_xcond_router_W"])

        def e1_part(part):
            return [rows(e_w1[e])[:, KC * part:KC * part + KC, :] for e in range(E)]

        block = ctx.enter_context(nc.Block())

        @block.sync
        def _(sp):
            n_small = 0
            for dst, src in [
                (cond[:, :], t["cond_1024"]), (b_ada[:, :], cols(t["L0_xcond_b_ada"])),
                (b_e1[:, 0:EC], t["L1_xcond_e_b1"].rearrange("e (m p) -> p (e m)", p=P)),
                (b_e1[:, EC:EC + 2], cols(t["L1_xcond_gate_b1"])),
                (b_r[:, :], t["L1_xcond_router_b"].rearrange("(e a) -> e a", a=1)),
                (b_qkv[:, :], cols(t["L0_xcond_b_qkv"])), (b_q[:, :], cols(t["L0_xcond_b_q"])),
                (b_kv[:, :], cols(t["L0_xcond_b_kv"])), (b_out[:, 0:2], cols(t["L0_xcond_b_so"])),
                (b_out[:, 2:4], cols(t["L0_xcond_b_co"])), (b_out[:, 4:6], cols(t["L0_xcond_b_m2"])),
                (b_m1[:, :], cols(t["L0_xcond_b_m1"])),
                (gamma[:, :], cols(t["L1_xcond_ln_gamma"])), (beta[:, :], cols(t["L1_xcond_ln_beta"])),
                (eb2T[:, 0, :], t["L1_xcond_e_b2"].rearrange("e (k p) -> p k e", p=P)[:, 0, :]),
                (eb2T[:, 1, :], t["L1_xcond_e_b2"].rearrange("e (k p) -> p k e", p=P)[:, 1, :]),
                (out_b3[:, :], t["L1_xcond_out_b"].rearrange("(a n) -> a n", a=1).to_broadcast([3 * 32, C])),
                (b_v[:, 0, :], t["L0_xcond_b_qkv"][2 * C:3 * C].rearrange("(a n) -> a n", a=1).to_broadcast([P, C])),
                (b_v[:, 1, :], t["L0_xcond_b_kv"][C:2 * C].rearrange("(a n) -> a n", a=1).to_broadcast([P, C])),
                *((bias_rows[32 * i + E:32 * i + E + 1, :], t["L1_xcond_gate_b2"].rearrange("(a n) -> a n", a=1))
                  for i in range(3)),
            ]:
                if n_small == N_SMALL - 3:
                    sp.wait_ge(s_const, 4)
                sp.dma_start(dst, src, allow_slow_non_contiguous=True).then_inc(s_small, 16)
                n_small += 1
            assert n_small == N_SMALL
            sp.dma_start(w_ada[:, :, :], rows(t["L0_xcond_w_ada"])).then_inc(s_ada, 16)
            for e, src in enumerate(e1_part(2)):
                sp.dma_start(e1_anchor[:, :, e * RH:(e + 1) * RH], src).then_inc(s_ada, 16)
            sp.dma_start(g1_raw[:, :, :], g_w1[:, KC:, :]).then_inc(s_ada, 16)
            sp.dma_start(r_raw[:, :, :], r_w[:, KC:, :]).then_inc(s_ada, 16)
            for dst, name in ((Wq, "Wq"), (Wk, "Wk"), (Wv, "Wv"), (out_w, "out_w"), (w_g2, "gate_w2")):
                sp.dma_start(dst[:, :, :], rows(t[f"L1_xcond_{name}"])).then_inc(s_fold, 16)
            for e, src in enumerate(e1_part(1)):
                sp.dma_start(e1_ev[:, :, e * RH:(e + 1) * RH], src).then_inc(s_fold, 16)
            for e in range(E):
                sp.dma_start(e2[:, 4 * e:4 * e + 4, :], rows(t["L1_xcond_e_w2"][e])).then_inc(s_fold, 16)
            for dst, name in ((w_qkv, "w_qkv"), (w_so, "w_so"), (w_q, "w_q"), (w_kv, "w_kv"), (w_co, "w_co"),
                              (w_m1, "w_m1"), (w_m2, "w_m2")):
                sp.dma_start(dst[:, :, :], rows(t[f"L0_xcond_{name}"])).then_inc(s_main, 16)
            for e, src in enumerate(e1_part(0)):
                sp.dma_start(w_e1[:, 0:KC, e * RH:(e + 1) * RH], src).then_inc(s_main, 16)
            sp.dma_start(w_g1[:, 0:KC, :], g_w1[:, 0:KC, :]).then_inc(s_main, 16)
            sp.dma_start(w_r[:, 0:KC, :], r_w[:, 0:KC, :]).then_inc(s_main, 16)
            sp.wait_ge(s_ready, 4)
            sp.dma_start(vectors_d.rearrange("n p v -> p n v"), vectors[:, :, :, :].rearrange("p n v g -> p n (v g)"))\
                .then_inc(s_vectors, 16)
            sp.wait_ge(s_vectors, 16)
            sp.dma_start(x_in[:, :, :], x_d[0]).then_inc(s_group, 16)
            sp.dma_start(ctx_a[:, :, :], ctx_d[0]).then_inc(s_group, 16)
            sp.dma_start(vec_1[:, :, :].rearrange("p v g -> p (v g)"), vectors_d[0][:, 0:N1 * G]).then_inc(s_group, 16)
            sp.wait_ge(s_group, 48)
            sp.wait_ge(s_main, 16 * N_MAIN)
            sp.sem_inc(go)

            def after(use):
                b, n = use
                sp.wait_ge(drained[b], n + 1)

            def round_(with_a, with_b, next_a, group_b):
                if with_a:
                    sp.dma_start(vec_a[:, :, :].rearrange("p v g -> p (v g)"), vectors_d[group_b + 1][:, 0:NA * G])\
                        .then_inc(R["vec_a_loaded"], 16)
                if with_b:
                    sp.dma_start(vec_b[:, :, :].rearrange("p v g -> p (v g)"), vectors_d[group_b])\
                        .then_inc(R["vec_b_loaded"], 16)
                if with_a:
                    after(A_USE["x1", 0])
                    after(A_USE["x1", 1])
                    sp.dma_start(vec_1[:, :, :].rearrange("p v g -> p (v g)"), vectors_d[next_a][:, 0:N1 * G])\
                        .then_inc(R["vec_1_loaded"], 16)
                    after(A_USE["r1", 1])
                    sp.dma_start(x_in[:, :, :], x_d[next_a]).then_inc(R["x_loaded"], 16)
                    after(A_USE["v2", 1])
                    sp.wait_ge(filled[A_USE["k2", 1][0]], A_USE["k2", 1][1] + 1)
                    if with_b:
                        after(B_USE["evidence", 1])
                    sp.dma_start(ctx_b[:, :, :], ctx_a[:, :, :]).then_inc(R["moved"], 16)
                    sp.dma_start(ctxT_b[:, :, :], ctxT_a[:, :, :]).then_inc(R["moved"], 16)
                    sp.wait_ge(R["moved"], 32)
                    sp.dma_start(ctx_a[:, :, :], ctx_d[next_a]).then_inc(R["loaded"], 16)
                if with_b:
                    for b in range(G):
                        sp.wait_ge(R["summed"], b + 1)
                        sp.dma_start(out_d[group_b, b], mix[:, b, :]).then_inc(R["stored"], 16)
                    sp.wait_ge(R["stored"], 16 * G)
                if with_a:
                    sp.wait_ge(R["vec_1_loaded"], 16)
                    sp.wait_ge(R["x_loaded"], 16)
                    sp.wait_ge(R["loaded"], 16)
                sp.wait_ge(R["arrived"], 4)
                sp.sem_clear(round_sems)
                sp.sem_inc(go)

            round_(True, False, 1 % NG, -1)
            with sp.Fori(1, NG) as i:
                round_(True, True, (i + 1) % NG, i - 1)
            round_(False, True, None, NG - 1)

        def enter(eng, n):
            eng.wait_ge(go, n)
            eng.sem_inc(seen)

        def leave(eng):
            eng.drain().then_inc(R["arrived"], 1)

        @block.gpsimd
        def _(pool):
            pool.memset(minus_half[:, :], -0.5).then_inc(s_const, 1)
            pool.memset(ident[:, :], 0.0).then_inc(s_const, 1)
            pool.memset(row_of32[:, :, :], 0.0).then_inc(s_const, 1)
            pool.memset(bias_rows[:, :], 0.0).then_inc(s_const, 1)
            pool.wait_ge(s_const, 4)
            pool.affine_select(out=ident[:, :], in_=ident[:, :], compare_op=ALU.not_equal, fill=1.0, base=0,
                               pattern=[[-1, P]], channel_multiplier=1).then_inc(s_const, 1)
            for i in range(3):
                pool.affine_select(out=row_of32[:, :, :], in_=row_of32[:, :, :], compare_op=ALU.not_equal, fill=1.0,
                                   base=-32 * i, pattern=[[-1, E + 1], [0, P]], channel_multiplier=1)\
                    .then_inc(s_const, 1)
                pool.wait_ge(s_const, 6 + i)
            pool.tensor_copy(row_of[:, :, :], row_of32[:, :, :]).then_inc(s_const, 1)
            pool.drain().then_inc(s_ready, 1)

            def round_(steps, n, group_b):
                enter(pool, n)
                if group_b is None:
                    pool.memset(vM[:, :, :, :], 0.0).then_inc(s_const, 1)
                else:
                    pool.tensor_copy(rb_b[:, :], router_b[:, group_b, :]).then_inc(R["rb_ready"], 1)
                for stage, (name, k) in steps:
                    if name == "ln":
                        pool.wait_ge(R["var_ready"], k if steps is ONLY_A else k - 1)
                        pool.tensor_tensor(rstd[:, :], var_eps[:, :], minus_half[:, :], ALU.pow)\
                            .then_inc(R["rstd_ready"], 1)
                    elif (name == "unit_a" and k % 2 == 0 and k % UNITS) or name == "last_a":
                        m = (k - 1) // 2 if name == "unit_a" else k // 2
                        pool.wait_ge(R["inverted"], m + 1)
                        if m:
                            pool.wait_ge(R["valued"], m)
                        pool.tensor_copy(p_inv_wide[:, :, :], p_inv[:, m % 2, :].unsqueeze(2).to_broadcast([P, H, D]))\
                            .then_inc(R["widened"], 1)
                    elif name == "lnb":
                        pool.wait_ge(R["var_ready_b"], k - 2)
                        pool.tensor_tensor(rstd_b[:, :], var_eps_b[:, :], minus_half[:, :], ALU.pow)\
                            .then_inc(R["rstd_ready_b"], 1)
                    elif name == "add":
                        b, n_ = B_USE["mix", 2 * k + 1]
                        pool.wait_ge(drained[b], n_ + 1)
                        pool.tensor_tensor(mix[:, k, :], mix[:, k, :], x2[:, k, :], ALU.add)\
                            .then_inc(R["summed"], 1)
                leave(pool)

            round_(ONLY_A, 1, None)
            with pool.Fori(1, NG) as i:
                round_(BOTH, i + 1, i - 1)
            round_(ONLY_B, NG + 1, NG - 1)

        @block.tensor
        def _(pe):
            mm = nc.tensor.matmul

            fills = [0]

            def begin():
                if fills[0] >= 4:
                    pe.wait_ge(s_drain, fills[0] - 3)
                return bank[4 + fills[0] % 4]

            def end(ins):
                ins.then_inc(s_fill, 1)
                fills[0] += 1

            pe.wait_ge(s_const, 5)
            pe.wait_ge(s_dve, 1)
            ps = begin()
            for i, a in enumerate((cond, cond_silu)):
                for c in range(KC):
                    last = nc.tensor.transpose(ps[:, (2 * i + c) * B:(2 * i + c + 1) * B], a[:, c * P:(c + 1) * P],
                                               ident[0:B, 0:B])
            end(last)
            pe.wait_ge(s_ada, 16 * 6)
            pe.wait_ge(s_drain, 1)
            for m in range(18):
                if m % 4 == 0:
                    ps = begin()
                for kk in range(KC):
                    last = mm(ps[:, m % 4 * B:(m % 4 + 1) * B], w_ada[:, kk, m * P:(m + 1) * P], siluT[:, kk, :],
                              start=kk == 0, stop=kk == KC - 1)
                if m % 4 == 3 or m == 17:
                    end(last)
            for j in range(EC + 2):
                if j % 4 == 0:
                    ps = begin()
                for kk in range(KC):
                    w = e1_anchor[:, kk, j * P:(j + 1) * P] if j < EC else \
                        g1_raw[:, KC + kk, (j - EC) * P:(j - EC + 1) * P]
                    last = mm(ps[:, j % 4 * B:(j % 4 + 1) * B], w, condT[:, kk, :], start=kk == 0, stop=kk == KC - 1)
                if j % 4 == 3 or j == EC + 1:
                    end(last)
            ps = begin()
            for kk in range(KC):
                last = mm(ps[0:E, 0:B], r_raw[:, KC + kk, :], condT[:, kk, :], start=kk == 0, stop=kk == KC - 1)
            end(last)
            pe.wait_ge(s_fold, 16 * N_FOLD)
            for a in (Wq, Wk, Wv):
                ps = begin()
                for jj in range(KC):
                    for kk in range(KC):
                        last = nc.tensor.transpose(ps[:, (jj * KC + kk) * P:(jj * KC + kk + 1) * P],
                                                   a[:, kk, jj * P:(jj + 1) * P], ident[:, :])
                end(last)
            for i in range(EC // 2):
                ps = begin()
                for c in range(KC):
                    for r in range(2):
                        last = nc.tensor.transpose(ps[:, (c * 2 + r) * P:(c * 2 + r + 1) * P],
                                                   e2[:, 2 * i + r, c * P:(c + 1) * P], ident[:, :])
                end(last)
            pe.wait_ge(s_drain, fills[0])
            ps = begin()
            for kk in range(KC):
                for jj in range(KC):
                    last = mm(ps[:, kk * C:(kk + 1) * C], WqT[:, jj, kk * P:(kk + 1) * P], WkT[:, jj, :],
                              start=jj == 0, stop=jj == KC - 1)
            end(last)
            for kk in range(KC):
                for e in range(E):
                    ps = begin()
                    for jj in range(KC):
                        last = mm(ps[:, :], WvT[:, jj, kk * P:(kk + 1) * P], e1_ev[:, jj, e * RH:(e + 1) * RH],
                                  start=jj == 0, stop=jj == KC - 1)
                    end(last)
            ps = begin()
            for kk in range(KC):
                for jj in range(KC):
                    last = mm(ps[:, kk * C:(kk + 1) * C], WvT[:, jj, kk * P:(kk + 1) * P], g1_raw[:, jj, :],
                              start=jj == 0, stop=jj == KC - 1)
            end(last)
            ps = begin()
            for kk in range(KC):
                for jj in range(KC):
                    last = mm(ps[:, kk * E:(kk + 1) * E], WvT[:, jj, kk * P:(kk + 1) * P], r_raw[:, jj, :],
                              start=jj == 0, stop=jj == KC - 1)
            end(last)
            for i in range(EC // 2):
                ps = begin()
                for r in range(2):
                    for c in range(KC):
                        last = mm(ps[:, r * C:(r + 1) * C], e2T[:, c, (2 * i + r) * P:(2 * i + r + 1) * P],
                                  out_w[:, c, :], start=c == 0, stop=c == KC - 1)
                end(last)
            ps = begin()
            for c in range(KC):
                for i in range(3):
                    last = mm(ps[32 * i:32 * i + E, 0:C], eb2T[:, c, :], out_w[:, c, :], start=c == 0,
                              stop=c == KC - 1)
            end(last)
            assert fills[0] == SETUP_FILLS
            pe.drain().then_inc(s_ready, 1)

            def fill_a(name):
                b, n = A_USE[name]
                if n:
                    pe.wait_ge(drained[b], n)
                if b == 5 and all_o_before(name):
                    pe.wait_ge(R["o_ready"], all_o_before(name))
                return bank[b], filled[b]

            def fill_b(name):
                b, n = B_USE[name]
                if n:
                    pe.wait_ge(drained[b], n)
                return bank[b], filled[b]

            def has(use):
                pe.wait_ge(drained[use[0]], use[1] + 1)

            def scores(k):
                b, half = k % UNITS // 2, k % 2
                if k >= 2:
                    pe.wait_ge(R["copied"], k - 1)
                for c in range(KC):
                    for g in range(2):
                        r = slice(32 * (2 * half + g), 32 * (2 * half + g) + 32)
                        last = mm(score[:, k % 2, 4 * g + 2 * c:4 * g + 2 * c + 2, :].rearrange("p e n -> p (e n)"),
                                  qT[r, c, b * P:(b + 1) * P],
                                  kM[r, c, b, :, :].rearrange("p e n -> p (e n)"), start=True, stop=True)
                last.then_inc(R["scored"], 1)

            def turn_probs(k):
                if k < UNITS:
                    pe.wait_ge(R["exped"], 2 * k + 2)
                else:
                    pe.wait_ge(R["picked"], 2 * (k - UNITS) + 2)
                for j in range(8):
                    last = nc.tensor.transpose(score[:, k % 2, j, :], prob[:, k % 2, j, :], ident[:, :])
                last.then_inc(R["turned"], 1)

            def values(n):
                b = n % G
                pe.wait_ge(R["copied"], 2 * n + 2)
                if n:
                    pe.wait_ge(R["o_ready"], n)
                if b == 0:
                    u = A_USE[[a for a in (A_BETWEEN if n else A_BEFORE) if A_USE[a][0] == 5][-1]]
                    has(u)
                    for p in range(2):
                        has(A_USE[f"v{n // G + 1}", p])
                for c in range(KC):
                    for e in range(2):
                        for g in range(4):
                            j = slot_of(8 * c + 2 * g + e)
                            mm(bank[5][32 * g:32 * g + 32, c * P:(c + 1) * P],
                               vM[:, b, 4 * c + g, e:e + 2, :].rearrange("p i d -> p (i d)"), probT[:, j // 8, j % 8, :],
                               start=e == 0, stop=e == 1)
                pe.wait_ge(R["widened"], n + 1)
                for c in range(KC):
                    last = nc.tensor.transpose(
                        bank[5][:, (KC + c) * P:(KC + c + 1) * P],
                        p_inv_wide[:, 8 * c:8 * c + 8, :].rearrange("p h d -> p (h d)"), ident[:, :])
                last.then_inc(R["valued"], 1)

            def project(names, weight, c0, source):
                for m in range(KC):
                    ps, f = fill_a((names, m))
                    for kk in range(KC):
                        last = mm(ps[:, :], weight[:, kk, c0 + m * P:c0 + (m + 1) * P], source[:, kk, :],
                                  start=kk == 0, stop=kk == KC - 1)
                    last.then_inc(f, 1)

            def turn(names, source, fill):
                for c in range(KC):
                    ps, f = fill((names, c))
                    for b in range(G):
                        last = nc.tensor.transpose(ps[:, b * P:(b + 1) * P], source[:, b, c * P:(c + 1) * P],
                                                   ident[:, :])
                    last.then_inc(f, 1)

            def lns(k):
                return k if first_round[0] else k - 1

            first_round = [True]

            def turn_back(names, source, fill):
                for p in range(2):
                    ps, f = fill((names, p))
                    for b in range(2):
                        for c in range(KC):
                            last = nc.tensor.transpose(ps[:, b * C + c * P:b * C + (c + 1) * P],
                                                       source[:, c, (2 * p + b) * P:(2 * p + b + 1) * P], ident[:, :])
                    last.then_inc(f, 1)

            def step_a(name, k):
                if name == "turn_ctx":
                    turn("ctx", ctx_a, fill_a)
                elif name == "turn_x":
                    if lns(k):
                        pe.wait_ge(R["xn_ready"], lns(k))
                    turn(f"x{k}", xn, fill_a)
                elif name == "q":
                    has(A_USE[f"x{k}", 1])
                    has(A_USE[f"x{k}", 0])
                    project(f"q{k}", *((w_qkv, 0) if k == 1 else (w_q, 0)), hT)
                elif name == "k":
                    project(f"k{k}", *((w_qkv, C) if k == 1 else (w_kv, 0)), hT if k == 1 else ctxT_a)
                elif name == "v":
                    source, w, c0 = (hT, w_qkv, 2 * C) if k == 1 else (ctxT_a, w_kv, C)
                    for p in range(2):
                        ps, f = fill_a((f"v{k}", p))
                        for b in range(2):
                            for kk in range(KC):
                                last = mm(ps[:, b * C:(b + 1) * C],
                                          source[:, kk, (2 * p + b) * P:(2 * p + b + 1) * P],
                                          w[:, kk, c0:c0 + C], start=kk == 0, stop=kk == KC - 1)
                        last.then_inc(f, 1)
                elif name == "first_scores":
                    n = 1 if k == 0 else 2
                    for u in (f"q{n}", f"k{n}"):
                        has(A_USE[u, 0])
                        has(A_USE[u, 1])
                    scores(k)
                elif name == "unit_b":
                    if k % UNITS:
                        turn_probs(k - 1)
                elif name == "unit_c":
                    if (k + 1) % UNITS:
                        scores(k + 1)
                    if k % UNITS and k % 2 == 0:
                        values(k // 2 - 1)
                elif name == "last_a":
                    turn_probs(k)
                elif name == "last_b":
                    values(k // 2)
                elif name == "project":
                    pe.wait_ge(R["o_ready"], k * G)
                    project(f"y{k}", w_so if k == 1 else w_co, 0, oT)
                elif name == "residual":
                    has(A_USE[f"y{k}", 0])
                    has(A_USE[f"y{k}", 1])
                    turn_back(f"r{k}", yT, fill_a)

            def step_b(name, k):
                if name == "turn_b":
                    pe.wait_ge(R["xn_ready_b"], k - 2)
                    turn(f"x{k}", xnb, fill_b)
                elif name in ("mlp_a", "mlp_b"):
                    ps, f = fill_b((name[-1], k))
                    if (name, k) == ("mlp_a", 0):
                        has(B_USE["x3", 0])
                        has(B_USE["x3", 1])
                    c0 = (HID if name == "mlp_b" else 0) + k * P
                    for kk in range(KC):
                        last = mm(ps[:, :], w_m1[:, kk, c0:c0 + P], hB[:, kk, :], start=kk == 0, stop=kk == KC - 1)
                    last.then_inc(f, 1)
                elif name == "mlp_down":
                    m, quarter = k // 4, k % 4
                    if quarter == 0:
                        fill_b(("down", m))
                        has(B_USE["b", MC - 1])
                    b = B_USE["down", m][0]
                    for kk in (2 * quarter, 2 * quarter + 1):
                        last = mm(bank[b][:, :], w_m2[:, kk, m * P:(m + 1) * P], hidden[:, kk, :],
                                  start=kk == 0, stop=kk == MC - 1)
                    if quarter == 3:
                        last.then_inc(filled[b], 1)
                elif name == "residual_b":
                    has(B_USE["down", 0])
                    has(B_USE["down", 1])
                    turn_back("r3", hB, fill_b)
                elif name == "query":
                    ps, f = fill_b(("query", k))
                    if k == 0:
                        has(B_USE["x4", 0])
                        has(B_USE["x4", 1])
                    for kk in range(KC):
                        last = mm(ps[:, :], w_query[:, kk, k * P:(k + 1) * P], hB[:, kk, :],
                                  start=kk == 0, stop=kk == KC - 1)
                    last.then_inc(f, 1)
                elif name == "match":
                    ps, f = fill_b(("match", 0))
                    has(B_USE["query", 0])
                    has(B_USE["query", 1])
                    for b in range(G):
                        for kk in range(KC):
                            last = mm(ps[:, b * P:(b + 1) * P], qs[:, kk, b * P:(b + 1) * P],
                                      ctxT_b[:, kk, b * P:(b + 1) * P], start=kk == 0, stop=kk == KC - 1)
                    last.then_inc(f, 1)
                elif name == "weights":
                    ps, f = fill_b(("weights", 0))
                    pe.wait_ge(R["wgt_ready"], 1)
                    for b in range(G):
                        last = nc.tensor.transpose(ps[:, b * P:(b + 1) * P], wgt[:, b, :], ident[:, :])
                    last.then_inc(f, 1)
                elif name == "evidence":
                    ps, f = fill_b(("evidence", k))
                    has(B_USE["weights", 0])
                    for b in range(G):
                        last = mm(ps[:, b * P:(b + 1) * P], ctx_b[:, b, k * P:(k + 1) * P],
                                  wgtT[:, b * P:(b + 1) * P], start=True, stop=True)
                    last.then_inc(f, 1)
                elif name == "router":
                    ps, f = fill_b(("router", 0))
                    has(B_USE["evidence", 0])
                    has(B_USE["evidence", 1])
                    for kk in range(2 * KC):
                        source = hB if kk < KC else evT
                        last = mm(ps[0:E, :], w_r[:, kk, :], source[:, kk % KC, :], start=kk == 0,
                                  stop=kk == 2 * KC - 1)
                    last.then_inc(f, 1)
                elif name == "router_turn":
                    ps, f = fill_b(("router", 1))
                    has(B_USE["router", 0])
                    for b in range(G):
                        last = nc.tensor.transpose(ps[:, b * E:(b + 1) * E], logitT[:, b * P:(b + 1) * P],
                                                   ident[0:E, 0:E])
                    last.then_inc(f, 1)
                elif name in ("expert_x", "expert_v"):
                    w, c0 = (w_e1, k * P) if k < EC else (w_g1, (k - EC) * P)
                    if name == "expert_x":
                        fill_b(("expert", k))
                    b = B_USE["expert", k][0]
                    source, k0 = (hB, 0) if name == "expert_x" else (evT, KC)
                    for kk in range(KC):
                        last = mm(bank[b][:, :], w[:, k0 + kk, c0:c0 + P], source[:, kk, :],
                                  start=k0 + kk == 0, stop=k0 + kk == 2 * KC - 1)
                    if name == "expert_v":
                        last.then_inc(filled[b], 1)
                elif name in ("mix0", "mix1"):
                    half = int(name[-1])
                    ps, f = fill_b(("mix", 2 * k + half))
                    if k == half == 0:
                        pe.wait_ge(R["hidden_ready"], EC + 2)
                    for side in range(2):
                        e = 2 * half + side
                        chunks = range(4 * e, 4 * e + 4) if e < E else range(EC, EC + 2)
                        o = ps[:, side * C:(side + 1) * C]
                        for j in chunks:
                            w = w_e2[:, j, :] if e < E else w_g2[:, j - EC, :]
                            mm(o, hidden[:, j, k * P:(k + 1) * P], w, start=j == chunks[0], stop=False)
                        last = mm(o, row_of[:, e, :], bias_parts[:, :], start=False, stop=True)
                    last.then_inc(f, 1)

            def round_(steps, n):
                first_round[0] = steps is ONLY_A
                enter(pe, n)
                for stage, step in steps:
                    (step_a if stage == "A" else step_b)(*step)
                leave(pe)

            round_(ONLY_A, 1)
            with pe.Fori(1, NG) as i:
                round_(BOTH, i + 1)
            round_(ONLY_B, NG + 1)

        @block.scalar
        def _(act):
            f_ = nc.scalar.activation

            drains = [0]

            def begin():
                act.wait_ge(s_fill, drains[0] + 1)
                return bank[4 + drains[0] % 4]

            def end(ins):
                ins.then_inc(s_drain, 1)
                drains[0] += 1

            act.wait_ge(s_small, 16 * N_SMALL)
            f_(cond_th[:, :], cond[:, :], ACT.Tanh, scale=0.5).then_inc(s_act, 1)
            ps = begin()
            f_(condT[:, :, :].rearrange("p c b -> p (c b)"), ps[:, 0:KC * B], ACT.Copy)
            end(f_(siluT[:, :, :].rearrange("p c b -> p (c b)"), ps[:, KC * B:2 * KC * B], ACT.Copy, scale=0.5))

            def vector_rows(first, count, bias):
                for j in range(count):
                    if j % 4 == 0:
                        ps = begin()
                    ins = f_(vectors[:, :, first + j, :], ps[:, j % 4 * B:(j % 4 + 1) * B]
                             .rearrange("p (n g) -> p n g", g=G), ACT.Identity, bias=bias[:, j:j + 1])
                    if j % 4 == 3 or j == count - 1:
                        end(ins)

            vector_rows(0, 18, b_ada)
            vector_rows(EB, EC + 2, b_e1)
            ps = begin()
            end(f_(router_b[:, :, :], ps[0:E, 0:B].rearrange("p (n g) -> p n g", g=G), ACT.Identity,
                   bias=b_r[:, 0:1]))
            for a in (WqT, WkT, WvT):
                ps = begin()
                end(f_(a[:, :, :].rearrange("p c n -> p (c n)"), ps[:, :], ACT.Copy))
            for i in range(EC // 2):
                ps = begin()
                end(f_(e2T[:, :, 2 * i * P:(2 * i + 2) * P], ps[:, :].rearrange("p (c n) -> p c n", c=KC), ACT.Copy))
            ps = begin()
            end(f_(w_query[:, :, :].rearrange("p c n -> p (c n)"), ps[:, :], ACT.Copy, scale=float(C) ** -0.5))
            for kk in range(KC):
                for e in range(E):
                    ps = begin()
                    end(f_(w_e1[:, KC + kk, e * RH:(e + 1) * RH], ps[:, :], ACT.Copy))
            ps = begin()
            end(f_(w_g1[:, KC:, :].rearrange("p c n -> p (c n)"), ps[:, :], ACT.Copy))
            ps = begin()
            end(f_(w_r[:, KC:, :].rearrange("p c n -> p (c n)"), ps[:, 0:KC * E], ACT.Copy))
            for i in range(EC // 2):
                ps = begin()
                end(f_(w_e2[:, 2 * i:2 * i + 2, :].rearrange("p c n -> p (c n)"), ps[:, :], ACT.Copy, scale=0.5))
            ps = begin()
            for i in range(3):
                last = f_(bias_rows[32 * i:32 * i + E, :], ps[32 * i:32 * i + E, 0:C], ACT.Copy)
            end(last)
            assert drains[0] == SETUP_FILLS
            act.drain().then_inc(s_ready, 1)

            def take(use):
                b, n = use
                act.wait_ge(filled[b], n + 1)
                return bank[b], drained[b]

            def modulated(dest, use, scale, shift, vec):
                ps, d = take(use)
                for b in range(G):
                    last = f_(dest[:, b * P:(b + 1) * P], ps[:, b * P:(b + 1) * P], ACT.Identity,
                              scale=vec[:, scale, b:b + 1], bias=vec[:, shift, b:b + 1])
                last.then_inc(d, 1)

            def copied(dest, use, **kw):
                ps, d = take(use)
                f_(dest, ps[:, :], ACT.Identity if kw else ACT.Copy, **kw).then_inc(d, 1)

            def exps(k, half):
                act.wait_ge(R["maxed"], 2 * k + half + 1)
                for j in range(4 * half, 4 * half + 4):
                    kw = {}
                    if k < UNITS:
                        h = HEAD_AT[8 * (k % 2) + j]
                        kw["accum_out"] = p_sum[:, k // 2 % 2, h:h + 1]
                    last = f_(prob[:, k % 2, j, :], score[:, k % 2, j, :], ACT.Exp,
                              scale=float(D) ** -0.5, bias=neg_max[:, k % 2, j:j + 1], **kw)
                last.then_inc(R["exped"], 1)

            def copy_inverse(n):
                act.wait_ge(R["valued"], n + 1)
                f_(oT[:, :, n % G * P:(n % G + 1) * P], bank[5][:, C:].rearrange("p (c n) -> p c n", c=KC), ACT.Copy)\
                    .then_inc(R["inv_copied"], 1)

            def copy_turned(k):
                act.wait_ge(R["turned"], k + 1)
                if k >= 2:
                    act.wait_ge(R["valued"], k // 2)
                f_(probT[:, k % 2, :, :], score[:, k % 2, :, :], ACT.Copy).then_inc(R["copied"], 1)

            def step_a(name, k):
                if name == "turn_ctx":
                    for c in range(KC):
                        copied(ctxT_a[:, c, :], A_USE["ctx", c])
                elif name == "turn_x":
                    if k == 1:
                        modulated(hT[:, 0, :], A_USE["x1", 0], SC1, SH1, vec_1)
                    else:
                        act.wait_ge(R["vec_a_loaded"], 16)
                        modulated(hT[:, 0, :], A_USE["x2", 0], SC2, SH2, vec_a)
                elif name == "q":
                    for c in range(KC):
                        copied(qT[:, c, :], A_USE[f"q{k}", c], bias=(b_qkv if k == 1 else b_q)[:, c:c + 1])
                elif name == "k":
                    for c in range(KC):
                        ps, d = take(A_USE[f"k{k}", c])
                        for e in range(2):
                            last = f_(kM[:, c, :, e, :], ps[:, :].rearrange("p (b n) -> p b n", b=G), ACT.Identity,
                                      scale=head_mask[:, e:e + 1], bias=b_k[:, k - 1, e, c:c + 1])
                        last.then_inc(d, 1)
                elif name == "unit_a":
                    if k % 2 and k % UNITS > 1:
                        copy_inverse(k // 2 - 1)
                    exps(k, 0)
                elif name == "unit_b":
                    if k % UNITS:
                        copy_turned(k - 1)
                    exps(k, 1)
                elif name == "last_a":
                    copy_turned(k)
                elif name == "last_b":
                    copy_inverse(k // 2)
                elif name == "project":
                    act.wait_ge(R["vec_a_loaded"], 16)
                    modulated(yT[:, 0, :], A_USE[f"y{k}", 0], (GA1, GA2)[k - 1], (GB1, GB2)[k - 1], vec_a)

            def step_b(name, k):
                if name == "turn_b":
                    if k == 3:
                        act.wait_ge(R["vec_b_loaded"], 16)
                        modulated(hB[:, 0, :], B_USE["x3", 0], SC3, SH3, vec_b)
                    else:
                        for c in range(KC):
                            copied(hB[:, c, :], B_USE["x4", c], scale=gamma[:, c:c + 1], bias=beta[:, c:c + 1])
                elif name == "mlp_a":
                    ps, d = take(B_USE["a", k])
                    if k >= 2:
                        use = B_USE["b", k - 2]
                        act.wait_ge(drained[use[0]], use[1] + 1)
                    f_(z[:, k % 2, :], ps[:, :], ACT.Identity, bias=b_m1[:, k:k + 1])
                    f_(th[:, k % 2, :], ps[:, :], ACT.Tanh, scale=0.5, bias=b_m1h[:, k:k + 1]).then_inc(d, 1)
                elif name == "mlp_down" and k % 4 == 3:
                    m = k // 4
                    modulated(hB[:, m, :], B_USE["down", m], GA3 + m, GB3 + m, vec_b)
                elif name == "query":
                    copied(qs[:, k, :], B_USE["query", k])
                elif name == "match":
                    ps, d = take(B_USE["match", 0])
                    act.wait_ge(R["wmax_ready"], 1)
                    for b in range(G):
                        last = f_(wgt[:, b, :], ps[:, b * P:(b + 1) * P], ACT.Exp, bias=w_max[:, b:b + 1])
                    last.then_inc(d, 1)
                elif name == "weights":
                    copied(wgtT[:, :], B_USE["weights", 0])
                elif name == "evidence":
                    copied(evT[:, k, :], B_USE["evidence", k])
                elif name == "router":
                    ps, d = take(B_USE["router", 0])
                    act.wait_ge(R["rb_ready"], 1)
                    for b in range(G):
                        last = f_(logitT[:, b * P:(b + 1) * P], ps[0:E, b * P:(b + 1) * P], ACT.Identity,
                                  bias=rb_b[:, b:b + 1])
                    last.then_inc(d, 1)
                elif name == "router_turn":
                    b, n = B_USE["router", 1]
                    act.wait_ge(drained[b], n + 1)
                    f_(l_exp[:, :, :], logit[:, :, :], ACT.Exp).then_inc(R["lexp_ready"], 1)
                elif name == "expert_v":
                    b, n = B_USE["expert", k]
                    act.wait_ge(drained[b], n + 1)
                    f_(th[:, k % 2, :], z[:, k % 2, :], ACT.Tanh, scale=0.5).then_inc(R["th_ready"], 1)
                elif name == "mix1":
                    ps, d = take(B_USE["mix", 2 * k + 1])
                    if k >= 2:
                        b, n = B_USE["mix", 2 * k - 3]
                        act.wait_ge(drained[b], n + 1)
                    f_(gate_th[:, k % 2, :], ps[:, C:2 * C], ACT.Tanh, scale=0.5).then_inc(R["gate_ready"], 1)

            def round_(steps, n):
                enter(act, n)
                for stage, step in steps:
                    (step_a if stage == "A" else step_b)(*step)
                leave(act)

            round_(ONLY_A, 1)
            with act.Fori(1, NG) as i:
                round_(BOTH, i + 1)
            round_(ONLY_B, NG + 1)

        @block.vector
        def _(dve):
            v = nc.vector

            setup = [0]

            def done(ins):
                ins.then_inc(s_dve, 1)
                setup[0] += 1

            def settle():
                dve.wait_ge(s_dve, setup[0])

            dve.wait_ge(s_small, 16 * N_SMALL)
            dve.wait_ge(s_act, 1)
            done(v.scalar_tensor_tensor(cond_silu[:, :], cond_th[:, :], 1.0, cond[:, :], ALU.add, ALU.mult))
            dve.wait_ge(s_const, 5)
            for e in range(2):
                done(v.tensor_reduce(head_mask[:, e:e + 1],
                                     ident[:, :].rearrange("p (g e d) -> p e g d", e=2, d=D)[:, e],
                                     AX.XY, ALU.add))
            settle()
            for e in range(2):
                done(v.tensor_scalar(b_k[:, 0, e, :], b_qkv[:, 2:4], head_mask[:, e:e + 1], None, ALU.mult))
                done(v.tensor_scalar(b_k[:, 1, e, :], b_kv[:, 0:2], head_mask[:, e:e + 1], None, ALU.mult))
            done(v.tensor_scalar(b_m1h[:, :], b_m1[:, :], 0.5, None, ALU.mult))
            dve.wait_ge(s_drain, 1 + 5)
            for row in (SC1, SC2, SC3):
                done(v.tensor_scalar(vectors[:, :, row:row + 2, :], vectors[:, :, row:row + 2, :], 1.0, None,
                                     ALU.add))
            for i, (gate, gb) in enumerate(((GA1, GB1), (GA2, GB2), (GA3, GB3))):
                for c in range(KC):
                    done(v.tensor_scalar(vectors[:, :, gb + c, :], vectors[:, :, gate + c, :],
                                         b_out[:, 2 * i + c:2 * i + c + 1], None, ALU.mult))
            settle()
            done(v.tensor_scalar(vectors[:, :, GA3:GA3 + 2, :], vectors[:, :, GA3:GA3 + 2, :], 0.5, None, ALU.mult))
            dve.wait_ge(s_fold, 16 * N_FOLD)
            done(v.tensor_scalar(w_g2[:, :, :], w_g2[:, :, :], 0.5, None, ALU.mult))
            dve.wait_ge(s_drain, SETUP_FILLS)
            for i in range(3):
                r = slice(32 * i, 32 * i + E)
                done(v.tensor_tensor(bias_rows[r, :], bias_rows[r, :], out_b3[r, :], ALU.add))
            settle()
            rest = bias_rows
            for i in range(3):
                done(v.tensor_copy(part_of[i][:, :], rest[:, :]))
                settle()
                done(v.tensor_copy(bias_parts[32 * i:32 * i + 32, :], part_of[i][32 * i:32 * i + 32, :]))
                if i < 2:
                    done(v.tensor_tensor(bias_rest[:, :], rest[:, :], part_of[i][:, :], ALU.subtract))
                    rest = bias_rest
                    settle()
            dve.drain().then_inc(s_ready, 1)

            count = [0]

            def step(ins):
                ins.then_inc(R["dve_step"], 1)
                count[0] += 1
                return count[0]

            def after(n):
                dve.wait_ge(R["dve_step"], n)

            def take(use):
                b, n = use
                dve.wait_ge(filled[b], n + 1)
                return bank[b], drained[b]

            def layer_norm(x, xn, k, stats, mean_var, var_eps, rstd, eps, sems):
                ready, rstd_ready, xn_ready = (R[s] for s in sems)
                ns = [step(v.bn_stats(stats[:, b, :], x[:, b, :])) for b in range(G)]
                for b in range(G):
                    after(ns[b])
                    n = step(v.bn_aggr(mean_var[:, b, :], stats[:, b, :]))
                after(n)
                v.tensor_scalar(var_eps[:, :], mean_var[:, :, 1], eps, None, ALU.add).then_inc(ready, 1)
                dve.wait_ge(rstd_ready, k)
                for b in range(G):
                    last = v.tensor_scalar(xn[:, b, :], x[:, b, :], mean_var[:, b, 0:1], rstd[:, b:b + 1],
                                           ALU.subtract, ALU.mult)
                last.then_inc(xn_ready, 1)

            def modulated(dest, use, scale, shift, vec):
                ps, d = take(use)
                for b in range(G):
                    last = v.tensor_scalar(dest[:, b * P:(b + 1) * P], ps[:, b * P:(b + 1) * P],
                                           vec[:, scale, b:b + 1], vec[:, shift, b:b + 1], ALU.mult, ALU.add)
                last.then_inc(d, 1)

            def maxima(k, half):
                if half == 0:
                    dve.wait_ge(R["scored"], k + 1)
                j = slice(4 * half, 4 * half + 4)
                after(step(v.tensor_reduce(rowmax[:, j], score[:, k % 2, j, :], AX.X, ALU.max)))
                v.tensor_scalar(neg_max[:, k % 2, j], rowmax[:, j], -float(D) ** -0.5, None, ALU.mult)\
                    .then_inc(R["maxed"], 1)

            def top(k, half):
                if half == 0:
                    dve.wait_ge(R["scored"], k + 1)
                heads = range(4 * half, 4 * half + 4)
                s = score[:, k % 2]
                at = heads[0]
                n = {j: step(v.max(top1[:, j - at, :], s[:, j, :])) for j in heads}
                for j in heads:
                    after(n[j])
                    n[j] = step(v.match_replace(left[:, j - at, :], top1[:, j - at, :], s[:, j, :], GONE))
                after(n[heads[-1]])
                v.tensor_scalar(neg_max[:, k % 2, heads[0]:heads[0] + 4], top1[:, :, 0],
                                -float(D) ** -0.5, None, ALU.mult).then_inc(R["maxed"], 1)
                for j in heads:
                    after(n[j])
                    n[j] = step(v.max(top2[:, j - at, :], left[:, j - at, :]))
                for j in heads:
                    after(n[j])
                    n[j] = step(v.match_replace(left[:, j - at, :], top2[:, j - at, :], left[:, j - at, :], GONE))
                return n[heads[-1]]

            def pick(k, half, n):
                dve.wait_ge(R["exped"], 2 * k + half + 1)
                after(n)
                for i in range(4):
                    j = 4 * half + i
                    h = HEAD_AT[8 * (k % 2) + j]
                    last = v.scalar_tensor_tensor(prob[:, k % 2, j, :], left[:, i, :], GONE, prob[:, k % 2, j, :],
                                                  ALU.is_equal, ALU.mult, accum_out=p_sum[:, k // 2 % 2, h:h + 1])
                last.then_inc(R["picked"], 1)

            def invert(n):
                if n < G:
                    dve.wait_ge(R["exped"], 4 * n + 4)
                else:
                    dve.wait_ge(R["picked"], 4 * (n - G) + 4)
                v.reciprocal(p_inv[:, n % 2, :], p_sum[:, n % 2, :]).then_inc(R["inverted"], 1)

            def output(n):
                b = n % G
                dve.wait_ge(R["inv_copied"], n + 1)
                out_ = oT[:, :, b * P:(b + 1) * P]
                v.tensor_tensor(out_, bank[5][:, 0:C].rearrange("p (c n) -> p c n", c=KC), out_, ALU.mult)\
                    .then_inc(R["o_ready"], 1)

            def step_a(name, k):
                if name == "ln":
                    if k == 2:
                        b, n = A_USE["r1", 1]
                        dve.wait_ge(drained[b], n + 1)
                        b, n = A_USE["r1", 0]
                        dve.wait_ge(drained[b], n + 1)
                    elif k == 3:
                        dve.wait_ge(R["x_loaded"], 16)
                        for c in range(KC):
                            b, n = A_USE["x2", c]
                            dve.wait_ge(filled[b], n + 1)
                    layer_norm(x_mid if k == 2 else x_in, xn, k - 1 if with_b[0] else k, stats, mean_var, var_eps,
                               rstd, EPS0,
                               ("var_ready", "rstd_ready", "xn_ready"))
                elif name == "turn_x":
                    if k == 1:
                        modulated(hT[:, 1, :], A_USE["x1", 1], SC1 + 1, SH1 + 1, vec_1)
                    else:
                        dve.wait_ge(R["vec_a_loaded"], 16)
                        modulated(hT[:, 1, :], A_USE["x2", 1], SC2 + 1, SH2 + 1, vec_a)
                elif name == "project":
                    dve.wait_ge(R["vec_a_loaded"], 16)
                    modulated(yT[:, 1, :], A_USE[f"y{k}", 1], (GA1, GA2)[k - 1] + 1, (GB1, GB2)[k - 1] + 1, vec_a)
                elif name == "v":
                    for p in range(2):
                        ps, d = take(A_USE[f"v{k}", p])
                        for e in range(2):
                            last = v.tensor_tensor(
                                vM[:, 2 * p:2 * p + 2, :, 2 * e, :],
                                ps[:, :].rearrange("p (b x e d) -> p b x e d", b=2, e=2, d=D)[:, :, :, e],
                                b_v[:, k - 1, :].rearrange("p (x e d) -> p x e d", e=2, d=D)[:, :, e]
                                .unsqueeze(1).to_broadcast([P, 2, 8, D]), ALU.add)
                        last.then_inc(d, 1)
                elif name in ("unit_a", "unit_b"):
                    half = int(name == "unit_b")
                    first = half == 0 and k % 2 == 0 and k % UNITS > 0
                    if k < UNITS:
                        maxima(k, half)
                        if first:
                            invert(k // 2 - 1)
                    else:
                        if first:
                            invert(k // 2 - 1)
                        pick(k, half, top(k, half))
                    if half == 0 and k % 2 and k % UNITS > 1:
                        output(k // 2 - 1)
                elif name == "last_a":
                    invert(k // 2)
                elif name == "last_b":
                    output(k // 2)
                elif name == "residual":
                    for p in range(2):
                        ps, d = take(A_USE[f"r{k}", p])
                        source, dest = x_in if k == 1 else x1, x1
                        if k == 1 and p == 0 and with_b[0]:
                            b, n = B_USE["r3", 1]
                            dve.wait_ge(drained[b], n + 1)
                        v.tensor_tensor(dest[:, 2 * p:2 * p + 2, :].rearrange("p b c -> p (b c)"), ps[:, :],
                                        source[:, 2 * p:2 * p + 2, :].rearrange("p b c -> p (b c)"), ALU.add)\
                            .then_inc(d, 1)

            def silu_done(j):
                dve.wait_ge(R["th_ready"], j + 1)
                v.scalar_tensor_tensor(hidden[:, j, :], th[:, j % 2, :], 1.0, z[:, j % 2, :], ALU.add, ALU.mult)\
                    .then_inc(R["hidden_ready"], 1)

            def step_b(name, k):
                if name == "lnb":
                    if k == 4:
                        for p in range(2):
                            b, n = B_USE["r3", p]
                            dve.wait_ge(drained[b], n + 1)
                    layer_norm(x1 if k == 3 else x2, xnb, k - 2, stats_b, mean_var_b, var_eps_b, rstd_b,
                               EPS0 if k == 3 else EPS1, ("var_ready_b", "rstd_ready_b", "xn_ready_b"))
                elif name == "turn_b" and k == 3:
                    dve.wait_ge(R["vec_b_loaded"], 16)
                    modulated(hB[:, 1, :], B_USE["x3", 1], SC3 + 1, SH3 + 1, vec_b)
                elif name == "mlp_b":
                    b, n = B_USE["a", k]
                    dve.wait_ge(drained[b], n + 1)
                    n = step(v.scalar_tensor_tensor(z[:, k % 2, :], th[:, k % 2, :], 1.0, z[:, k % 2, :],
                                                    ALU.add, ALU.mult))
                    ps, d = take(B_USE["b", k])
                    after(n)
                    v.scalar_tensor_tensor(hidden[:, k, :], ps[:, :], b_m1[:, MC + k:MC + k + 1], z[:, k % 2, :],
                                           ALU.add, ALU.mult).then_inc(d, 1)
                elif name == "residual_b":
                    for p in range(2):
                        ps, d = take(B_USE["r3", p])
                        v.tensor_tensor(x2[:, 2 * p:2 * p + 2, :].rearrange("p b c -> p (b c)"), ps[:, :],
                                        x1[:, 2 * p:2 * p + 2, :].rearrange("p b c -> p (b c)"), ALU.add)\
                            .then_inc(d, 1)
                elif name == "match":
                    ps, d = take(B_USE["match", 0])
                    v.tensor_reduce(w_max[:, :], ps[:, :].rearrange("p (b n) -> p b n", b=G), AX.X, ALU.max,
                                    negate=True).then_inc(R["wmax_ready"], 1)
                elif name == "normalise":
                    b, n = B_USE["match", 0]
                    dve.wait_ge(drained[b], n + 1)
                    after(step(v.tensor_reduce(w_sum[:, :], wgt[:, :, :], AX.X, ALU.add)))
                    after(step(v.reciprocal(w_sum[:, :], w_sum[:, :])))
                    v.tensor_tensor(wgt[:, :, :], wgt[:, :, :], w_sum[:, :].unsqueeze(2).to_broadcast([P, G, P]),
                                    ALU.mult).then_inc(R["wgt_ready"], 1)
                elif name == "router_turn":
                    ps, d = take(B_USE["router", 1])
                    logits = ps[:, 0:G * E].rearrange("p (b e) -> p b e", b=G)
                    after(step(v.tensor_reduce(l_max[:, :], logits, AX.X, ALU.max)))
                    v.tensor_tensor(logit[:, :, :], logits, l_max[:, :].unsqueeze(2).to_broadcast([P, G, E]),
                                    ALU.subtract).then_inc(d, 1)
                elif name == "route":
                    dve.wait_ge(R["lexp_ready"], 1)
                    after(step(v.tensor_reduce(l_sum[:, :], l_exp[:, :, :], AX.X, ALU.add)))
                    after(step(v.reciprocal(l_sum[:, :], l_sum[:, :])))
                    route_step[0] = step(v.scalar_tensor_tensor(
                        route[:, :, :], l_exp[:, :, :], 0.5, l_sum[:, :].unsqueeze(2).to_broadcast([P, G, E]),
                        ALU.mult, ALU.mult))
                elif name == "expert_v":
                    ps, d = take(B_USE["expert", k])
                    if k == 0:
                        dve.wait_ge(R["vec_b_loaded"], 16)
                    if k >= 2:
                        dve.wait_ge(R["hidden_ready"], k - 1)
                    v.tensor_tensor(z[:, k % 2, :].rearrange("p (b n) -> p b n", b=G),
                                    ps[:, :].rearrange("p (b n) -> p b n", b=G),
                                    vec_b[:, EB + k, :].unsqueeze(2).to_broadcast([P, G, P]), ALU.add)\
                        .then_inc(d, 1)
                    if k:
                        silu_done(k - 1)
                elif name == "expert_end":
                    silu_done(EC + 1)
                elif name == "mix0":
                    ps, d = take(B_USE["mix", 2 * k])
                    after(route_step[0])
                    after(step(v.tensor_scalar(mix[:, k, :], ps[:, 0:C], route[:, k, 0:1], None, ALU.mult)))
                    v.scalar_tensor_tensor(mix[:, k, :], ps[:, C:2 * C], route[:, k, 1:2], mix[:, k, :],
                                           ALU.mult, ALU.add).then_inc(d, 1)
                elif name == "mix1":
                    ps, d = take(B_USE["mix", 2 * k + 1])
                    b, n = B_USE["mix", 2 * k]
                    dve.wait_ge(drained[b], n + 1)
                    dve.wait_ge(R["gate_ready"], k + 1)
                    n = step(v.scalar_tensor_tensor(mix[:, k, :], ps[:, 0:C], route[:, k, 2:3], mix[:, k, :],
                                                    ALU.mult, ALU.add))
                    after(n)
                    v.scalar_tensor_tensor(mix[:, k, :], gate_th[:, k % 2, :], 1.0, mix[:, k, :],
                                           ALU.add, ALU.mult).then_inc(d, 1)

            route_step = [0]
            with_b = [False]

            def round_(steps, n):
                count[0] = 0
                with_b[0] = steps is BOTH
                enter(dve, n)
                if steps is ONLY_A:
                    dve.wait_ge(s_const, 10)
                for stage, step_ in steps:
                    (step_a if stage == "A" else step_b)(*step_)
                leave(dve)

            round_(ONLY_A, 1)
            with dve.Fori(1, NG) as i:
                round_(BOTH, i + 1)
            round_(ONLY_B, NG + 1)


_INS = ["x", "cond_1024", "ctx_1024"] + [f"L0_xcond_{n}" for n in (
    "w_ada", "b_ada", "w_qkv", "b_qkv", "w_so", "b_so", "w_q", "b_q", "w_kv", "b_kv", "w_co", "b_co", "w_m1", "b_m1",
    "w_m2", "b_m2")] + [f"L1_xcond_{n}" for n in (
        "ln_gamma", "ln_beta", "Wq", "Wk", "Wv", "router_W", "router_b", "e_w1", "e_b1", "e_w2", "e_b2", "gate_w1",
        "gate_b1", "gate_w2", "gate_b2", "out_w", "out_b")]


def kernel(**inputs):
    import numpy as _np
    import concourse.bacc as _bacc
    from concourse import mybir as _mybir
    from concourse.bass_utils import run_bass_kernel_spmd as _run

    nc = _bacc.Bacc("TRN2", target_bir_lowering=False, num_devices=1)
    arrays, t = {}, {}
    for name in _INS:
        a = _np.ascontiguousarray(inputs[name])
        arrays[f"in_{name}"] = a
        t[name] = nc.dram_tensor(f"in_{name}", a.shape, _mybir.dt.from_np(a.dtype), kind="ExternalInput").ap()
    out = nc.dram_tensor("out", arrays["in_x"].shape, _mybir.dt.float32, kind="ExternalOutput").ap()
    program(nc, t, out)
    r = _run(nc, [arrays], core_ids=[0])
    return r.results[0]["out"]
```

```python
from contextlib import ExitStack

import concourse.bass as bass
from concourse import mybir
import numpy as np

F32 = mybir.dt.float32
BF16 = mybir.dt.bfloat16
ACT = mybir.ActivationFunctionType
ALU = mybir.AluOpType
AX = mybir.AxisListType

P = 128
C = 256
KC = C // P
G = 4
T = G * P
H = 16
D = C // H
HID = 1024
E = 3
RH = 2 * C
EC = E * RH // P
MC = HID // P
TOPK = 16
GONE = float(np.float32(-3.0e38))
EPS0, EPS1 = 1e-6, 1e-5

SH1, SC1, GA1, SH2, SC2, GA2, SH3, SC3, GA3 = range(0, 18, 2)
GB1, GB2, GB3 = 18, 20, 22
N_SMALL, N_FOLD, N_EVIDENCE, N_ANCHOR, N_MAIN_A, N_MAIN_B = 21, 5, 3, 5, 5, 7
EB = 24
GB = EB + EC
NV = GB + 2
N1 = SC1 + 2
NA = GB2 + 2

SETUP = (
    [("cond", 0)] + [("turn_w", i) for i in range(3)] + [("turn_e2", i) for i in range(EC // 2)]
    + [("query", 0), ("e_b2", 0)] + [("ada", i) for i in range(5)]
)
FOLDS = (
    [("anchor", i) for i in range(4)] + [("anchor_router", 0)]
    + [("evidence", i) for i in range(2 * E)] + [("evidence_gate", 0), ("evidence_router", 0)]
    + [("e2_out", i) for i in range(EC // 2)]
)


UNITS = 2 * G


def attention_steps(n):
    ks = range(n * UNITS, (n + 1) * UNITS)
    return [(s, k) for k in ks for s in ("unit_a", "unit_b", "unit_c")] + [("last_a", ks[-1]), ("last_b", ks[-1])]


def with_next(steps, at):
    out = list(steps)
    for step, i in zip([("ln", 3), ("turn_next", 0), ("turn_next", 1), ("ctx_next", 0), ("ctx_next", 1)], at):
        out.insert(i, step)
    return out


STAGE_A = (
    [("q", 1), ("k", 1), ("first_scores", 0)]
    + attention_steps(0)
    + [("k", 2), ("project", 1), ("v", 2), ("residual", 1), ("ln", 2), ("turn_x", 2), ("q", 2),
       ("first_scores", UNITS)]
    + with_next(attention_steps(1), (12, 19, 22, 26, 29))
    + [("v_next", 0), ("project", 2), ("v_next", 1), ("residual", 2)]
)
STAGE_B = (
    [("lnb", 3), ("turn_b", 3)]
    + [(s, m) for m in range(MC) for s in ("mlp_a", "mlp_b")]
    + [("mlp_down", i) for i in range(MC)]
    + [("residual_b", 0), ("lnb", 4), ("turn_b", 4), ("query", 0), ("query", 1), ("match", 0), ("normalise", 0)]
    + [("weights", 0), ("evidence", 0), ("evidence", 1), ("router", 0), ("router_turn", 0), ("route", 0)]
    + [(s, j) for j in range(EC + 2) for s in ("expert_x", "expert_v")] + [("expert_end", 0)]
    + [(s, b) for b in range(G) for s in ("mix0", "mix1", "add")]
)


BESIDE = [1, 1, 1, 0, 1, 0, 2, 1, 0, 2, 1, 0, 0, 1, 1, 1, 2, 0, 3, 1, 0, 1, 2, 0, 2, 2, 0, 1, 0, 1, 1, 0, 0,
          2, 2, 0, 2, 5, 0, 2, 3, 2, 0, 3, 3, 1, 2, 1, 1, 4, 2, 4, 0, 1, 3, 0, 0, 1, 0, 2, 0, 1, 2, 0, 1, 0,
          0, 0, 0, 1, 0, 0]


def merged():
    out, b = [], 0
    for step, n in zip(STAGE_A, BESIDE, strict=True):
        out += [("A", step)] + [("B", s) for s in STAGE_B[b:b + n]]
        b += n
    assert b == len(STAGE_B)
    return out


ONLY_A = [("A", s) for s in (("turn_x", 1), ("turn_ctx", 1), ("v", 1))]
for _step in STAGE_A:
    ONLY_A.append(("A", _step))
    if _step[0] == "unit_b":
        ONLY_A += [("fold", f) for i, f in enumerate(FOLDS) if max(i // 2, i - 3) == _step[1]]
ONLY_B = [("B", s) for s in STAGE_B]
BOTH = merged()


def uses(names, banks, fixed=None):
    count, out, i = {b: 0 for b in banks}, {}, 0
    for name in names:
        if fixed and name in fixed:
            b = fixed[name]
        else:
            b = banks[i % len(banks)]
            i += 1
        out[name] = (b, count[b])
        count[b] += 1
    return out


def two(*names):
    return [(n, i) for n in names for i in range(2)]


A_BEFORE = two("q1", "k1")
A_BETWEEN = two("k2", "y1", "v2", "r1", "x2", "q2")
A_WITHIN = two("x3", "ctx3")
A_AFTER = [("v3", 0), ("y2", 0), ("y2", 1), ("v3", 1)] + two("r2")
A_USE = uses(A_BEFORE + A_BETWEEN + A_WITHIN + A_AFTER, (4, 5), {n: 4 for n in A_WITHIN})
for _n, _name in enumerate(("x1", "ctx1", "v1")):
    A_USE[_name, 0], A_USE[_name, 1] = (6, _n), (7, _n)
B_USE = uses(
    two("x3")
    + [(n, m) for m in range(MC) for n in ("a", "b")]
    + two("down", "r3", "x4", "query") + [("match", 0), ("weights", 0)] + two("evidence")
    + [("router", 0), ("router", 1)] + [("expert", j) for j in range(EC + 2)]
    + [("mix", 2 * b + i) for b in range(G) for i in range(2)],
    (6, 7),
)


def slot_of(h):
    c, g, e = h // 8, h % 8 // 2, h % 2
    return 4 * g + 2 * c + e


HEAD_AT = sorted(range(H), key=slot_of)


def program(nc, t, out):
    B = t["x"].shape[0]
    NG = B // G
    ctx = ExitStack()
    with ctx:
        def sb(name, shape, kind=F32):
            return ctx.enter_context(nc.sbuf_tensor(name, shape, kind))

        ident = sb("ident", [P, P])
        w_qkv = sb("w_qkv", [P, KC, 3 * C])
        w_so = sb("w_so", [P, KC, C])
        w_q = sb("w_q", [P, KC, C])
        w_kv = sb("w_kv", [P, KC, 2 * C])
        w_co = sb("w_co", [P, KC, C])
        w_m1 = sb("w_m1", [P, KC, 2 * HID])
        w_m2 = sb("w_m2", [P, MC, C])
        w_query = sb("w_query", [P, KC, C])
        w_r = sb("w_r", [P, 2 * KC, E])
        w_e1 = sb("w_e1", [P, 2 * KC, E * RH])
        w_g1 = sb("w_g1", [P, 2 * KC, C])
        w_g2 = sb("w_g2", [P, KC, C])
        w_e2 = sb("w_e2", [P, EC, C])
        bias_parts = sb("bias_parts", [P, C], BF16)
        row_of = sb("row_of", [P, E + 1, P], BF16)
        router_b = sb("router_b", [E, NG, G])
        vec_a = sb("vec_a", [P, NA, G])
        vec_1 = sb("vec_1", [P, N1, G])
        vec_b = sb("vec_b", [P, NV, G])
        rb_b = sb("rb_b", [E, G])
        minus_half = sb("minus_half", [P, G])
        b_qkv = sb("b_qkv", [P, 6])
        b_q = sb("b_q", [P, 2])
        b_kv = sb("b_kv", [P, 4])
        b_out = sb("b_out", [P, 6])
        b_m1 = sb("b_m1", [P, 2 * MC])
        b_m1h = sb("b_m1h", [P, 2 * MC])
        gamma = sb("gamma", [P, KC])
        beta = sb("beta", [P, KC])
        head_mask = sb("head_mask", [P, 2])
        b_v = sb("b_v", [P, 2, C])
        b_k = sb("b_k", [P, 2, 2, KC])

        with ExitStack() as early:
            def st(name, shape, kind=F32):
                return early.enter_context(nc.sbuf_tensor(name, shape, kind))

            e1_ev = st("e1_ev", [P, KC, E * RH])
            g1_raw = st("g1_raw", [P, 2 * KC, C])
            r_raw = st("r_raw", [P, 2 * KC, E])
            out_w = st("out_w", [P, KC, C])
            WvT = st("WvT", [P, KC, C])
            e2T = st("e2T", [P, KC, EC * P])
            vectors = st("vectors", [P, NG, NV, G])
            e1_anchor = st("e1_anchor", [P, KC, E * RH])
            condT = st("condT", [P, KC, B])
            b_e1 = st("b_e1", [P, EC + 2])
            b_r = st("b_r", [E, 1])
            w_ada = st("w_ada", [P, KC, 9 * C])
            Wq = st("Wq", [P, KC, C])
            Wk = st("Wk", [P, KC, C])
            Wv = st("Wv", [P, KC, C])
            WqT = st("WqT", [P, KC, C])
            WkT = st("WkT", [P, KC, C])
            e2 = st("e2", [P, EC, C])
            eb2T = st("eb2T", [P, KC, E])
            out_b3 = st("out_b3", [3 * 32, C])
            bias_rows = st("bias_rows", [P, C])
            bias_rest = st("bias_rest", [P, C])
            part_of = [st(f"part{i}", [P, C], BF16) for i in range(3)]
            row_of32 = st("row_of32", [P, E + 1, P])
            cond = st("cond", [B, C])
            cond_silu = st("cond_silu", [B, C])
            cond_th = st("cond_th", [B, C])
            siluT = st("siluT", [P, KC, B])
            b_ada = st("b_ada", [P, 18])

        xnb = sb("xnb", [P, G, C])
        qs = xnb[:, :, :].rearrange("p (k g) c -> p k (g c)", k=KC)
        evT = qs
        mix = xnb
        hB = sb("hB", [P, KC, T])
        z = sb("z", [P, 2, T])
        th = sb("th", [P, 2, T])
        hidden = sb("hidden", [P, EC + 2, T])
        x2 = sb("x2", [P, G, C])
        x1 = sb("x1", [P, G, C])
        x_mid = x1
        ctx_b = sb("ctx_b", [P, G, C])
        ctxT_b = sb("ctxT_b", [P, KC, T])
        ctxT_a = sb("ctxT_a", [P, KC, T])
        hT = sb("hT", [P, KC, T])
        qT = sb("qT", [P, KC, T])
        oT = qT
        kM = sb("kM", [P, KC, G, 2, P])
        yT2 = kM[:, :, 0:2, :, :].rearrange("p c b e n -> p c (b e n)")
        yT = {1: hT, 2: yT2}
        vM = sb("vM", [P, G, H // 2, 3, D])
        top2 = sb("top2", [P, 4, 8])
        rowmax = sb("rowmax", [P, 8])
        neg_max = sb("neg_max", [P, 2, 8])
        left = sb("left", [P, 4, P])
        prob = sb("prob", [P, 2, 8, P])
        probT = sb("probT", [P, 2, 8, P])
        p_sum = sb("p_sum", [P, 2, H])
        p_inv = sb("p_inv", [P, 2, H])
        p_inv_wide = sb("p_inv_wide", [P, H, D])
        stats_b = top2[:, :, 0:6]
        mean_var_b = sb("mean_var_b", [P, G, 2])
        var_eps_b = sb("var_eps_b", [P, G])
        rstd_b = sb("rstd_b", [P, G])
        wgt = z[:, 0, :].rearrange("p (b n) -> p b n", b=G)
        wgtT = z[:, 1, :]
        w_max = sb("w_max", [P, G])
        w_sum = sb("w_sum", [P, G])
        logitT = th[0:E, 0, :]
        logit = sb("logit", [P, G, E])
        l_max = w_max
        l_exp = logit
        l_sum = w_sum
        route = sb("route", [P, G, E])
        gate_th = z[:, 0, :].rearrange("p (i c) -> p i c", i=2)

        x_in = sb("x_in", [P, G, C])
        ctx_a = sb("ctx_a", [P, G, C])
        xn = sb("xn", [P, G, C])
        mean_var = sb("mean_var", [P, G, 2])
        var_eps = sb("var_eps", [P, G])
        rstd = sb("rstd", [P, G])
        top1 = sb("top1", [P, 4, 8])
        stats = top1[:, :, 0:6]

        bank = [ctx.enter_context(nc.psum_tensor(f"bank{i}", [P, T], F32)) for i in range(4, 8)]
        bank = {i + 4: b for i, b in enumerate(bank)}
        score = ctx.enter_context(nc.psum_tensor("score", [P, 2, 8, P], F32))

        def sem(name):
            return ctx.enter_context(nc.semaphore(name))

        go, seen = sem("go"), sem("seen")
        s_small, s_ada, s_fold, s_evidence, s_anchor, s_main_a, s_main_b, s_group = (
            sem(n) for n in ("s_small", "s_ada", "s_fold", "s_evidence", "s_anchor", "s_main_a", "s_main_b", "s_group"))
        s_fill, s_drain = sem("s_fill"), sem("s_drain")
        s_cond, s_qkv, s_x, s_out = sem("s_cond"), sem("s_qkv"), sem("s_x"), sem("s_out")
        s_const, s_dve, s_act, s_ready = sem("s_const"), sem("s_dve"), sem("s_act"), sem("s_ready")
        names = ("arrived filled4 filled5 filled6 filled7 drained4 drained5 drained6 drained7 "
                 "vec_1_loaded vec_a_loaded vec_b_loaded rb_ready "
                 "var_ready rstd_ready xn_ready var_ready_b rstd_ready_b xn_ready_b "
                 "scored maxed exped picked turned copied inverted widened valued inv_copied o_ready dve_step act_step "
                 "th_ready hidden_ready wmax_ready wgt_ready lexp_ready "
                 "gate_ready summed x_loaded loaded moved mix_free").split()
        R = {n: sem(n) for n in names}
        nums = [R[n].num for n in names]
        round_sems = range(min(nums), max(nums) + 1)
        assert len(round_sems) == len(names)
        filled = {i: R[f"filled{i}"] for i in (4, 5, 6, 7)}
        drained = {i: R[f"drained{i}"] for i in (4, 5, 6, 7)}

        def all_o_before(name):
            return {True: 0}.get(name in A_BEFORE, G if name in A_BETWEEN else 2 * G)

        vectors_d = nc.dram_tensor("vectors_d", [NG, P, NV * G], F32, kind="Internal").ap()
        x_d = t["x"].rearrange("(n g) l c -> n l g c", g=G)
        ctx_d = t["ctx_1024"].rearrange("(n g) l c -> n l g c", g=G)
        out_d = out.rearrange("(n g) l c -> n g l c", g=G)

        def rows(a):
            return a.rearrange("(k p) n -> p k n", p=P)

        def cols(a):
            return a.rearrange("(m p) -> p m", p=P)

        e_w1 = t["L1_xcond_e_w1"]
        g_w1 = rows(t["L1_xcond_gate_w1"])
        r_w = rows(t["L1_xcond_router_W"])

        def e1_part(part):
            return [rows(e_w1[e])[:, KC * part:KC * part + KC, :] for e in range(E)]

        block = ctx.enter_context(nc.Block())

        @block.sync
        def _(sp):
            sp.dma_start(cond[:, :], t["cond_1024"]).then_inc(s_cond, 16)
            for dst, name in ((Wq, "Wq"), (Wk, "Wk"), (Wv, "Wv")):
                sp.dma_start(dst[:, :, :], rows(t[f"L1_xcond_{name}"])).then_inc(s_qkv, 16)
            for dst, name in ((out_w, "out_w"), (w_g2, "gate_w2")):
                sp.dma_start(dst[:, :, :], rows(t[f"L1_xcond_{name}"])).then_inc(s_fold, 16)
            for e in range(E):
                sp.dma_start(e2[:, 4 * e:4 * e + 4, :], rows(t["L1_xcond_e_w2"][e])).then_inc(s_fold, 16)
            n_small = 0
            for dst, src in [
                (b_ada[:, :], cols(t["L0_xcond_b_ada"])),
                (b_e1[:, 0:EC], t["L1_xcond_e_b1"].rearrange("e (m p) -> p (e m)", p=P)),
                (b_e1[:, EC:EC + 2], cols(t["L1_xcond_gate_b1"])),
                (b_r[:, :], t["L1_xcond_router_b"].rearrange("(e a) -> e a", a=1)),
                (b_qkv[:, :], cols(t["L0_xcond_b_qkv"])), (b_q[:, :], cols(t["L0_xcond_b_q"])),
                (b_kv[:, :], cols(t["L0_xcond_b_kv"])), (b_out[:, 0:2], cols(t["L0_xcond_b_so"])),
                (b_out[:, 2:4], cols(t["L0_xcond_b_co"])), (b_out[:, 4:6], cols(t["L0_xcond_b_m2"])),
                (b_m1[:, :], cols(t["L0_xcond_b_m1"])),
                (gamma[:, :], cols(t["L1_xcond_ln_gamma"])), (beta[:, :], cols(t["L1_xcond_ln_beta"])),
                (eb2T[:, 0, :], t["L1_xcond_e_b2"].rearrange("e (k p) -> p k e", p=P)[:, 0, :]),
                (eb2T[:, 1, :], t["L1_xcond_e_b2"].rearrange("e (k p) -> p k e", p=P)[:, 1, :]),
                (out_b3[:, :], t["L1_xcond_out_b"].rearrange("(a n) -> a n", a=1).to_broadcast([3 * 32, C])),
                (b_v[:, 0, :], t["L0_xcond_b_qkv"][2 * C:3 * C].rearrange("(a n) -> a n", a=1).to_broadcast([P, C])),
                (b_v[:, 1, :], t["L0_xcond_b_kv"][C:2 * C].rearrange("(a n) -> a n", a=1).to_broadcast([P, C])),
                *((bias_rows[32 * i + E:32 * i + E + 1, :], t["L1_xcond_gate_b2"].rearrange("(a n) -> a n", a=1))
                  for i in range(3)),
            ]:
                if n_small == N_SMALL - 3:
                    sp.wait_ge(s_const, 4)
                sp.dma_start(dst, src, allow_slow_non_contiguous=True).then_inc(s_small, 16)
                n_small += 1
            assert n_small == N_SMALL
            sp.dma_start(w_ada[:, :, :], rows(t["L0_xcond_w_ada"])).then_inc(s_ada, 16)
            sp.dma_start(x_in[:, :, :], x_d[0]).then_inc(s_x, 16)
            for dst, name in ((w_qkv, "w_qkv"), (w_so, "w_so"), (w_q, "w_q"), (w_kv, "w_kv"), (w_co, "w_co")):
                sp.dma_start(dst[:, :, :], rows(t[f"L0_xcond_{name}"])).then_inc(s_main_a, 16)
            sp.dma_start(ctx_a[:, :, :], ctx_d[0]).then_inc(s_group, 16)
            sp.dma_start(g1_raw[:, :, :], g_w1[:, KC:, :]).then_inc(s_anchor, 16)
            sp.dma_start(r_raw[:, :, :], r_w[:, KC:, :]).then_inc(s_anchor, 16)
            for e, src in enumerate(e1_part(2)):
                sp.dma_start(e1_anchor[:, :, e * RH:(e + 1) * RH], src).then_inc(s_anchor, 16)
            for e, src in enumerate(e1_part(1)):
                sp.dma_start(e1_ev[:, :, e * RH:(e + 1) * RH], src).then_inc(s_evidence, 16)
            for dst, name in ((w_m1, "w_m1"), (w_m2, "w_m2")):
                sp.dma_start(dst[:, :, :], rows(t[f"L0_xcond_{name}"])).then_inc(s_main_b, 16)
            for e, src in enumerate(e1_part(0)):
                sp.dma_start(w_e1[:, 0:KC, e * RH:(e + 1) * RH], src).then_inc(s_main_b, 16)
            sp.dma_start(w_g1[:, 0:KC, :], g_w1[:, 0:KC, :]).then_inc(s_main_b, 16)
            sp.dma_start(w_r[:, 0:KC, :], r_w[:, 0:KC, :]).then_inc(s_main_b, 16)
            sp.wait_ge(s_group, 16)
            sp.wait_ge(s_main_a, 16 * N_MAIN_A)
            sp.wait_ge(s_ready, 4)
            sp.sem_inc(go)
            sp.dma_start(vectors_d[:, :, 0:EB * G].rearrange("n p v -> p n v"),
                         vectors[:, :, 0:EB, :].rearrange("p n v g -> p n (v g)")).then_inc(s_out, 16)
            sp.wait_ge(s_out, 16)

            def after(use):
                b, n = use
                sp.wait_ge(drained[b], n + 1)

            def round_(with_a, with_b, next_a, group_b):
                if with_b:
                    sp.wait_ge(s_out, group_b * (16 * G) + 32)
                    sp.sem_inc(R["mix_free"])
                if with_a:
                    sp.dma_start(vec_a[:, :, :].rearrange("p v g -> p (v g)"), vectors_d[group_b + 1][:, 0:NA * G])\
                        .then_inc(R["vec_a_loaded"], 16)
                if with_b:
                    sp.dma_start(vec_b[:, :, :].rearrange("p v g -> p (v g)"), vectors_d[group_b])\
                        .then_inc(R["vec_b_loaded"], 16)
                if with_a:
                    if not with_b:
                        sp.wait_ge(s_drain, len(SETUP) + FOLDS.index(("anchor", 3)) + 1)
                        sp.dma_start(vectors_d[:, :, EB * G:].rearrange("n p v -> p n v"),
                                     vectors[:, :, EB:, :].rearrange("p n v g -> p n (v g)")).then_inc(s_out, 16)
                        sp.wait_ge(s_out, 32)
                        after(A_USE["x1", 0])
                        after(A_USE["x1", 1])
                    sp.dma_start(vec_1[:, :, :].rearrange("p v g -> p (v g)"), vectors_d[next_a][:, 0:N1 * G])\
                        .then_inc(R["vec_1_loaded"], 16)
                    after(A_USE["r1", 1])
                    sp.dma_start(x_in[:, :, :], x_d[next_a]).then_inc(R["x_loaded"], 16)
                    after(A_USE["v2", 1])
                    sp.wait_ge(filled[A_USE["k2", 1][0]], A_USE["k2", 1][1] + 1)
                    if with_b:
                        after(B_USE["evidence", 1])
                    sp.dma_start(ctx_b[:, :, :], ctx_a[:, :, :]).then_inc(R["moved"], 16)
                    sp.dma_start(ctxT_b[:, :, :], ctxT_a[:, :, :]).then_inc(R["moved"], 16)
                    sp.wait_ge(R["moved"], 32)
                    sp.dma_start(ctx_a[:, :, :], ctx_d[next_a]).then_inc(R["loaded"], 16)
                if with_b:
                    for b in range(G):
                        sp.wait_ge(R["summed"], b + 1)
                        sp.dma_start(out_d[group_b, b], mix[:, b, :]).then_inc(s_out, 16)
                if with_a and not with_b:
                    sp.wait_ge(s_main_b, 16 * N_MAIN_B)
                if with_a:
                    sp.wait_ge(R["vec_1_loaded"], 16)
                    sp.wait_ge(R["x_loaded"], 16)
                    sp.wait_ge(R["loaded"], 16)
                sp.wait_ge(R["arrived"], 4)
                sp.sem_clear(round_sems)
                sp.sem_inc(go)

            round_(True, False, 1 % NG, -1)
            with sp.Fori(1, NG) as i:
                round_(True, True, (i + 1) % NG, i - 1)
            round_(False, True, None, NG - 1)
            sp.wait_ge(s_out, NG * (16 * G) + 32)

        def enter(eng, n):
            eng.wait_ge(go, n)
            eng.sem_inc(seen)

        def leave(eng):
            eng.drain().then_inc(R["arrived"], 1)

        @block.gpsimd
        def _(pool):
            pool.memset(minus_half[:, :], -0.5).then_inc(s_const, 1)
            pool.memset(ident[:, :], 0.0).then_inc(s_const, 1)
            pool.memset(row_of32[:, :, :], 0.0).then_inc(s_const, 1)
            pool.memset(bias_rows[:, :], 0.0).then_inc(s_const, 1)
            pool.wait_ge(s_const, 4)
            pool.affine_select(out=ident[:, :], in_=ident[:, :], compare_op=ALU.not_equal, fill=1.0, base=0,
                               pattern=[[-1, P]], channel_multiplier=1).then_inc(s_const, 1)
            for i in range(3):
                pool.affine_select(out=row_of32[:, :, :], in_=row_of32[:, :, :], compare_op=ALU.not_equal, fill=1.0,
                                   base=-32 * i, pattern=[[-1, E + 1], [0, P]], channel_multiplier=1)\
                    .then_inc(s_const, 1)
                pool.wait_ge(s_const, 6 + i)
            pool.tensor_copy(row_of[:, :, :], row_of32[:, :, :]).then_inc(s_const, 1)

            def rstd_a(k):
                pool.wait_ge(R["var_ready"], k)
                pool.tensor_tensor(rstd[:, :], var_eps[:, :], minus_half[:, :], ALU.pow).then_inc(R["rstd_ready"], 1)

            def round_(steps, n, group_b):
                enter(pool, n)
                if group_b is None:
                    pool.memset(vM[:, :, :, :], 0.0).then_inc(s_const, 1)
                else:
                    pool.tensor_copy(rb_b[:, :], router_b[:, group_b, :]).then_inc(R["rb_ready"], 1)
                for stage, (name, k) in steps:
                    if name == "ln":
                        rstd_a(k if steps is ONLY_A else k - 1)
                    elif (name == "unit_a" and k % 2 == 0 and k % UNITS) or name == "last_a":
                        m = (k - 1) // 2 if name == "unit_a" else k // 2
                        pool.wait_ge(R["inverted"], m + 1)
                        if m:
                            pool.wait_ge(R["valued"], m)
                        pool.tensor_copy(p_inv_wide[:, :, :], p_inv[:, m % 2, :].unsqueeze(2).to_broadcast([P, H, D]))\
                            .then_inc(R["widened"], 1)
                    elif name == "lnb":
                        pool.wait_ge(R["var_ready_b"], k - 2)
                        pool.tensor_tensor(rstd_b[:, :], var_eps_b[:, :], minus_half[:, :], ALU.pow)\
                            .then_inc(R["rstd_ready_b"], 1)
                    elif name == "add":
                        b, n_ = B_USE["mix", 2 * k + 1]
                        pool.wait_ge(drained[b], n_ + 1)
                        pool.tensor_tensor(mix[:, k, :], mix[:, k, :], x2[:, k, :], ALU.add)\
                            .then_inc(R["summed"], 1)
                leave(pool)

            rstd_a(1)
            pool.drain().then_inc(s_ready, 1)
            round_(ONLY_A, 1, None)
            with pool.Fori(1, NG) as i:
                round_(BOTH, i + 1, i - 1)
            round_(ONLY_B, NG + 1, NG - 1)

        @block.tensor
        def _(pe):
            mm = nc.tensor.matmul

            def drained_of(name, k):
                pe.wait_ge(s_drain, SETUP.index((name, k)) + 1)

            def setup_product(name, k, ps):
                if name == "cond":
                    for i, a in enumerate((cond, cond_silu)):
                        for c in range(KC):
                            last = nc.tensor.transpose(ps[:, (2 * i + c) * B:(2 * i + c + 1) * B],
                                                       a[:, c * P:(c + 1) * P], ident[0:B, 0:B])
                elif name == "turn_w":
                    if k == 0:
                        pe.wait_ge(s_qkv, 16 * 3)
                    for jj in range(KC):
                        for kk in range(KC):
                            last = nc.tensor.transpose(ps[:, (jj * KC + kk) * P:(jj * KC + kk + 1) * P],
                                                       (Wq, Wk, Wv)[k][:, kk, jj * P:(jj + 1) * P], ident[:, :])
                elif name == "turn_e2":
                    if k == 0:
                        pe.wait_ge(s_fold, 16 * N_FOLD)
                    for c in range(KC):
                        for r in range(2):
                            last = nc.tensor.transpose(ps[:, (c * 2 + r) * P:(c * 2 + r + 1) * P],
                                                       e2[:, 2 * k + r, c * P:(c + 1) * P], ident[:, :])
                elif name == "query":
                    drained_of("turn_w", 1)
                    for kk in range(KC):
                        for jj in range(KC):
                            last = mm(ps[:, kk * C:(kk + 1) * C], WqT[:, jj, kk * P:(kk + 1) * P], WkT[:, jj, :],
                                      start=jj == 0, stop=jj == KC - 1)
                elif name == "e_b2":
                    pe.wait_ge(s_small, 16 * N_SMALL)
                    for c in range(KC):
                        for i in range(3):
                            last = mm(ps[32 * i:32 * i + E, 0:C], eb2T[:, c, :], out_w[:, c, :], start=c == 0,
                                      stop=c == KC - 1)
                elif name == "e2_out":
                    drained_of("turn_e2", k)
                    for r in range(2):
                        for c in range(KC):
                            last = mm(ps[:, r * C:(r + 1) * C], e2T[:, c, (2 * k + r) * P:(2 * k + r + 1) * P],
                                      out_w[:, c, :], start=c == 0, stop=c == KC - 1)
                elif name == "ada":
                    if k == 0:
                        pe.wait_ge(s_ada, 16)
                        drained_of("cond", 0)
                    for m in range(4 * k, min(4 * k + 4, 18)):
                        for kk in range(KC):
                            last = mm(ps[:, m % 4 * B:(m % 4 + 1) * B], w_ada[:, kk, m * P:(m + 1) * P],
                                      siluT[:, kk, :], start=kk == 0, stop=kk == KC - 1)
                elif name == "evidence":
                    if k == 0:
                        pe.wait_ge(s_evidence, 16 * N_EVIDENCE)
                        drained_of("turn_w", 2)
                    kk, e = k // E, k % E
                    for jj in range(KC):
                        last = mm(ps[:, :], WvT[:, jj, kk * P:(kk + 1) * P], e1_ev[:, jj, e * RH:(e + 1) * RH],
                                  start=jj == 0, stop=jj == KC - 1)
                elif name == "evidence_gate":
                    for kk in range(KC):
                        for jj in range(KC):
                            last = mm(ps[:, kk * C:(kk + 1) * C], WvT[:, jj, kk * P:(kk + 1) * P], g1_raw[:, jj, :],
                                      start=jj == 0, stop=jj == KC - 1)
                elif name == "evidence_router":
                    for kk in range(KC):
                        for jj in range(KC):
                            last = mm(ps[:, kk * E:(kk + 1) * E], WvT[:, jj, kk * P:(kk + 1) * P], r_raw[:, jj, :],
                                      start=jj == 0, stop=jj == KC - 1)
                elif name == "anchor":
                    if k == 0:
                        pe.wait_ge(s_anchor, 16 * N_ANCHOR)
                    for j in range(4 * k, min(4 * k + 4, EC + 2)):
                        for kk in range(KC):
                            w = e1_anchor[:, kk, j * P:(j + 1) * P] if j < EC else \
                                g1_raw[:, KC + kk, (j - EC) * P:(j - EC + 1) * P]
                            last = mm(ps[:, j % 4 * B:(j % 4 + 1) * B], w, condT[:, kk, :], start=kk == 0,
                                      stop=kk == KC - 1)
                elif name == "anchor_router":
                    for kk in range(KC):
                        last = mm(ps[0:E, 0:B], r_raw[:, KC + kk, :], condT[:, kk, :], start=kk == 0,
                                  stop=kk == KC - 1)
                last.then_inc(s_fill, 1)

            pe.wait_ge(s_const, 5)
            pe.wait_ge(s_dve, 1)
            for n, step in enumerate(SETUP):
                if n >= 4:
                    pe.wait_ge(s_drain, n - 3)
                setup_product(*step, bank[4 + n % 4])
            pe.drain().then_inc(s_ready, 1)

            def fill_a(name):
                b, n = A_USE[name]
                if n:
                    pe.wait_ge(drained[b], n)
                if b == 5 and all_o_before(name):
                    pe.wait_ge(R["o_ready"], all_o_before(name))
                return bank[b], filled[b]

            def fill_b(name):
                b, n = B_USE[name]
                if n:
                    pe.wait_ge(drained[b], n)
                return bank[b], filled[b]

            def has(use):
                pe.wait_ge(drained[use[0]], use[1] + 1)

            def scores(k):
                b, half = k % UNITS // 2, k % 2
                if k >= 2:
                    pe.wait_ge(R["copied"], k - 1)
                for c in range(KC):
                    if k % UNITS == 0:
                        has(A_USE[f"q{k // UNITS + 1}", c])
                        has(A_USE[f"k{k // UNITS + 1}", c])
                    for g in range(2):
                        r = slice(32 * (2 * half + g), 32 * (2 * half + g) + 32)
                        last = mm(score[:, k % 2, 4 * g + 2 * c:4 * g + 2 * c + 2, :].rearrange("p e n -> p (e n)"),
                                  qT[r, c, b * P:(b + 1) * P],
                                  kM[r, c, b, :, :].rearrange("p e n -> p (e n)"), start=True, stop=True)
                last.then_inc(R["scored"], 1)

            def turn_probs(k):
                if k < UNITS:
                    pe.wait_ge(R["exped"], 2 * k + 2)
                else:
                    pe.wait_ge(R["picked"], 2 * (k - UNITS) + 2)
                for j in range(8):
                    last = nc.tensor.transpose(score[:, k % 2, j, :], prob[:, k % 2, j, :], ident[:, :])
                last.then_inc(R["turned"], 1)

            def values(n):
                b = n % G
                pe.wait_ge(R["copied"], 2 * n + 2)
                if n:
                    pe.wait_ge(R["o_ready"], n)
                if b == 0:
                    u = A_USE[[a for a in (A_BETWEEN if n else A_BEFORE) if A_USE[a][0] == 5][-1]]
                    has(u)
                    if n or first_round[0]:
                        for p in range(2):
                            has(A_USE[f"v{n // G + 1}", p])
                for c in range(KC):
                    for e in range(2):
                        for g in range(4):
                            j = slot_of(8 * c + 2 * g + e)
                            mm(bank[5][32 * g:32 * g + 32, c * P:(c + 1) * P],
                               vM[:, b, 4 * c + g, e:e + 2, :].rearrange("p i d -> p (i d)"),
                               probT[:, j // 8, j % 8, :], start=e == 0, stop=e == 1)
                pe.wait_ge(R["widened"], n + 1)
                for c in range(KC):
                    last = nc.tensor.transpose(
                        bank[5][:, (KC + c) * P:(KC + c + 1) * P],
                        p_inv_wide[:, 8 * c:8 * c + 8, :].rearrange("p h d -> p (h d)"), ident[:, :])
                last.then_inc(R["valued"], 1)

            def project(names, weight, c0, source):
                for m in range(KC):
                    ps, f = fill_a((names, m))
                    for kk in range(KC):
                        last = mm(ps[:, :], weight[:, kk, c0 + m * P:c0 + (m + 1) * P], source[:, kk, :],
                                  start=kk == 0, stop=kk == KC - 1)
                    last.then_inc(f, 1)

            def turn(names, source, fill, chunks=range(KC)):
                for c in chunks:
                    ps, f = fill((names, c))
                    for b in range(G):
                        last = nc.tensor.transpose(ps[:, b * P:(b + 1) * P], source[:, b, c * P:(c + 1) * P],
                                                   ident[:, :])
                    last.then_inc(f, 1)

            def lns(k):
                return k if first_round[0] else k - 1

            first_round = [True]

            def make_values(name, p, source, w, c0):
                ps, f = fill_a((name, p))
                for b in range(2):
                    for kk in range(KC):
                        last = mm(ps[:, b * C:(b + 1) * C], source[:, kk, (2 * p + b) * P:(2 * p + b + 1) * P],
                                  w[:, kk, c0:c0 + C], start=kk == 0, stop=kk == KC - 1)
                last.then_inc(f, 1)

            def turn_back(names, source, fill):
                for p in range(2):
                    ps, f = fill((names, p))
                    for b in range(2):
                        for c in range(KC):
                            last = nc.tensor.transpose(ps[:, b * C + c * P:b * C + (c + 1) * P],
                                                       source[:, c, (2 * p + b) * P:(2 * p + b + 1) * P], ident[:, :])
                    last.then_inc(f, 1)

            def step_a(name, k):
                if name == "turn_ctx":
                    turn("ctx1", ctx_a, fill_a)
                elif name == "ctx_next":
                    pe.wait_ge(R["loaded"], 16)
                    turn("ctx3", ctx_a, fill_a, [k])
                elif name == "turn_x":
                    pe.wait_ge(R["xn_ready"], lns(k))
                    turn(f"x{k}", xn, fill_a)
                elif name == "turn_next":
                    pe.wait_ge(R["xn_ready"], lns(3))
                    turn("x3", xn, fill_a, [k])
                elif name == "q":
                    if k == 2 or first_round[0]:
                        has(A_USE[f"x{k}", 1])
                        has(A_USE[f"x{k}", 0])
                    project(f"q{k}", *((w_qkv, 0) if k == 1 else (w_q, 0)), hT)
                elif name == "k":
                    project(f"k{k}", *((w_qkv, C) if k == 1 else (w_kv, 0)), hT if k == 1 else ctxT_a)
                elif name == "v":
                    if k == 1:
                        for c in range(KC):
                            has(A_USE["x1", c])
                    for p in range(2):
                        make_values(f"v{k}", p, *((hT, w_qkv, 2 * C) if k == 1 else (ctxT_a, w_kv, C)))
                elif name == "v_next":
                    if k == 0:
                        for c in range(KC):
                            has(A_USE["x3", c])
                    make_values("v3", k, hT, w_qkv, 2 * C)
                elif name == "first_scores":
                    scores(k)
                elif name == "unit_b":
                    if k % UNITS:
                        turn_probs(k - 1)
                elif name == "unit_c":
                    if (k + 1) % UNITS:
                        scores(k + 1)
                    if k % UNITS and k % 2 == 0:
                        values(k // 2 - 1)
                elif name == "last_a":
                    turn_probs(k)
                elif name == "last_b":
                    values(k // 2)
                elif name == "project":
                    pe.wait_ge(R["o_ready"], k * G)
                    project(f"y{k}", w_so if k == 1 else w_co, 0, oT)
                elif name == "residual":
                    has(A_USE[f"y{k}", 0])
                    has(A_USE[f"y{k}", 1])
                    turn_back(f"r{k}", yT[k], fill_a)

            def step_b(name, k):
                if name == "turn_b":
                    pe.wait_ge(R["xn_ready_b"], k - 2)
                    turn(f"x{k}", xnb, fill_b)
                elif name in ("mlp_a", "mlp_b"):
                    ps, f = fill_b((name[-1], k))
                    if (name, k) == ("mlp_a", 0):
                        has(B_USE["x3", 0])
                        has(B_USE["x3", 1])
                    c0 = (HID if name == "mlp_b" else 0) + k * P
                    for kk in range(KC):
                        last = mm(ps[:, :], w_m1[:, kk, c0:c0 + P], hB[:, kk, :], start=kk == 0, stop=kk == KC - 1)
                    last.then_inc(f, 1)
                elif name == "mlp_down":
                    m, quarter = k // 4, k % 4
                    if quarter == 0:
                        fill_b(("down", m))
                    b = B_USE["down", m][0]
                    for kk in (2 * quarter, 2 * quarter + 1):
                        if m == 0:
                            has(B_USE["b", kk])
                        last = mm(bank[b][:, :], w_m2[:, kk, m * P:(m + 1) * P], hidden[:, kk, :],
                                  start=kk == 0, stop=kk == MC - 1)
                    if quarter == 3:
                        last.then_inc(filled[b], 1)
                elif name == "residual_b":
                    has(B_USE["down", 0])
                    has(B_USE["down", 1])
                    turn_back("r3", hB, fill_b)
                elif name == "query":
                    ps, f = fill_b(("query", k))
                    if k == 0:
                        has(B_USE["x4", 0])
                        has(B_USE["x4", 1])
                    for kk in range(KC):
                        last = mm(ps[:, :], w_query[:, kk, k * P:(k + 1) * P], hB[:, kk, :],
                                  start=kk == 0, stop=kk == KC - 1)
                    last.then_inc(f, 1)
                elif name == "match":
                    ps, f = fill_b(("match", 0))
                    has(B_USE["query", 0])
                    has(B_USE["query", 1])
                    for b in range(G):
                        for kk in range(KC):
                            last = mm(ps[:, b * P:(b + 1) * P], qs[:, kk, b * P:(b + 1) * P],
                                      ctxT_b[:, kk, b * P:(b + 1) * P], start=kk == 0, stop=kk == KC - 1)
                    last.then_inc(f, 1)
                elif name == "weights":
                    ps, f = fill_b(("weights", 0))
                    pe.wait_ge(R["wgt_ready"], 1)
                    for b in range(G):
                        last = nc.tensor.transpose(ps[:, b * P:(b + 1) * P], wgt[:, b, :], ident[:, :])
                    last.then_inc(f, 1)
                elif name == "evidence":
                    ps, f = fill_b(("evidence", k))
                    has(B_USE["weights", 0])
                    for b in range(G):
                        last = mm(ps[:, b * P:(b + 1) * P], ctx_b[:, b, k * P:(k + 1) * P],
                                  wgtT[:, b * P:(b + 1) * P], start=True, stop=True)
                    last.then_inc(f, 1)
                elif name == "router":
                    ps, f = fill_b(("router", 0))
                    for kk in range(2 * KC):
                        if kk >= KC:
                            has(B_USE["evidence", kk - KC])
                        source = hB if kk < KC else evT
                        last = mm(ps[0:E, :], w_r[:, kk, :], source[:, kk % KC, :], start=kk == 0,
                                  stop=kk == 2 * KC - 1)
                    last.then_inc(f, 1)
                elif name == "router_turn":
                    ps, f = fill_b(("router", 1))
                    has(B_USE["router", 0])
                    for b in range(G):
                        last = nc.tensor.transpose(ps[:, b * E:(b + 1) * E], logitT[:, b * P:(b + 1) * P],
                                                   ident[0:E, 0:E])
                    last.then_inc(f, 1)
                elif name in ("expert_x", "expert_v"):
                    w, c0 = (w_e1, k * P) if k < EC else (w_g1, (k - EC) * P)
                    if name == "expert_x":
                        fill_b(("expert", k))
                    b = B_USE["expert", k][0]
                    source, k0 = (hB, 0) if name == "expert_x" else (evT, KC)
                    for kk in range(KC):
                        last = mm(bank[b][:, :], w[:, k0 + kk, c0:c0 + P], source[:, kk, :],
                                  start=k0 + kk == 0, stop=k0 + kk == 2 * KC - 1)
                    if name == "expert_v":
                        last.then_inc(filled[b], 1)
                elif name in ("mix0", "mix1"):
                    half = int(name[-1])
                    ps, f = fill_b(("mix", 2 * k + half))
                    if k == 0:
                        pe.wait_ge(R["hidden_ready"], EC + 2 if half else 2 * RH // P)
                    for side in range(2):
                        e = 2 * half + side
                        chunks = range(4 * e, 4 * e + 4) if e < E else range(EC, EC + 2)
                        o = ps[:, side * C:(side + 1) * C]
                        for j in chunks:
                            w = w_e2[:, j, :] if e < E else w_g2[:, j - EC, :]
                            mm(o, hidden[:, j, k * P:(k + 1) * P], w, start=j == chunks[0], stop=False)
                        last = mm(o, row_of[:, e, :], bias_parts[:, :], start=False, stop=True)
                    last.then_inc(f, 1)

            def round_(steps, n):
                first_round[0] = steps is ONLY_A
                enter(pe, n)
                for stage, step in steps:
                    if stage == "fold":
                        n = FOLDS.index(step)
                        if n < 2:
                            has(A_USE["v1", n])
                        else:
                            pe.wait_ge(s_drain, len(SETUP) + n - 1)
                        setup_product(*step, bank[6 + n % 2])
                    else:
                        (step_a if stage == "A" else step_b)(*step)
                leave(pe)

            round_(ONLY_A, 1)
            with pe.Fori(1, NG) as i:
                round_(BOTH, i + 1)
            round_(ONLY_B, NG + 1)

        @block.scalar
        def _(act):
            f_ = nc.scalar.activation

            def vector_rows(ps, first, k, count, bias):
                for j in range(4 * k, min(4 * k + 4, count)):
                    last = f_(vectors[:, :, first + j, :], ps[:, j % 4 * B:(j % 4 + 1) * B]
                              .rearrange("p (n g) -> p n g", g=G), ACT.Identity, bias=bias[:, j:j + 1])
                return last

            def setup_drain(name, k, ps):
                if name == "cond":
                    f_(condT[:, :, :].rearrange("p c b -> p (c b)"), ps[:, 0:KC * B], ACT.Copy)
                    last = f_(siluT[:, :, :].rearrange("p c b -> p (c b)"), ps[:, KC * B:2 * KC * B], ACT.Copy,
                              scale=0.5)
                elif name == "turn_w":
                    last = f_((WqT, WkT, WvT)[k][:, :, :].rearrange("p c n -> p (c n)"), ps[:, :], ACT.Copy)
                elif name == "turn_e2":
                    last = f_(e2T[:, :, 2 * k * P:(2 * k + 2) * P], ps[:, :].rearrange("p (c n) -> p c n", c=KC),
                              ACT.Copy)
                elif name == "query":
                    last = f_(w_query[:, :, :].rearrange("p c n -> p (c n)"), ps[:, :], ACT.Copy,
                              scale=float(C) ** -0.5)
                elif name == "e_b2":
                    for i in range(3):
                        last = f_(bias_rows[32 * i:32 * i + E, :], ps[32 * i:32 * i + E, 0:C], ACT.Copy)
                elif name == "e2_out":
                    last = f_(w_e2[:, 2 * k:2 * k + 2, :].rearrange("p c n -> p (c n)"), ps[:, :], ACT.Copy,
                              scale=0.5)
                elif name == "ada":
                    last = vector_rows(ps, 0, k, 18, b_ada)
                elif name == "evidence":
                    kk, e = k // E, k % E
                    last = f_(w_e1[:, KC + kk, e * RH:(e + 1) * RH], ps[:, :], ACT.Copy)
                elif name == "evidence_gate":
                    last = f_(w_g1[:, KC:, :].rearrange("p c n -> p (c n)"), ps[:, :], ACT.Copy)
                elif name == "evidence_router":
                    last = f_(w_r[:, KC:, :].rearrange("p c n -> p (c n)"), ps[:, 0:KC * E], ACT.Copy)
                elif name == "anchor":
                    last = vector_rows(ps, EB, k, EC + 2, b_e1)
                elif name == "anchor_router":
                    last = f_(router_b[:, :, :], ps[0:E, 0:B].rearrange("p (n g) -> p n g", g=G), ACT.Identity,
                              bias=b_r[:, 0:1])
                last.then_inc(s_drain, 1)

            act.wait_ge(s_cond, 16)
            f_(cond_th[:, :], cond[:, :], ACT.Tanh, scale=0.5).then_inc(s_act, 1)
            for n, step in enumerate(SETUP):
                if step == ("e_b2", 0):
                    act.wait_ge(s_small, 16 * N_SMALL)
                act.wait_ge(s_fill, n + 1)
                setup_drain(*step, bank[4 + n % 4])
            act.drain().then_inc(s_ready, 1)

            def take(use):
                b, n = use
                act.wait_ge(filled[b], n + 1)
                return bank[b], drained[b]

            def modulated(dest, use, scale, shift, vec):
                ps, d = take(use)
                for b in range(G):
                    last = f_(dest[:, b * P:(b + 1) * P], ps[:, b * P:(b + 1) * P], ACT.Identity,
                              scale=vec[:, scale, b:b + 1], bias=vec[:, shift, b:b + 1])
                last.then_inc(d, 1)

            def copied(dest, use, **kw):
                ps, d = take(use)
                f_(dest, ps[:, :], ACT.Identity if kw else ACT.Copy, **kw).then_inc(d, 1)

            def exps(k, half):
                act.wait_ge(R["maxed"], 2 * k + half + 1)
                for j in range(4 * half, 4 * half + 4):
                    kw = {}
                    if k < UNITS:
                        h = HEAD_AT[8 * (k % 2) + j]
                        kw["accum_out"] = p_sum[:, k // 2 % 2, h:h + 1]
                    last = f_(prob[:, k % 2, j, :], score[:, k % 2, j, :], ACT.Exp,
                              scale=float(D) ** -0.5, bias=neg_max[:, k % 2, j:j + 1], **kw)
                last.then_inc(R["exped"], 1)

            def copy_inverse(n):
                act.wait_ge(R["valued"], n + 1)
                f_(oT[:, :, n % G * P:(n % G + 1) * P], bank[5][:, C:].rearrange("p (c n) -> p c n", c=KC), ACT.Copy)\
                    .then_inc(R["inv_copied"], 1)

            def copy_turned(k):
                act.wait_ge(R["turned"], k + 1)
                if k >= 2:
                    act.wait_ge(R["valued"], k // 2)
                f_(probT[:, k % 2, :, :], score[:, k % 2, :, :], ACT.Copy).then_inc(R["copied"], 1)

            def step_a(name, k):
                if name == "turn_ctx":
                    for c in range(KC):
                        copied(ctxT_a[:, c, :], A_USE["ctx1", c])
                elif name == "ctx_next":
                    act.wait_ge(R["moved"], 32)
                    copied(ctxT_a[:, k, :], A_USE["ctx3", k])
                elif name == "turn_x":
                    if k == 1:
                        modulated(hT[:, 0, :], A_USE["x1", 0], SC1, SH1, vec_1)
                    else:
                        act.wait_ge(R["vec_a_loaded"], 16)
                        modulated(hT[:, 0, :], A_USE["x2", 0], SC2, SH2, vec_a)
                elif (name, k) == ("turn_next", 0):
                    act.wait_ge(R["vec_1_loaded"], 16)
                    modulated(hT[:, 0, :], A_USE["x3", 0], SC1, SH1, vec_1)
                elif name == "q":
                    for c in range(KC):
                        copied(qT[:, c, :], A_USE[f"q{k}", c], bias=(b_qkv if k == 1 else b_q)[:, c:c + 1])
                elif name == "k":
                    for c in range(KC):
                        ps, d = take(A_USE[f"k{k}", c])
                        for e in range(2):
                            last = f_(kM[:, c, :, e, :], ps[:, :].rearrange("p (b n) -> p b n", b=G), ACT.Identity,
                                      scale=head_mask[:, e:e + 1], bias=b_k[:, k - 1, e, c:c + 1])
                        last.then_inc(d, 1)
                elif name == "unit_a":
                    if k % 2 and k % UNITS > 1:
                        copy_inverse(k // 2 - 1)
                    exps(k, 0)
                elif name == "unit_b":
                    if k % UNITS:
                        copy_turned(k - 1)
                    exps(k, 1)
                elif name == "last_a":
                    copy_turned(k)
                elif name == "last_b":
                    copy_inverse(k // 2)
                elif name == "project":
                    act.wait_ge(R["vec_a_loaded"], 16)
                    modulated(yT[k][:, 0, :], A_USE[f"y{k}", 0], (GA1, GA2)[k - 1], (GB1, GB2)[k - 1], vec_a)

            def step_b(name, k):
                if name == "turn_b":
                    if k == 3:
                        act.wait_ge(R["vec_b_loaded"], 16)
                        modulated(hB[:, 0, :], B_USE["x3", 0], SC3, SH3, vec_b)
                    else:
                        for c in range(KC):
                            copied(hB[:, c, :], B_USE["x4", c], scale=gamma[:, c:c + 1], bias=beta[:, c:c + 1])
                elif name == "mlp_a":
                    ps, d = take(B_USE["a", k])
                    if k >= 2:
                        use = B_USE["b", k - 2]
                        act.wait_ge(drained[use[0]], use[1] + 1)
                    f_(z[:, k % 2, :], ps[:, :], ACT.Identity, bias=b_m1[:, k:k + 1])
                    f_(th[:, k % 2, :], ps[:, :], ACT.Tanh, scale=0.5, bias=b_m1h[:, k:k + 1]).then_inc(d, 1)
                elif name == "mlp_down" and k % 4 == 3:
                    m = k // 4
                    modulated(hB[:, m, :], B_USE["down", m], GA3 + m, GB3 + m, vec_b)
                elif name == "query":
                    copied(qs[:, k, :], B_USE["query", k])
                elif name == "match":
                    ps, d = take(B_USE["match", 0])
                    act.wait_ge(R["wmax_ready"], 1)
                    for b in range(G):
                        last = f_(wgt[:, b, :], ps[:, b * P:(b + 1) * P], ACT.Exp, bias=w_max[:, b:b + 1],
                                  accum_out=w_sum[:, b:b + 1])
                    last.then_inc(d, 1)
                elif name == "weights":
                    copied(wgtT[:, :], B_USE["weights", 0])
                elif name == "evidence":
                    copied(evT[:, k, :], B_USE["evidence", k])
                elif name == "router":
                    ps, d = take(B_USE["router", 0])
                    act.wait_ge(R["rb_ready"], 1)
                    for b in range(G):
                        last = f_(logitT[:, b * P:(b + 1) * P], ps[0:E, b * P:(b + 1) * P], ACT.Identity,
                                  bias=rb_b[:, b:b + 1])
                    last.then_inc(d, 1)
                elif name == "router_turn":
                    b, n = B_USE["router", 1]
                    act.wait_ge(drained[b], n + 1)
                    f_(l_exp[:, :, :], logit[:, :, :], ACT.Exp).then_inc(R["lexp_ready"], 1)
                elif name == "expert_v":
                    b, n = B_USE["expert", k]
                    act.wait_ge(drained[b], n + 1)
                    f_(th[:, k % 2, :], z[:, k % 2, :], ACT.Tanh, scale=0.5).then_inc(R["th_ready"], 1)
                elif name == "mix1":
                    ps, d = take(B_USE["mix", 2 * k + 1])
                    if k >= 2:
                        b, n = B_USE["mix", 2 * k - 3]
                        act.wait_ge(drained[b], n + 1)
                    f_(gate_th[:, k % 2, :], ps[:, C:2 * C], ACT.Tanh, scale=0.5).then_inc(R["gate_ready"], 1)

            def round_(steps, n):
                enter(act, n)
                for stage, step in steps:
                    if stage == "fold":
                        n = FOLDS.index(step)
                        act.wait_ge(s_fill, len(SETUP) + n + 1)
                        setup_drain(*step, bank[6 + n % 2])
                    else:
                        (step_a if stage == "A" else step_b)(*step)
                leave(act)

            round_(ONLY_A, 1)
            with act.Fori(1, NG) as i:
                round_(BOTH, i + 1)
            round_(ONLY_B, NG + 1)

        @block.vector
        def _(dve):
            v = nc.vector

            count = [0]

            def step(ins):
                ins.then_inc(R["dve_step"], 1)
                count[0] += 1
                return count[0]

            def after(n):
                dve.wait_ge(R["dve_step"], n)

            def take(use):
                b, n = use
                dve.wait_ge(filled[b], n + 1)
                return bank[b], drained[b]

            def layer_norm(x, xn, k, stats, mean_var, var_eps, rstd, eps, sems):
                ready, rstd_ready, xn_ready = (R[s] for s in sems)
                ns = [step(v.bn_stats(stats[:, b, :], x[:, b, :])) for b in range(G)]
                for b in range(G):
                    after(ns[b])
                    n = step(v.bn_aggr(mean_var[:, b, :], stats[:, b, :]))
                after(n)
                v.tensor_scalar(var_eps[:, :], mean_var[:, :, 1], eps, None, ALU.add).then_inc(ready, 1)
                dve.wait_ge(rstd_ready, k)
                for b in range(G):
                    last = v.tensor_scalar(xn[:, b, :], x[:, b, :], mean_var[:, b, 0:1], rstd[:, b:b + 1],
                                           ALU.subtract, ALU.mult)
                last.then_inc(xn_ready, 1)

            def normalise_a(x, n):
                layer_norm(x, xn, n, stats, mean_var, var_eps, rstd, EPS0, ("var_ready", "rstd_ready", "xn_ready"))

            def modulated(dest, use, scale, shift, vec):
                ps, d = take(use)
                for b in range(G):
                    last = v.tensor_scalar(dest[:, b * P:(b + 1) * P], ps[:, b * P:(b + 1) * P],
                                           vec[:, scale, b:b + 1], vec[:, shift, b:b + 1], ALU.mult, ALU.add)
                last.then_inc(d, 1)

            def keep_values(use, p, attention):
                ps, d = take(use)
                for e in range(2):
                    last = v.tensor_tensor(
                        vM[:, 2 * p:2 * p + 2, :, 2 * e, :],
                        ps[:, :].rearrange("p (b x e d) -> p b x e d", b=2, e=2, d=D)[:, :, :, e],
                        b_v[:, attention, :].rearrange("p (x e d) -> p x e d", e=2, d=D)[:, :, e]
                        .unsqueeze(1).to_broadcast([P, 2, 8, D]), ALU.add)
                last.then_inc(d, 1)

            def maxima(k, half):
                if half == 0:
                    dve.wait_ge(R["scored"], k + 1)
                j = slice(4 * half, 4 * half + 4)
                after(step(v.tensor_reduce(rowmax[:, j], score[:, k % 2, j, :], AX.X, ALU.max)))
                v.tensor_scalar(neg_max[:, k % 2, j], rowmax[:, j], -float(D) ** -0.5, None, ALU.mult)\
                    .then_inc(R["maxed"], 1)

            def top(k, half):
                if half == 0:
                    dve.wait_ge(R["scored"], k + 1)
                heads = range(4 * half, 4 * half + 4)
                s = score[:, k % 2]
                at = heads[0]
                n = {j: step(v.max(top1[:, j - at, :], s[:, j, :])) for j in heads}
                for j in heads:
                    after(n[j])
                    n[j] = step(v.match_replace(left[:, j - at, :], top1[:, j - at, :], s[:, j, :], GONE))
                after(n[heads[-1]])
                v.tensor_scalar(neg_max[:, k % 2, heads[0]:heads[0] + 4], top1[:, :, 0],
                                -float(D) ** -0.5, None, ALU.mult).then_inc(R["maxed"], 1)
                for j in heads:
                    after(n[j])
                    n[j] = step(v.max(top2[:, j - at, :], left[:, j - at, :]))
                for j in heads:
                    after(n[j])
                    n[j] = step(v.match_replace(left[:, j - at, :], top2[:, j - at, :], left[:, j - at, :], GONE))
                return n[heads[-1]]

            def pick(k, half, n):
                dve.wait_ge(R["exped"], 2 * k + half + 1)
                after(n)
                for i in range(4):
                    j = 4 * half + i
                    h = HEAD_AT[8 * (k % 2) + j]
                    last = v.scalar_tensor_tensor(prob[:, k % 2, j, :], left[:, i, :], GONE, prob[:, k % 2, j, :],
                                                  ALU.is_equal, ALU.mult, accum_out=p_sum[:, k // 2 % 2, h:h + 1])
                last.then_inc(R["picked"], 1)

            def invert(n):
                if n < G:
                    dve.wait_ge(R["exped"], 4 * n + 4)
                else:
                    dve.wait_ge(R["picked"], 4 * (n - G) + 4)
                v.reciprocal(p_inv[:, n % 2, :], p_sum[:, n % 2, :]).then_inc(R["inverted"], 1)

            def output(n):
                b = n % G
                dve.wait_ge(R["inv_copied"], n + 1)
                out_ = oT[:, :, b * P:(b + 1) * P]
                v.tensor_tensor(out_, bank[5][:, 0:C].rearrange("p (c n) -> p c n", c=KC), out_, ALU.mult)\
                    .then_inc(R["o_ready"], 1)

            def step_a(name, k):
                if name == "ln":
                    if k == 2:
                        b, n = A_USE["r1", 1]
                        dve.wait_ge(drained[b], n + 1)
                        b, n = A_USE["r1", 0]
                        dve.wait_ge(drained[b], n + 1)
                    elif k == 3:
                        dve.wait_ge(R["x_loaded"], 16)
                        for c in range(KC):
                            b, n = A_USE["x2", c]
                            dve.wait_ge(filled[b], n + 1)
                    normalise_a(x_mid if k == 2 else x_in, k - 1 if with_b[0] else k)
                elif name == "turn_x":
                    if k == 1:
                        modulated(hT[:, 1, :], A_USE["x1", 1], SC1 + 1, SH1 + 1, vec_1)
                    else:
                        dve.wait_ge(R["vec_a_loaded"], 16)
                        modulated(hT[:, 1, :], A_USE["x2", 1], SC2 + 1, SH2 + 1, vec_a)
                elif (name, k) == ("turn_next", 1):
                    dve.wait_ge(R["vec_1_loaded"], 16)
                    modulated(hT[:, 1, :], A_USE["x3", 1], SC1 + 1, SH1 + 1, vec_1)
                elif name == "project":
                    dve.wait_ge(R["vec_a_loaded"], 16)
                    modulated(yT[k][:, 1, :], A_USE[f"y{k}", 1], (GA1, GA2)[k - 1] + 1, (GB1, GB2)[k - 1] + 1, vec_a)
                elif name == "v":
                    for p in range(2):
                        keep_values(A_USE[f"v{k}", p], p, k - 1)
                elif name == "v_next":
                    keep_values(A_USE["v3", k], k, 0)
                elif name in ("unit_a", "unit_b"):
                    half = int(name == "unit_b")
                    first = half == 0 and k % 2 == 0 and k % UNITS > 0
                    if k < UNITS:
                        maxima(k, half)
                        if first:
                            invert(k // 2 - 1)
                    else:
                        if first:
                            invert(k // 2 - 1)
                        pick(k, half, top(k, half))
                    if half == 0 and k % 2 and k % UNITS > 1:
                        output(k // 2 - 1)
                elif name == "last_a":
                    invert(k // 2)
                elif name == "last_b":
                    output(k // 2)
                elif name == "residual":
                    for p in range(2):
                        ps, d = take(A_USE[f"r{k}", p])
                        source, dest = x_in if k == 1 else x1, x1
                        if k == 1 and p == 0 and with_b[0]:
                            b, n = B_USE["r3", 1]
                            dve.wait_ge(drained[b], n + 1)
                        v.tensor_tensor(dest[:, 2 * p:2 * p + 2, :].rearrange("p b c -> p (b c)"), ps[:, :],
                                        source[:, 2 * p:2 * p + 2, :].rearrange("p b c -> p (b c)"), ALU.add)\
                            .then_inc(d, 1)

            def silu_done(j):
                dve.wait_ge(R["th_ready"], j + 1)
                v.scalar_tensor_tensor(hidden[:, j, :], th[:, j % 2, :], 1.0, z[:, j % 2, :], ALU.add, ALU.mult)\
                    .then_inc(R["hidden_ready"], 1)

            def step_b(name, k):
                if name == "lnb":
                    if k == 3:
                        dve.wait_ge(R["mix_free"], 1)
                    if k == 4:
                        for p in range(2):
                            b, n = B_USE["r3", p]
                            dve.wait_ge(drained[b], n + 1)
                    layer_norm(x1 if k == 3 else x2, xnb, k - 2, stats_b, mean_var_b, var_eps_b, rstd_b,
                               EPS0 if k == 3 else EPS1, ("var_ready_b", "rstd_ready_b", "xn_ready_b"))
                elif name == "turn_b" and k == 3:
                    dve.wait_ge(R["vec_b_loaded"], 16)
                    modulated(hB[:, 1, :], B_USE["x3", 1], SC3 + 1, SH3 + 1, vec_b)
                elif name == "mlp_b":
                    b, n = B_USE["a", k]
                    dve.wait_ge(drained[b], n + 1)
                    n = step(v.scalar_tensor_tensor(z[:, k % 2, :], th[:, k % 2, :], 1.0, z[:, k % 2, :],
                                                    ALU.add, ALU.mult))
                    ps, d = take(B_USE["b", k])
                    after(n)
                    v.scalar_tensor_tensor(hidden[:, k, :], ps[:, :], b_m1[:, MC + k:MC + k + 1], z[:, k % 2, :],
                                           ALU.add, ALU.mult).then_inc(d, 1)
                elif name == "residual_b":
                    for p in range(2):
                        ps, d = take(B_USE["r3", p])
                        v.tensor_tensor(x2[:, 2 * p:2 * p + 2, :].rearrange("p b c -> p (b c)"), ps[:, :],
                                        x1[:, 2 * p:2 * p + 2, :].rearrange("p b c -> p (b c)"), ALU.add)\
                            .then_inc(d, 1)
                elif name == "match":
                    ps, d = take(B_USE["match", 0])
                    v.tensor_reduce(w_max[:, :], ps[:, :].rearrange("p (b n) -> p b n", b=G), AX.X, ALU.max,
                                    negate=True).then_inc(R["wmax_ready"], 1)
                elif name == "normalise":
                    b, n = B_USE["match", 0]
                    dve.wait_ge(drained[b], n + 1)
                    after(step(v.reciprocal(w_sum[:, :], w_sum[:, :])))
                    v.tensor_tensor(wgt[:, :, :], wgt[:, :, :], w_sum[:, :].unsqueeze(2).to_broadcast([P, G, P]),
                                    ALU.mult).then_inc(R["wgt_ready"], 1)
                elif name == "router_turn":
                    ps, d = take(B_USE["router", 1])
                    logits = ps[:, 0:G * E].rearrange("p (b e) -> p b e", b=G)
                    after(step(v.tensor_reduce(l_max[:, :], logits, AX.X, ALU.max)))
                    v.tensor_tensor(logit[:, :, :], logits, l_max[:, :].unsqueeze(2).to_broadcast([P, G, E]),
                                    ALU.subtract).then_inc(d, 1)
                elif name == "route":
                    dve.wait_ge(R["lexp_ready"], 1)
                    after(step(v.tensor_reduce(l_sum[:, :], l_exp[:, :, :], AX.X, ALU.add)))
                    after(step(v.reciprocal(l_sum[:, :], l_sum[:, :])))
                    route_step[0] = step(v.scalar_tensor_tensor(
                        route[:, :, :], l_exp[:, :, :], 0.5, l_sum[:, :].unsqueeze(2).to_broadcast([P, G, E]),
                        ALU.mult, ALU.mult))
                elif name == "expert_v":
                    ps, d = take(B_USE["expert", k])
                    if k == 0:
                        dve.wait_ge(R["vec_b_loaded"], 16)
                    if k >= 2:
                        dve.wait_ge(R["hidden_ready"], k - 1)
                    v.tensor_tensor(z[:, k % 2, :].rearrange("p (b n) -> p b n", b=G),
                                    ps[:, :].rearrange("p (b n) -> p b n", b=G),
                                    vec_b[:, EB + k, :].unsqueeze(2).to_broadcast([P, G, P]), ALU.add)\
                        .then_inc(d, 1)
                    if k:
                        silu_done(k - 1)
                elif name == "expert_end":
                    silu_done(EC + 1)
                elif name == "mix0":
                    ps, d = take(B_USE["mix", 2 * k])
                    after(route_step[0])
                    after(step(v.tensor_scalar(mix[:, k, :], ps[:, 0:C], route[:, k, 0:1], None, ALU.mult)))
                    v.scalar_tensor_tensor(mix[:, k, :], ps[:, C:2 * C], route[:, k, 1:2], mix[:, k, :],
                                           ALU.mult, ALU.add).then_inc(d, 1)
                elif name == "mix1":
                    ps, d = take(B_USE["mix", 2 * k + 1])
                    b, n = B_USE["mix", 2 * k]
                    dve.wait_ge(drained[b], n + 1)
                    dve.wait_ge(R["gate_ready"], k + 1)
                    n = step(v.scalar_tensor_tensor(mix[:, k, :], ps[:, 0:C], route[:, k, 2:3], mix[:, k, :],
                                                    ALU.mult, ALU.add))
                    after(n)
                    v.scalar_tensor_tensor(mix[:, k, :], gate_th[:, k % 2, :], 1.0, mix[:, k, :],
                                           ALU.add, ALU.mult).then_inc(d, 1)

            route_step = [0]
            with_b = [False]

            def round_(steps, n):
                if steps is not ONLY_A:
                    count[0] = 0
                with_b[0] = steps is BOTH
                enter(dve, n)
                if steps is ONLY_A:
                    dve.wait_ge(s_const, 10)
                for stage, step_ in steps:
                    if stage != "fold":
                        (step_a if stage == "A" else step_b)(*step_)
                leave(dve)

            setup = [0]

            def done(ins):
                ins.then_inc(s_dve, 1)
                setup[0] += 1

            def settle():
                dve.wait_ge(s_dve, setup[0])

            dve.wait_ge(s_cond, 16)
            dve.wait_ge(s_act, 1)
            done(v.scalar_tensor_tensor(cond_silu[:, :], cond_th[:, :], 1.0, cond[:, :], ALU.add, ALU.mult))
            dve.wait_ge(s_const, 5)
            for e in range(2):
                done(v.tensor_reduce(head_mask[:, e:e + 1],
                                     ident[:, :].rearrange("p (g e d) -> p e g d", e=2, d=D)[:, e],
                                     AX.XY, ALU.add))
            settle()
            dve.wait_ge(s_small, 16 * N_SMALL)
            for e in range(2):
                done(v.tensor_scalar(b_k[:, 0, e, :], b_qkv[:, 2:4], head_mask[:, e:e + 1], None, ALU.mult))
                done(v.tensor_scalar(b_k[:, 1, e, :], b_kv[:, 0:2], head_mask[:, e:e + 1], None, ALU.mult))
            done(v.tensor_scalar(b_m1h[:, :], b_m1[:, :], 0.5, None, ALU.mult))
            dve.wait_ge(s_fold, 16 * N_FOLD)
            done(v.tensor_scalar(w_g2[:, :, :], w_g2[:, :, :], 0.5, None, ALU.mult))
            dve.wait_ge(s_drain, SETUP.index(("e_b2", 0)) + 1)
            for i in range(3):
                r = slice(32 * i, 32 * i + E)
                done(v.tensor_tensor(bias_rows[r, :], bias_rows[r, :], out_b3[r, :], ALU.add))
            settle()
            rest = bias_rows
            for i in range(3):
                done(v.tensor_copy(part_of[i][:, :], rest[:, :]))
                settle()
                r = slice(32 * i, 32 * i + 32 if i < 2 else P)
                done(v.tensor_copy(bias_parts[r, :], part_of[i][r, :]))
                if i < 2:
                    done(v.tensor_tensor(bias_rest[:, :], rest[:, :], part_of[i][:, :], ALU.subtract))
                    rest = bias_rest
                    settle()
            dve.wait_ge(s_x, 16)
            normalise_a(x_in, 1)
            dve.wait_ge(s_drain, SETUP.index(("ada", 4)) + 1)
            for row in (SC1, SC2, SC3):
                done(v.tensor_scalar(vectors[:, :, row:row + 2, :], vectors[:, :, row:row + 2, :], 1.0, None,
                                     ALU.add))
            for i, (gate, gb) in enumerate(((GA1, GB1), (GA2, GB2), (GA3, GB3))):
                for c in range(KC):
                    done(v.tensor_scalar(vectors[:, :, gb + c, :], vectors[:, :, gate + c, :],
                                         b_out[:, 2 * i + c:2 * i + c + 1], None, ALU.mult))
            settle()
            done(v.tensor_scalar(vectors[:, :, GA3:GA3 + 2, :], vectors[:, :, GA3:GA3 + 2, :], 0.5, None, ALU.mult))
            settle()
            done(v.tensor_copy(vec_1[:, :, :], vectors[:, 0, 0:N1, :]))
            dve.drain().then_inc(s_ready, 1)

            round_(ONLY_A, 1)
            with dve.Fori(1, NG) as i:
                round_(BOTH, i + 1)
            round_(ONLY_B, NG + 1)


_INS = ["x", "cond_1024", "ctx_1024"] + [f"L0_xcond_{n}" for n in (
    "w_ada", "b_ada", "w_qkv", "b_qkv", "w_so", "b_so", "w_q", "b_q", "w_kv", "b_kv", "w_co", "b_co", "w_m1", "b_m1",
    "w_m2", "b_m2")] + [f"L1_xcond_{n}" for n in (
        "ln_gamma", "ln_beta", "Wq", "Wk", "Wv", "router_W", "router_b", "e_w1", "e_b1", "e_w2", "e_b2", "gate_w1",
        "gate_b1", "gate_w2", "gate_b2", "out_w", "out_b")]


def kernel(**inputs):
    import numpy as _np
    import concourse.bacc as _bacc
    from concourse import mybir as _mybir
    from concourse.bass_utils import run_bass_kernel_spmd as _run

    nc = _bacc.Bacc("TRN2", target_bir_lowering=False, num_devices=1)
    arrays, t = {}, {}
    for name in _INS:
        a = _np.ascontiguousarray(inputs[name])
        arrays[f"in_{name}"] = a
        t[name] = nc.dram_tensor(f"in_{name}", a.shape, _mybir.dt.from_np(a.dtype), kind="ExternalInput").ap()
    out = nc.dram_tensor("out", arrays["in_x"].shape, _mybir.dt.float32, kind="ExternalOutput").ap()
    program(nc, t, out)
    r = _run(nc, [arrays], core_ids=[0])
    return r.results[0]["out"]
```
